# Optimizing a Trainium2 kernel written in Bass

```python
import numpy as np
import jax
import jax.numpy as jnp

def _softmax(x, axis=-1):
    return jax.nn.softmax(x, axis=axis)

def _gelu(x):
    return jax.nn.gelu(x, approximate=True)

def _silu(x):
    return jax.nn.silu(x)

def _sigmoid(x):
    return jax.nn.sigmoid(x)

def _layernorm(x, axis=-1, eps=1e-05):
    m = jnp.mean(x, axis=axis, keepdims=True)
    v = jnp.var(x, axis=axis, keepdims=True)
    return (x - m) / jnp.sqrt(v + eps)

def _scatter_add(tgt, idx, src, axis=0):
    return tgt.at[idx].add(src)

def _segment_sum(src, seg, n):
    return jax.ops.segment_sum(src, seg, n)
kernel_name = 'mk_decoder_postln_d1_seqx_r8_d5aff5'

def setup_inputs(seed: int=0):
    np.random.seed(seed)
    _w = jnp.asarray

    def _rec_inputs():
        import jax
        import jax.numpy as jnp
        _rk = jax.random.key(seed)
        x = -0.0002928 + 1 * jax.random.normal(jax.random.fold_in(_rk, 1), (64, 64, 256), jnp.float32)
        _lenS = 64 - jax.random.randint(jax.random.fold_in(_rk, 7), (64,), 0, max(1, 64 // 4) + 1, jnp.int32)
        _lenS2 = 64 - jax.random.randint(jax.random.fold_in(_rk, 8), (64,), 0, max(1, 64 // 4) + 1, jnp.int32)
        _ctx_2048P = jax.random.normal(jax.random.fold_in(_rk, 11), (64, 16, 256), jnp.float32)
        _ctx_2048c = jax.random.dirichlet(jax.random.fold_in(_rk, 511), 0.3 * jnp.ones((16,), jnp.float32), (64, 64))
        _ctx_2048t = jnp.einsum('bsk,bkd->bsd', _ctx_2048c, _ctx_2048P)
        _ctx_2048t = _ctx_2048t * jax.lax.rsqrt(jnp.mean(jnp.square(_ctx_2048t)) + 1e-12) * 0.953939
        ctx_2048 = 4.13588e-05 + 0.999923 * (_ctx_2048t + 0.3 * jax.random.normal(jax.random.fold_in(_rk, 611), (64, 64, 256), jnp.float32))
        _validS = jnp.arange(64)[None, :] < _lenS[:, None]
        _validS2 = jnp.arange(64)[None, :] < _lenS2[:, None]
        _causal = jnp.tril(jnp.ones((64, 64), dtype=bool))
        mask_1xSxS2_ff0 = jnp.where(jnp.ones((1, 64, 64), dtype=bool), 0.0, -1000000000.0).astype(jnp.float32)
        return (x, ctx_2048, mask_1xSxS2_ff0)
    x, ctx_2048, mask_1xSxS2_ff0 = _rec_inputs()

    def _L0_attn_setup():
        import jax, jax.numpy as jnp
        import numpy as np
        HIDDEN = 256
        KEY = 256
        EPS = 1e-05
        key = jax.random.key(seed)
        k1, k2, k3 = jax.random.split(key, 3)
        B, S = (4, 256)
        x = jax.random.normal(k1, (B, S, HIDDEN), dtype=jnp.float32)
        bq = 1.0 / np.sqrt(HIDDEN)
        qkv = jax.random.uniform(k2, (HIDDEN, KEY * 3), minval=-bq, maxval=bq, dtype=jnp.float32)
        bo = 1.0 / np.sqrt(KEY)
        o_proj = jax.random.uniform(k3, (KEY, HIDDEN), minval=-bo, maxval=bo, dtype=jnp.float32)
        gamma = jnp.ones((HIDDEN,), dtype=jnp.float32)
        beta = jnp.zeros((HIDDEN,), dtype=jnp.float32)
        return {'x': x, 'qkv': qkv, 'o_proj': o_proj, 'gamma': gamma, 'beta': beta}
    _L0_attn_all = _L0_attn_setup()
    _L0_attn_in = {k: v for k, v in _L0_attn_all.items() if k in ('qkv', 'o_proj', 'gamma', 'beta')}
    del _L0_attn_all

    def _L0_xattn_setup():
        import jax, jax.numpy as jnp
        import numpy as np
        H = 256
        NH = 16
        NKV = 4
        HD = 128
        GROUPS = NH // NKV
        EPS = 1e-06
        B, S, SE = (1, 256, 512)

        def _rmsnorm(x, w, eps=EPS):
            xf = x.astype(jnp.float32)
            var = jnp.mean(xf * xf, axis=-1, keepdims=True)
            return (xf * jax.lax.rsqrt(var + eps)).astype(x.dtype) * w
        key = jax.random.key(seed)
        ks = jax.random.split(key, 12)
        sc = 0.02
        return {'hidden_states': jax.random.normal(ks[0], (B, S, H), jnp.float32), 'encoder_hidden_states': jax.random.normal(ks[1], (B, SE, H), jnp.float32), 'attention_mask': jnp.zeros((B, S, SE), jnp.float32), 'Wq': jax.random.normal(ks[2], (H, NH * HD), jnp.float32) * sc, 'bq': jax.random.normal(ks[3], (NH * HD,), jnp.float32) * sc, 'Wk': jax.random.normal(ks[4], (H, NKV * HD), jnp.float32) * sc, 'bk': jax.random.normal(ks[5], (NKV * HD,), jnp.float32) * sc, 'Wv': jax.random.normal(ks[6], (H, NKV * HD), jnp.float32) * sc, 'bv': jax.random.normal(ks[7], (NKV * HD,), jnp.float32) * sc, 'Wo': jax.random.normal(ks[8], (NH * HD, H), jnp.float32) * sc, 'qn_w': jnp.ones((HD,), jnp.float32), 'kn_w': jnp.ones((HD,), jnp.float32)}
    _L0_xattn_all = _L0_xattn_setup()
    _L0_xattn_in = {k: v for k, v in _L0_xattn_all.items() if k in ('Wq', 'bq', 'Wk', 'bk', 'Wv', 'bv', 'Wo', 'qn_w', 'kn_w')}
    del _L0_xattn_all

    def _L0_ffn_setup():
        import jax, jax.numpy as jnp
        import numpy as np
        H = 256
        E = 64
        I = 64
        SI = 64
        TOP_K = 8
        B, T = (2, 64)
        key = jax.random.key(seed)
        ks = jax.random.split(key, 8)
        s = 0.02
        return {'h': jax.random.normal(ks[0], (B, T, H), jnp.float32), 'gate_w': jax.random.normal(ks[1], (E, H), jnp.float32) * s, 'gu_w': jax.random.normal(ks[2], (E, 2 * I, H), jnp.float32) * s, 'dp_w': jax.random.normal(ks[3], (E, H, I), jnp.float32) * s, 'sh_gate_w': jax.random.normal(ks[4], (SI, H), jnp.float32) * s, 'sh_up_w': jax.random.normal(ks[5], (SI, H), jnp.float32) * s, 'sh_down_w': jax.random.normal(ks[6], (H, SI), jnp.float32) * s, 'sh_gate1_w': jax.random.normal(ks[7], (1, H), jnp.float32) * s}
    _L0_ffn_all = _L0_ffn_setup()
    _L0_ffn_in = {k: v for k, v in _L0_ffn_all.items() if k in ('gate_w', 'gu_w', 'dp_w', 'sh_gate_w', 'sh_up_w', 'sh_down_w', 'sh_gate1_w')}
    del _L0_ffn_all
    return {'x': x, 'ctx_2048': ctx_2048, 'mask_1xSxS2_ff0': mask_1xSxS2_ff0, 'L0_attn_qkv': _L0_attn_in['qkv'], 'L0_attn_o_proj': _L0_attn_in['o_proj'], 'L0_attn_gamma': _L0_attn_in['gamma'], 'L0_attn_beta': _L0_attn_in['beta'], 'L0_xattn_Wq': _L0_xattn_in['Wq'], 'L0_xattn_bq': _L0_xattn_in['bq'], 'L0_xattn_Wk': _L0_xattn_in['Wk'], 'L0_xattn_bk': _L0_xattn_in['bk'], 'L0_xattn_Wv': _L0_xattn_in['Wv'], 'L0_xattn_bv': _L0_xattn_in['bv'], 'L0_xattn_Wo': _L0_xattn_in['Wo'], 'L0_xattn_qn_w': _L0_xattn_in['qn_w'], 'L0_xattn_kn_w': _L0_xattn_in['kn_w'], 'L0_ffn_gate_w': _L0_ffn_in['gate_w'], 'L0_ffn_gu_w': _L0_ffn_in['gu_w'], 'L0_ffn_dp_w': _L0_ffn_in['dp_w'], 'L0_ffn_sh_gate_w': _L0_ffn_in['sh_gate_w'], 'L0_ffn_sh_up_w': _L0_ffn_in['sh_up_w'], 'L0_ffn_sh_down_w': _L0_ffn_in['sh_down_w'], 'L0_ffn_sh_gate1_w': _L0_ffn_in['sh_gate1_w']}

def reference(x, ctx_2048, mask_1xSxS2_ff0, L0_attn_qkv, L0_attn_o_proj, L0_attn_gamma, L0_attn_beta, L0_xattn_Wq, L0_xattn_bq, L0_xattn_Wk, L0_xattn_bk, L0_xattn_Wv, L0_xattn_bv, L0_xattn_Wo, L0_xattn_qn_w, L0_xattn_kn_w, L0_ffn_gate_w, L0_ffn_gu_w, L0_ffn_dp_w, L0_ffn_sh_gate_w, L0_ffn_sh_up_w, L0_ffn_sh_down_w, L0_ffn_sh_gate1_w):
    import jax
    import jax.numpy as jnp

    def _L0_attn_ref(x, qkv, o_proj, gamma, beta):
        import jax, jax.numpy as jnp
        import numpy as np
        HIDDEN = 256
        KEY = 256
        EPS = 1e-05
        residual = x
        mu = jnp.mean(x, axis=-1, keepdims=True)
        var = jnp.mean((x - mu) ** 2, axis=-1, keepdims=True)
        x_norm = (x - mu) / jnp.sqrt(var + EPS) * gamma + beta
        q = x_norm @ qkv[:, :KEY]
        k = x_norm @ qkv[:, KEY:2 * KEY]
        v = x_norm @ qkv[:, 2 * KEY:]
        scale = 1.0 / jnp.sqrt(jnp.float32(KEY))
        scores = jnp.einsum('bsk,btk->bst', q, k) * scale
        S_len = x.shape[1]
        causal = jnp.tril(jnp.ones((S_len, S_len), dtype=bool))
        scores = jnp.where(causal[None], scores, -jnp.inf)
        attn = jax.nn.softmax(scores, axis=-1)
        out = attn @ v
        out = out @ o_proj
        return out + residual

    def _L0_xattn_ref(hidden_states, encoder_hidden_states, attention_mask, Wq, bq, Wk, bk, Wv, bv, Wo, qn_w, kn_w):
        import jax, jax.numpy as jnp
        import numpy as np
        H = 256
        NH = 16
        NKV = 4
        HD = 128
        GROUPS = NH // NKV
        EPS = 1e-06
        B, S, SE = (1, 256, 512)

        def _rmsnorm(x, w, eps=EPS):
            xf = x.astype(jnp.float32)
            var = jnp.mean(xf * xf, axis=-1, keepdims=True)
            return (xf * jax.lax.rsqrt(var + eps)).astype(x.dtype) * w
        b, s, _ = hidden_states.shape
        se = encoder_hidden_states.shape[1]
        q = (hidden_states @ Wq + bq).reshape(b, s, NH, HD).transpose(0, 2, 1, 3)
        k = (encoder_hidden_states @ Wk + bk).reshape(b, se, NKV, HD).transpose(0, 2, 1, 3)
        v = (encoder_hidden_states @ Wv + bv).reshape(b, se, NKV, HD).transpose(0, 2, 1, 3)
        k = jnp.repeat(k, GROUPS, axis=1)
        v = jnp.repeat(v, GROUPS, axis=1)
        q = _rmsnorm(q, qn_w)
        k = _rmsnorm(k, kn_w)
        scale = 1.0 / np.sqrt(HD).astype(np.float32)
        scores = jnp.einsum('bhsd,bhed->bhse', q, k) * scale
        scores = scores + attention_mask[:, None, :, :]
        probs = jax.nn.softmax(scores.astype(jnp.float32), axis=-1).astype(q.dtype)
        out = jnp.einsum('bhse,bhed->bhsd', probs, v)
        out = out.transpose(0, 2, 1, 3).reshape(b, s, NH * HD)
        return out @ Wo

    def _L0_ffn_ref(h, gate_w, gu_w, dp_w, sh_gate_w, sh_up_w, sh_down_w, sh_gate1_w):
        import jax, jax.numpy as jnp
        import numpy as np
        H = 256
        E = 64
        I = 64
        SI = 64
        TOP_K = 8
        B, T = (2, 64)
        Bb, Tt, Hh = h.shape
        x = h.reshape(Bb * Tt, Hh)
        N = x.shape[0]
        logits = x @ gate_w.T
        topv, topi = jax.lax.top_k(logits, TOP_K)
        rw = jax.nn.softmax(topv.astype(jnp.float32), axis=-1).astype(x.dtype)
        W = jnp.zeros((N, E), x.dtype).at[jnp.arange(N)[:, None], topi].set(rw)
        gu = jnp.einsum('nh,eih->nei', x, gu_w)
        gate, up = (gu[..., :I], gu[..., I:])
        inter = jax.nn.silu(gate) * up
        inter_w = inter * W[:, :, None]
        out = jnp.einsum('nei,ehi->nh', inter_w, dp_w)
        sh_inter = jax.nn.silu(x @ sh_gate_w.T) * (x @ sh_up_w.T)
        sh_out = sh_inter @ sh_down_w.T
        sh_g = jax.nn.sigmoid(x @ sh_gate1_w.T)
        out = out + sh_g * sh_out
        return out.reshape(Bb, Tt, Hh)
    x = _layernorm(x + _L0_attn_ref(x, L0_attn_qkv, L0_attn_o_proj, L0_attn_gamma, L0_attn_beta), axis=-1)
    x = _layernorm(x + _L0_xattn_ref(x, ctx_2048, mask_1xSxS2_ff0, L0_xattn_Wq, L0_xattn_bq, L0_xattn_Wk, L0_xattn_bk, L0_xattn_Wv, L0_xattn_bv, L0_xattn_Wo, L0_xattn_qn_w, L0_xattn_kn_w), axis=-1)
    x = _layernorm(x + _L0_ffn_ref(x, L0_ffn_gate_w, L0_ffn_gu_w, L0_ffn_dp_w, L0_ffn_sh_gate_w, L0_ffn_sh_up_w, L0_ffn_sh_down_w, L0_ffn_sh_gate1_w), axis=-1)
    return x

_drawn_inputs = setup_inputs


def setup_inputs(seed=0):
    import zlib

    import numpy as np

    out = dict(_drawn_inputs(seed))
    spreads = {'L0_attn_gamma': (1.0, 0.6),
     'L0_attn_beta': (0.0, 0.571),
     'L0_xattn_qn_w': (1.0, 0.6),
     'L0_xattn_kn_w': (1.0, 0.6)}
    factors = {'L0_xattn_bq': 8.0,
     'L0_xattn_bk': 8.0,
     'L0_xattn_bv': 3.302,
     'L0_ffn_gate_w': 8.0,
     'L0_ffn_gu_w': 8.0,
     'L0_ffn_dp_w': 8.0,
     'L0_ffn_sh_gate_w': 8.0,
     'L0_ffn_sh_up_w': 8.0,
     'L0_ffn_sh_down_w': 8.0,
     'L0_ffn_sh_gate1_w': 8.0}
    for name, (base, spread) in spreads.items():
        noise = np.random.default_rng([zlib.crc32(name.encode()), seed]).standard_normal(out[name].shape)
        drawn = base * np.exp(spread * noise) if base else spread * noise
        out[name] = jnp.asarray(drawn.astype(out[name].dtype))
    for name, factor in factors.items():
        out[name] = (out[name] * factor).astype(out[name].dtype)
    return out
```

```python
from contextlib import ExitStack

import concourse.bass as bass
from concourse import mybir

F32 = mybir.dt.float32
F32R = mybir.dt.float32r
BF16 = mybir.dt.bfloat16
ALU = mybir.AluOpType
ACT = mybir.ActivationFunctionType
AX = mybir.AxisListType

P = 128
B, S, D = 64, 64, 256
C = D // P
N = B * S
TILES = N // P
HEADS, KV, HD = 16, 4, 128
PAIRS = HEADS // 2
QW, KW = HEADS * HD, KV * HD
EXPERTS, INNER, TOP_K = 64, 64, 8
EPAIRS = EXPERTS // 2 + 1
GROUP = 3
GROUPS = EPAIRS // GROUP
BLOCK = 512
BLOCKS = N // BLOCK
ROUNDS = BLOCKS // 2
UNITS = 2 * GROUP
LN_EPS, RMS_EPS = 1e-5, 1e-6
SELF_SCALE = float(D) ** -0.5
MASKED = -1e30
REMOVED = -3e38
HI, LO = 0, 1
PASSES = ((HI, HI), (LO, HI), (HI, LO))


def decoder(nc, x, ctx, mask, qkv, o_proj, gamma, beta, wq, bq, wk, bk, wv, bv, wo, qn_w, kn_w, router, gate_up,
            down, out):
    x2t_d = nc.dram_tensor("x2t_scratch", [P, C, N], F32).ap()
    wt_d = nc.dram_tensor("route_weight_scratch", [P, N], F32).ap()
    sh_d = nc.dram_tensor("shared_gate_scratch", [2, N], F32).ap()
    attention = {name: nc.alloc_semaphore(name) for name in ATTENTION_SIGNALS}
    attention_phase(nc, attention, x, ctx, mask, qkv, o_proj, gamma, beta, wq, bq, wk, bk, wv, bv, wo, qn_w, kn_w,
                    router, x2t_d, wt_d, sh_d)
    nc.clear_and_free_semaphores(list(attention.values()))
    nc.all_engine_barrier()
    expert = {name: nc.alloc_semaphore(name) for name in EXPERT_SIGNALS}
    acc_loaded = [nc.alloc_semaphore(f"acc_loaded{b}") for b in range(BLOCKS)]
    expert_phase(nc, expert, acc_loaded, gate_up, down, x2t_d, wt_d, sh_d, out)


def wait_alone(eng, signal, count, held):
    eng.wait_ge(signal, count)
    eng.sem_inc(held)


ATTENTION_SIGNALS = """
dve_held pool_held
qkv_loaded wkv_loaded wq_loaded wo_loaded small_loaded qkv_hi qkv_lo wkv_hi wkv_lo wq_hi wq_lo wo_hi wo_lo
key_scale_a key_scale constants identity_zeroed identity_made causal_zeroed causal_half causal_made
x_loaded x_kept x_stats x_moments x_var x_rstd x_hat x_scaled x_normed xn_transposed xn_hi xn_lo
qk_projected v_projected qk_copied v_copied qk_transposed qkt_copied self_scored self_masked self_max self_bias
self_exp self_recip self_probs self_pt self_pt_copied self_out self_ot self_proj h1_done h1_stats h1_moments h1_var
h1_rstd x1_normed x1_transposed x1_hi x1_lo x1_kept
ctx_loaded ctx_transposed ctx_hi ctx_lo k_projected v2_projected k_biased v2_biased k_squared k_sumsq k_var k_rstd
k_normed k_transposed kt_copied q_projected q_biased q_squared q_sumsq q_var q_rstd q_normed_a q_normed_b q_transposed
qt_copied scored cross_masked cross_max cross_shifted cross_exp cross_sum cross_recip cross_probs cross_pt
cross_pt_copied cross_out ot_hi ot_lo cross_proj h2_done h2_stats h2_moments h2_var h2_rstd x2_normed x2_transposed
x2t_copied x2_stored routed logits_copied top8 top_removed top_mask top_bias route_exp shared_exp route_kept route_sum
shared_plus route_recip shared_gate route_w split_hi split_lo w_transposed wt_copied wt_stored sh_stored
""".split()


def attention_phase(nc, sig, x, ctx, mask, qkv, o_proj, gamma, beta, wq, bq, wk, bk, wv, bv, wo, qn_w, kn_w, router,
                    x2t_d, wt_d, sh_d):
    with ExitStack() as stack:
        def sb(name, shape, dt=F32):
            return stack.enter_context(nc.sbuf_tensor(name, shape, dt))

        qkv_w = [sb(f"qkv_w{n}", [P, C, 3 * D], F32R) for n in (HI, LO)]
        wq_w = [sb(f"wq_w{n}", [P, C, QW], F32R) for n in (HI, LO)]
        wkv_w = [sb(f"wkv_w{n}", [P, C, 2 * KW], F32R) for n in (HI, LO)]
        wo_w = [sb(f"wo_w{n}", [P, HEADS, D], F32R) for n in (HI, LO)]
        o_w = sb("o_w", [P, C, D])
        router_w = sb("router_w", [P, C, EXPERTS + 1])
        stage_b = sb("stage_b", [P, HEADS * D])
        bq_b = sb("bq_b", [P, QW])
        bkv_b = sb("bkv_b", [P, 2 * KW])
        gamma_b = sb("gamma_b", [P, D])
        beta_b = sb("beta_b", [P, D])
        mask_t = sb("mask_t", [P, S])
        causal = sb("causal", [P, P])
        identity = sb("identity", [P, P])
        minus_half = sb("minus_half", [P, HEADS])
        qn_c = sb("qn_c", [P, 1])
        kn_c = sb("kn_c", [P, 1])
        key_scale = sb("key_scale", [P, 1])

        x_in = sb("x_in", [P, D])
        x_keep = sb("x_keep", [P, D])
        x_stat = sb("x_stat", [P, 6])
        x_mv = sb("x_mv", [P, 2])
        x_ve = sb("x_ve", [P, 1])
        x_rs = sb("x_rs", [P, 1])
        x_hat = sb("x_hat", [P, D])
        x_g = sb("x_g", [P, D])
        x_n = sb("x_n", [P, D])
        xnt = [sb(f"xnt{n}", [P, C, P], F32R) for n in (HI, LO)]
        qk = sb("qk", [P, 2 * D])
        v = sb("v", [P, D])
        qkt = sb("qkt", [P, 2 * C, P])
        s1 = sb("s1", [P, P])
        s1_max = sb("s1_max", [P, 1])
        s1_bias = sb("s1_bias", [P, 1])
        p1 = sb("p1", [P, P])
        p1_sum = sb("p1_sum", [P, 1])
        p1_rec = sb("p1_rec", [P, 1])
        p1n = sb("p1n", [P, P])
        p1t = sb("p1t", [P, P])
        o1t = sb("o1t", [P, C, P])
        h1 = sb("h1", [P, D])
        h1_stat = sb("h1_stat", [P, 6])
        h1_mv = sb("h1_mv", [P, 2])
        h1_ve = sb("h1_ve", [P, 1])
        h1_rs = sb("h1_rs", [P, 1])
        x1 = sb("x1", [P, D])
        x1t = [sb(f"x1t{n}", [P, C, P], F32R) for n in (HI, LO)]

        ctx_in = sb("ctx_in", [P, D])
        x1_keep = sb("x1_keep", [P, D])
        ctxt = [sb(f"ctxt{n}", [P, C, P], F32R) for n in (HI, LO)]
        k2 = sb("k2", [P, KV, HD])
        v2 = sb("v2", [P, KV, HD])
        k2s = sb("k2s", [P, KV, HD])
        k2_ss = sb("k2_ss", [P, KV])
        k2_ve = sb("k2_ve", [P, KV])
        k2_rs = sb("k2_rs", [P, KV])
        k2t = sb("k2t", [P, KV, P])
        q_work = sb("q_work", [P, 2 * QW])
        q2 = q_work[:, 0:QW].rearrange("p (h d) -> p h d", d=HD)
        q2s = q_work[:, QW:2 * QW].rearrange("p (h d) -> p h d", d=HD)
        q2_ss = sb("q2_ss", [P, HEADS])
        q2_ve = sb("q2_ve", [P, HEADS])
        q2_rs = sb("q2_rs", [P, HEADS])
        q2t = stage_b[:, 0:QW].rearrange("p (b h s) -> p b h s", b=2, s=S)
        s2 = stage_b[:, QW:QW + PAIRS * P].rearrange("p (a b e) -> p a b e", b=2, e=S)
        p2t = stage_b[:, QW + PAIRS * P:QW + 2 * PAIRS * P].rearrange("p (a n) -> p a n", n=P)
        s2_max = sb("s2_max", [P, HEADS])
        s2_sum = sb("s2_sum", [P, HEADS])
        s2_rec = sb("s2_rec", [P, HEADS])
        o2t = [sb(f"o2t{n}", [P, HEADS, P], F32R) for n in (HI, LO)]
        h2 = sb("h2", [P, D])
        h2_stat = sb("h2_stat", [P, 6])
        h2_mv = sb("h2_mv", [P, 2])
        h2_ve = sb("h2_ve", [P, 1])
        h2_rs = sb("h2_rs", [P, 1])
        x2 = sb("x2", [P, D])
        x2t = sb("x2t", [P, C, P])
        logits = sb("logits", [P, EXPERTS + 1])
        top = sb("top", [P, TOP_K])
        rest = sb("rest", [P, EXPERTS])
        chosen = sb("chosen", [P, EXPERTS])
        top_neg = sb("top_neg", [P, 1])
        rexp = sb("rexp", [P, EXPERTS])
        rkept = sb("rkept", [P, EXPERTS])
        rsum = sb("rsum", [P, 1])
        rrec = sb("rrec", [P, 1])
        route = sb("route", [P, EXPERTS + 1])
        sh_e = sb("sh_e", [P, 1])
        sh_p = sb("sh_p", [P, 1])
        split = sb("split", [P, 2 * EXPERTS + 2], F32R)
        wt = sb("wt", [P, P])
        sht = sb("sht", [2, P])

        bank_xa = stack.enter_context(nc.psum_tensor("bank_xa", [P, 512], F32))
        bank_xb = stack.enter_context(nc.psum_tensor("bank_xb", [P, 512], F32))
        bank_c = stack.enter_context(nc.psum_tensor("bank_c", [P, 512], F32))
        bank_d = stack.enter_context(nc.psum_tensor("bank_d", [P, 512], F32))
        banks = stack.enter_context(nc.psum_tensor("banks_q", [P, 4, 512], F32))

        def split3(w):
            return w.rearrange("(c p) n -> p c n", p=P)

        def flat(a):
            return a.rearrange("p a b -> p (a b)")

        half = HEADS // 2
        block = stack.enter_context(nc.Block())

        @block.sync
        def _(sp):
            def load_x(t):
                sp.wait_ge(sig["x_hat"], t)
                sp.wait_ge(sig["x_kept"], t)
                sp.dma_start(x_in[:, :], x[bass.ts(t, P), :]).then_inc(sig["x_loaded"], 16)

            def load_ctx(t):
                sp.wait_ge(sig["ctx_transposed"], t)
                sp.dma_start(ctx_in[:, :], ctx[bass.ts(t, P), :]).then_inc(sig["ctx_loaded"], 16)

            def store(t):
                sp.wait_ge(sig["x2t_copied"], t + 1)
                sp.dma_start(x2t_d[:, :, bass.ts(t, P)], x2t[:, :, :]).then_inc(sig["x2_stored"], 16)
                sp.wait_ge(sig["wt_copied"], t + 1)
                sp.dma_start(wt_d[:, bass.ts(t, P)], wt[:, :]).then_inc(sig["wt_stored"], 16)
                sp.dma_start(sh_d[:, bass.ts(t, P)], sht[:, :]).then_inc(sig["sh_stored"], 16)

            sp.dma_start(q_work[:, 0:C * 3 * D].rearrange("p (c n) -> p c n", c=C), split3(qkv))\
              .then_inc(sig["qkv_loaded"], 16)
            sp.dma_start(x_in[:, :], x[0:P, :]).then_inc(sig["x_loaded"], 16)
            kv_stage = stage_b[:, 0:C * 2 * KW].rearrange("p (c n) -> p c n", c=C)
            sp.dma_start(kv_stage[:, :, 0:KW], split3(wk)).then_inc(sig["wkv_loaded"], 16)
            sp.dma_start(kv_stage[:, :, KW:2 * KW], split3(wv)).then_inc(sig["wkv_loaded"], 16)
            sp.dma_start(ctx_in[:, :], ctx[0:P, :]).then_inc(sig["ctx_loaded"], 16)
            sp.wait_ge(sig["qkv_lo"], 1)
            sp.dma_start(q_work[:, :].rearrange("p (c n) -> p c n", c=C), split3(wq)).then_inc(sig["wq_loaded"], 16)
            sp.wait_ge(sig["wkv_lo"], 1)
            sp.dma_start(stage_b[:, :].rearrange("p (h n) -> p h n", h=HEADS),
                         wo.rearrange("(h p) n -> p h n", p=P)).then_inc(sig["wo_loaded"], 16)
            load_x(1)
            with sp.Fori(1, TILES - 1) as t:
                load_ctx(t)
                load_x(t + 1)
                store(t - 1)
            load_ctx(TILES - 1)
            store(TILES - 2)
            store(TILES - 1)
            for name in ("x2_stored", "wt_stored", "sh_stored"):
                sp.wait_ge(sig[name], 16 * TILES)

        @block.gpsimd
        def _(pool):
            for part, source in ((gamma_b, gamma), (beta_b, beta), (bq_b, bq), (bkv_b[:, 0:KW], bk),
                                 (bkv_b[:, KW:2 * KW], bv)):
                pool.dma_start(part if isinstance(part, bass.AP) else part[:, :], source.partition_broadcast(P))\
                    .then_inc(sig["small_loaded"], 16)
            for n in range(2):
                pool.dma_start(mask_t[n * S:(n + 1) * S, :], mask).then_inc(sig["small_loaded"], 16)
            pool.dma_start(qn_c[:, :], qn_w.rearrange("(p a) -> p a", a=1)).then_inc(sig["small_loaded"], 16)
            pool.dma_start(kn_c[:, :], kn_w.rearrange("(p a) -> p a", a=1)).then_inc(sig["small_loaded"], 16)
            pool.dma_start(o_w[:, :, :], split3(o_proj)).then_inc(sig["small_loaded"], 16)
            pool.dma_start(router_w[:, :, :], split3(router)).then_inc(sig["small_loaded"], 16)
            nc.gpsimd.memset(minus_half[:, :], -0.5).then_inc(sig["constants"], 1)
            nc.gpsimd.memset(identity[:, :], 0.0).then_inc(sig["identity_zeroed"], 1)
            nc.gpsimd.memset(causal[:, :], 0.0).then_inc(sig["causal_zeroed"], 1)
            pool.wait_ge(sig["identity_zeroed"], 1)
            nc.gpsimd.affine_select(out=identity[:, :], in_=identity[:, :], compare_op=ALU.not_equal, fill=1.0,
                                    base=0, pattern=[[-1, P]], channel_multiplier=1).then_inc(sig["identity_made"], 1)
            pool.wait_ge(sig["causal_zeroed"], 1)
            nc.gpsimd.affine_select(out=causal[:, :], in_=causal[:, :], compare_op=ALU.is_ge, fill=MASKED,
                                    base=0, pattern=[[-1, P]], channel_multiplier=1).then_inc(sig["causal_half"], 1)
            pool.wait_ge(sig["causal_half"], 1)
            nc.gpsimd.affine_select(out=causal[:, 0:S], in_=causal[:, 0:S], compare_op=ALU.is_ge, fill=MASKED,
                                    base=S - 1, pattern=[[0, S]], channel_multiplier=-1)\
                .then_inc(sig["causal_made"], 1)
            pool.wait_ge(sig["constants"], 1)
            pool.wait_ge(sig["small_loaded"], 16 * 11)

            def power(done, out_, base, width, start, n1):
                pool.wait_ge(sig[start], n1)
                nc.gpsimd.tensor_tensor(out_, base, minus_half[:, 0:width], ALU.pow).then_inc(sig[done], 1)

            def norm_x(t):
                pool.wait_ge(sig["x_loaded"], 16 * t + 16)
                wait_alone(pool, sig["h1_done"], t, sig["pool_held"])
                nc.gpsimd.tensor_copy(x_keep[:, :], x_in[:, :]).then_inc(sig["x_kept"], 1)
                power("x_rstd", x_rs[:, :], x_ve[:, :], 1, "x_var", t + 1)
                pool.wait_ge(sig["x_hat"], t + 1)
                nc.gpsimd.tensor_tensor(x_g[:, :], x_hat[:, :], gamma_b[:, :], ALU.mult).then_inc(sig["x_scaled"], 1)
                pool.wait_ge(sig["x_scaled"], t + 1)
                nc.gpsimd.tensor_tensor(x_n[:, :], x_g[:, :], beta_b[:, :], ALU.add).then_inc(sig["x_normed"], 1)

            def keep_x1(t):
                pool.wait_ge(sig["x1_normed"], t + 1)
                wait_alone(pool, sig["h2_done"], t, sig["pool_held"])
                nc.gpsimd.tensor_copy(x1_keep[:, :], x1[:, :]).then_inc(sig["x1_kept"], 1)

            def norm_keys(t):
                pool.wait_ge(sig["k_biased"], t + 1)
                nc.gpsimd.tensor_tensor(k2s[:, :, :], k2[:, :, :], k2[:, :, :], ALU.mult).then_inc(sig["k_squared"], 1)
                power("k_rstd", k2_rs[:, :], k2_ve[:, :], KV, "k_var", t + 1)
                pool.wait_ge(sig["k_rstd"], t + 1)
                nc.gpsimd.tensor_tensor(k2s[:, :, :], k2[:, :, :], k2_rs[:, :].unsqueeze(2).to_broadcast([P, KV, HD]),
                                        ALU.mult).then_inc(sig["k_normed"], 1)

            def norm_queries(t):
                power("q_rstd", q2_rs[:, :], q2_ve[:, :], HEADS, "q_var", t + 1)
                pool.wait_ge(sig["q_rstd"], t + 1)
                nc.gpsimd.tensor_tensor(q2s[:, half:, :], q2[:, half:, :],
                                        q2_rs[:, half:].unsqueeze(2).to_broadcast([P, half, HD]),
                                        ALU.mult).then_inc(sig["q_normed_b"], 1)

            def norm_h1(t):
                power("h1_rstd", h1_rs[:, :], h1_ve[:, :], 1, "h1_var", t + 1)

            def norm_h2(t):
                power("h2_rstd", h2_rs[:, :], h2_ve[:, :], 1, "h2_var", t + 1)

            def step(t, u):
                if t is not None:
                    norm_x(t)
                if u is not None:
                    keep_x1(u)
                    norm_keys(u)
                    norm_queries(u)
                if t is not None:
                    norm_h1(t)
                if u is not None:
                    norm_h2(u)

            step(0, None)
            with pool.Fori(1, TILES) as t:
                step(t, t - 1)
            step(None, TILES - 1)

        @block.tensor
        def _(pe):
            def transpose_in(target, source):
                for c in range(C):
                    last = nc.tensor.transpose(target[:, c * P:(c + 1) * P], source[:, c * P:(c + 1) * P],
                                               identity[:, :])
                return last

            def product(target, left, right):
                for n, (a, b) in enumerate(PASSES):
                    for c in range(C):
                        last = nc.tensor.matmul(target, left[a][:, c, :], right(b, c), start=(n == 0 and c == 0),
                                                stop=(n == len(PASSES) - 1 and c == C - 1))
                return last

            def x_transpose(t):
                pe.wait_ge(sig["x_normed"], t + 1)
                pe.wait_ge(sig["x1_lo"], t)
                transpose_in(bank_xa, x_n).then_inc(sig["xn_transposed"], 1)

            def self_project(t):
                pe.wait_ge(sig["xn_lo"], t + 1)
                product(bank_xb[:, :], xnt, lambda b, c: qkv_w[b][:, c, 0:2 * D]).then_inc(sig["qk_projected"], 1)
                product(bank_xa[:, 0:D], xnt, lambda b, c: qkv_w[b][:, c, 2 * D:3 * D])\
                    .then_inc(sig["v_projected"], 1)

            def self_transpose(t):
                pe.wait_ge(sig["qk_copied"], t + 1)
                for c in range(2 * C):
                    last = nc.tensor.transpose(bank_xb[:, c * P:(c + 1) * P], qk[:, c * P:(c + 1) * P], identity[:, :])
                last.then_inc(sig["qk_transposed"], 1)

            def self_score(t):
                pe.wait_ge(sig["qkt_copied"], t + 1)
                pe.wait_ge(sig["v_copied"], t + 1)
                for c in range(C):
                    last = nc.tensor.matmul(bank_xa[:, D:D + P], qkt[:, c, :], qkt[:, C + c, :], start=(c == 0),
                                            stop=(c == C - 1))
                last.then_inc(sig["self_scored"], 1)

            def self_probs_transpose(t):
                pe.wait_ge(sig["self_probs"], t + 1)
                nc.tensor.transpose(bank_xb[:, 0:P], p1n[:, :], identity[:, :]).then_inc(sig["self_pt"], 1)

            def self_attend(t):
                pe.wait_ge(sig["self_pt_copied"], t + 1)
                for c in range(C):
                    last = nc.tensor.matmul(bank_xa[:, c * P:(c + 1) * P], v[:, c * P:(c + 1) * P], p1t[:, :],
                                            start=True, stop=True)
                last.then_inc(sig["self_out"], 1)

            def self_output(t):
                pe.wait_ge(sig["self_ot"], t + 1)
                for c in range(C):
                    last = nc.tensor.matmul(bank_xb[:, 0:D], o1t[:, c, :], o_w[:, c, :], start=(c == 0),
                                            stop=(c == C - 1))
                last.then_inc(sig["self_proj"], 1)

            def x1_transpose(t):
                pe.wait_ge(sig["x1_normed"], t + 1)
                transpose_in(bank_xa, x1).then_inc(sig["x1_transposed"], 1)

            def ctx_transpose(t):
                pe.wait_ge(sig["ctx_loaded"], 16 * t + 16)
                transpose_in(bank_c, ctx_in).then_inc(sig["ctx_transposed"], 1)

            def key_project(t):
                pe.wait_ge(sig["ctx_lo"], t + 1)
                pe.wait_ge(sig["wt_copied"], t)
                product(bank_d[:, :], ctxt, lambda b, c: wkv_w[b][:, c, 0:KW]).then_inc(sig["k_projected"], 1)
                product(bank_c[:, :], ctxt, lambda b, c: wkv_w[b][:, c, KW:2 * KW]).then_inc(sig["v2_projected"], 1)

            def query_project(t):
                pe.wait_ge(sig["x1_lo"], t + 1)
                pe.wait_ge(sig["ot_lo"], 2 * t)
                for g in range(KV):
                    product(banks[:, g, :], x1t, lambda b, c: wq_w[b][:, c, g * 512:(g + 1) * 512])\
                        .then_inc(sig["q_projected"], 1)

            def key_transpose(t):
                pe.wait_ge(sig["k_normed"], t + 1)
                for g in range(KV):
                    last = nc.tensor.transpose(bank_d[:, g * P:(g + 1) * P], k2s[:, g, :], identity[:, :])
                last.then_inc(sig["k_transposed"], 1)

            def query_transpose(t):
                for n, normed in enumerate(("q_normed_a", "q_normed_b")):
                    pe.wait_ge(sig[normed], t + 1)
                    for h in range(n * half, (n + 1) * half):
                        last = nc.tensor.transpose(banks[:, h // 4, (h % 4) * P:(h % 4 + 1) * P], q2s[:, h, :],
                                                   identity[:, :])
                    last.then_inc(sig["q_transposed"], 1)

            def cross_score(t):
                pe.wait_ge(sig["kt_copied"], t + 1)
                pe.wait_ge(sig["qt_copied"], 2 * t + 2)
                for n in range(2):
                    for p in range(PAIRS):
                        last = nc.tensor.matmul(banks[:, n, p * S:(p + 1) * S],
                                                q2t[:, n, 2 * p:2 * p + 2, :].rearrange("p h s -> p (h s)"),
                                                k2t[:, p // 2, n * S:(n + 1) * S], start=True, stop=True)
                    last.then_inc(sig["scored"], 1)

            def cross_probs_transpose(t):
                pe.wait_ge(sig["cross_probs"], t + 1)
                for p in range(PAIRS):
                    last = nc.tensor.transpose(banks[:, 2 + p // 4, (p % 4) * P:(p % 4 + 1) * P],
                                               s2[:, p, :, :].rearrange("p a b -> p (a b)"), identity[:, :])
                last.then_inc(sig["cross_pt"], 1)

            def cross_attend(t):
                pe.wait_ge(sig["cross_pt_copied"], t + 1)
                for n in range(2):
                    for g in range(KV):
                        last = nc.tensor.matmul(banks[:, 2 * n + g // 2, (g % 2) * 256:(g % 2 + 1) * 256],
                                                v2[n * S:(n + 1) * S, g, :], p2t[n * S:(n + 1) * S, 2 * g:2 * g + 2, :],
                                                start=True, stop=True)
                    last.then_inc(sig["cross_out"], 1)

            def cross_output(t):
                pe.wait_ge(sig["ot_lo"], 2 * t + 2)
                for n, (a, b) in enumerate(PASSES):
                    for h in range(HEADS):
                        last = nc.tensor.matmul(bank_c[:, 0:D], o2t[a][:, h, :], wo_w[b][:, h, :],
                                                start=(n == 0 and h == 0),
                                                stop=(n == len(PASSES) - 1 and h == HEADS - 1))
                last.then_inc(sig["cross_proj"], 1)

            def x2_transpose(t):
                pe.wait_ge(sig["x2_normed"], t + 1)
                transpose_in(bank_d, x2).then_inc(sig["x2_transposed"], 1)

            def route_score(t):
                pe.wait_ge(sig["x2t_copied"], t + 1)
                for c in range(C):
                    last = nc.tensor.matmul(bank_c[:, D:D + EXPERTS + 1], x2t[:, c, :], router_w[:, c, :],
                                            start=(c == 0), stop=(c == C - 1))
                last.then_inc(sig["routed"], 1)

            def route_transpose(t):
                pe.wait_ge(sig["split_lo"], t + 1)
                parts = split[:, :].bitcast(F32)
                nc.tensor.transpose(bank_d[:, D:D + P], parts[:, 0:P], identity[:, :])
                nc.tensor.transpose(bank_d[0:2, D + P:D + 2 * P], parts[:, P:P + 2], identity[:, :])\
                    .then_inc(sig["w_transposed"], 1)

            def step(t, u):
                if t is not None:
                    x_transpose(t)
                if u is not None:
                    ctx_transpose(u)
                if t is not None:
                    self_project(t)
                if u is not None:
                    key_project(u)
                if t is not None:
                    self_transpose(t)
                if u is not None:
                    query_project(u)
                    key_transpose(u)
                if t is not None:
                    self_score(t)
                if u is not None:
                    query_transpose(u)
                if t is not None:
                    self_probs_transpose(t)
                if u is not None:
                    cross_score(u)
                if t is not None:
                    self_attend(t)
                    self_output(t)
                if u is not None:
                    cross_probs_transpose(u)
                    cross_attend(u)
                if t is not None:
                    x1_transpose(t)
                if u is not None:
                    cross_output(u)
                    x2_transpose(u)
                    route_score(u)
                    route_transpose(u)

            pe.wait_ge(sig["identity_made"], 1)
            pe.wait_ge(sig["small_loaded"], 16 * 11)
            pe.wait_ge(sig["qkv_lo"], 1)
            step(0, None)
            pe.wait_ge(sig["wkv_lo"], 1)
            pe.wait_ge(sig["wq_lo"], 1)
            pe.wait_ge(sig["wo_lo"], 1)
            with pe.Fori(1, TILES) as t:
                step(t, t - 1)
            step(None, TILES - 1)

        @block.scalar
        def _(act):
            def copy(done, target, source, start, count):
                act.wait_ge(sig[start], count)
                nc.scalar.activation(target, source, ACT.Copy).then_inc(sig[done], 1)

            def self_exp(t):
                act.wait_ge(sig["self_bias"], t + 1)
                nc.scalar.activation(p1[:, :], s1[:, :], ACT.Exp, bias=s1_bias[:, :], scale=SELF_SCALE,
                                     accum_out=p1_sum[:, :]).then_inc(sig["self_exp"], 1)

            def square_queries(t):
                for n in range(2):
                    act.wait_ge(sig["q_biased"], 2 * t + n + 1)
                    nc.scalar.activation(q2s[:, n * half:(n + 1) * half, :], q2[:, n * half:(n + 1) * half, :],
                                         ACT.Square).then_inc(sig["q_squared"], 1)

            def copy_keys(t):
                act.wait_ge(sig["k_transposed"], t + 1)
                nc.scalar.activation(flat(k2t[:, :, :]), bank_d[:, :], ACT.Copy, scale=key_scale[:, :])\
                    .then_inc(sig["kt_copied"], 1)

            def copy_queries(t):
                for n in range(2):
                    copy("qt_copied", q2t[:, :, n * half:(n + 1) * half, :].rearrange("p b h s -> p h b s"),
                         flat(banks[:, 2 * n:2 * n + 2, :]).rearrange("p (h b s) -> p h b s", b=2, s=S),
                         "q_transposed", 2 * t + n + 1)

            def cross_exp(t):
                act.wait_ge(sig["cross_shifted"], t + 1)
                nc.scalar.activation(s2[:, :, :, :].rearrange("p a b c -> p (a b c)"),
                                     s2[:, :, :, :].rearrange("p a b c -> p (a b c)"), ACT.Exp)\
                    .then_inc(sig["cross_exp"], 1)

            def cross_out_high(t):
                for n in range(2):
                    copy("ot_hi", o2t[HI][:, :, n * S:(n + 1) * S],
                         banks[:, 2 * n:2 * n + 2, :].rearrange("p a (h s) -> p (a h) s", s=S), "cross_out",
                         2 * t + n + 1)

            def route_exp(t):
                act.wait_ge(sig["top_bias"], t + 1)
                nc.scalar.activation(rexp[:, :], logits[:, 0:EXPERTS], ACT.Exp, bias=top_neg[:, :])\
                    .then_inc(sig["route_exp"], 1)
                nc.scalar.activation(sh_e[:, :], logits[:, EXPERTS:EXPERTS + 1], ACT.Exp, scale=-1.0)\
                    .then_inc(sig["shared_exp"], 1)

            def route_split(t):
                act.wait_ge(sig["shared_gate"], t + 1)
                act.wait_ge(sig["route_w"], t + 1)
                nc.scalar.activation(split[:, 0:EXPERTS], route[:, 0:EXPERTS], ACT.Copy)
                nc.scalar.activation(split[:, 2 * EXPERTS:2 * EXPERTS + 1], route[:, EXPERTS:EXPERTS + 1], ACT.Copy)\
                    .then_inc(sig["split_hi"], 1)

            def route_store(t):
                act.wait_ge(sig["w_transposed"], t + 1)
                act.wait_ge(sig["wt_stored"], 16 * t)
                act.wait_ge(sig["sh_stored"], 16 * t)
                nc.scalar.activation(wt[:, :], bank_d[:, D:D + P], ACT.Copy)
                nc.scalar.activation(sht[:, :], bank_d[0:2, D + P:D + 2 * P], ACT.Copy).then_inc(sig["wt_copied"], 1)

            def step(t, u):
                if t is not None:
                    copy("xn_hi", flat(xnt[HI][:, :, :]), bank_xa[:, 0:D], "xn_transposed", t + 1)
                if u is not None:
                    copy("ctx_hi", flat(ctxt[HI][:, :, :]), bank_c[:, 0:D], "ctx_transposed", u + 1)
                if t is not None:
                    copy("qk_copied", qk[:, :], bank_xb[:, :], "qk_projected", t + 1)
                    copy("qkt_copied", flat(qkt[:, :, :]), bank_xb[:, :], "qk_transposed", t + 1)
                if u is not None:
                    square_queries(u)
                    copy_keys(u)
                if t is not None:
                    self_exp(t)
                if u is not None:
                    copy_queries(u)
                if t is not None:
                    copy("self_pt_copied", p1t[:, :], bank_xb[:, 0:P], "self_pt", t + 1)
                    copy("self_ot", flat(o1t[:, :, :]), bank_xa[:, 0:D], "self_out", t + 1)
                if u is not None:
                    cross_exp(u)
                    copy("cross_pt_copied", flat(p2t[:, :, :]), flat(banks[:, 2:4, :]), "cross_pt", u + 1)
                    cross_out_high(u)
                if t is not None:
                    copy("x1_hi", flat(x1t[HI][:, :, :]), bank_xa[:, 0:D], "x1_transposed", t + 1)
                if u is not None:
                    act.wait_ge(sig["x2_stored"], 16 * u)
                    copy("x2t_copied", flat(x2t[:, :, :]), bank_d[:, 0:D], "x2_transposed", u + 1)
                    route_exp(u)
                    route_split(u)
                    route_store(u)

            copy("qkv_hi", flat(qkv_w[HI][:, :, :]), q_work[:, 0:C * 3 * D], "qkv_loaded", 16)
            copy("wkv_hi", flat(wkv_w[HI][:, :, :]), stage_b[:, 0:C * 2 * KW], "wkv_loaded", 32)
            act.wait_ge(sig["small_loaded"], 16 * 11)
            copy("wq_hi", flat(wq_w[HI][:, :, :]), q_work[:, :], "wq_loaded", 16)
            copy("wo_hi", flat(wo_w[HI][:, :, :]), stage_b[:, :], "wo_loaded", 16)
            act.wait_ge(sig["key_scale"], 1)
            step(0, None)
            with act.Fori(1, TILES) as t:
                step(t, t - 1)
            step(None, TILES - 1)

        @block.vector
        def _(dve):
            def low(done, target, source, high, ready, count):
                dve.wait_ge(sig[ready], count)
                nc.vector.tensor_tensor(target, source, high.bitcast(F32), ALU.subtract).then_inc(sig[done], 1)

            def moments(source, stat, mv, ve, name, n1):
                nc.vector.bn_stats(stat[:, :], source[:, :]).then_inc(sig[name + "_stats"], 1)
                wait_alone(dve, sig[name + "_stats"], n1, sig["dve_held"])
                nc.vector.bn_aggr(mv[:, :], stat[:, :]).then_inc(sig[name + "_moments"], 1)
                dve.wait_ge(sig[name + "_moments"], n1)
                nc.vector.tensor_scalar_add(ve[:, :], mv[:, 1:2], LN_EPS).then_inc(sig[name + "_var"], 1)

            def normalise(done, target, source, mv, rs, name, n1):
                dve.wait_ge(sig[name + "_rstd"], n1)
                nc.vector.tensor_scalar(target[:, :], source[:, :], mv[:, 0:1], rs[:, :], ALU.subtract, ALU.mult)\
                    .then_inc(sig[done], 1)

            def x_norm(t):
                dve.wait_ge(sig["x_loaded"], 16 * t + 16)
                moments(x_in, x_stat, x_mv, x_ve, "x", t + 1)
                normalise("x_hat", x_hat, x_in, x_mv, x_rs, "x", t + 1)

            def x_low(t):
                low("xn_lo", flat(xnt[LO][:, :, :]), bank_xa[:, 0:D], flat(xnt[HI][:, :, :]), "xn_hi", t + 1)

            def copy_values(t):
                dve.wait_ge(sig["v_projected"], t + 1)
                nc.vector.tensor_copy(v[:, :], bank_xa[:, 0:D]).then_inc(sig["v_copied"], 1)

            def self_mask(t):
                dve.wait_ge(sig["self_scored"], t + 1)
                nc.vector.tensor_tensor(s1[:, :], bank_xa[:, D:D + P], causal[:, :], ALU.add)\
                    .then_inc(sig["self_masked"], 1)
                dve.wait_ge(sig["self_masked"], t + 1)
                nc.vector.reduce_max(s1_max[:, :], s1[:, :], AX.X).then_inc(sig["self_max"], 1)
                dve.wait_ge(sig["self_max"], t + 1)
                nc.vector.tensor_scalar_mul(s1_bias[:, :], s1_max[:, :], -SELF_SCALE).then_inc(sig["self_bias"], 1)

            def self_normalise(t):
                dve.wait_ge(sig["self_exp"], t + 1)
                nc.vector.reciprocal(p1_rec[:, :], p1_sum[:, :]).then_inc(sig["self_recip"], 1)
                dve.wait_ge(sig["self_recip"], t + 1)
                nc.vector.tensor_scalar_mul(p1n[:, :], p1[:, :], p1_rec[:, :]).then_inc(sig["self_probs"], 1)

            def x1_norm(t):
                dve.wait_ge(sig["self_proj"], t + 1)
                dve.wait_ge(sig["x_kept"], t + 1)
                nc.vector.scalar_tensor_tensor(h1[:, :], x_keep[:, :], 2.0, bank_xb[:, 0:D], ALU.mult, ALU.add)\
                    .then_inc(sig["h1_done"], 1)
                dve.wait_ge(sig["h1_done"], t + 1)
                moments(h1, h1_stat, h1_mv, h1_ve, "h1", t + 1)
                dve.wait_ge(sig["x1_kept"], t)
                normalise("x1_normed", x1, h1, h1_mv, h1_rs, "h1", t + 1)

            def x1_low(t):
                low("x1_lo", flat(x1t[LO][:, :, :]), bank_xa[:, 0:D], flat(x1t[HI][:, :, :]), "x1_hi", t + 1)

            def ctx_low(t):
                low("ctx_lo", flat(ctxt[LO][:, :, :]), bank_c[:, 0:D], flat(ctxt[HI][:, :, :]), "ctx_hi", t + 1)

            def bias_keys(t):
                dve.wait_ge(sig["k_projected"], t + 1)
                nc.vector.tensor_tensor(flat(k2[:, :, :]), bank_d[:, :], bkv_b[:, 0:KW], ALU.add)\
                    .then_inc(sig["k_biased"], 1)
                dve.wait_ge(sig["v2_projected"], t + 1)
                nc.vector.tensor_tensor(flat(v2[:, :, :]), bank_c[:, :], bkv_b[:, KW:2 * KW], ALU.add)\
                    .then_inc(sig["v2_biased"], 1)

            def mean_square(squares, ss, ve, name, n1):
                nc.vector.tensor_reduce(ss[:, :], squares, AX.X, ALU.add).then_inc(sig[name + "_sumsq"], 1)
                dve.wait_ge(sig[name + "_sumsq"], n1)
                nc.vector.tensor_scalar(ve[:, :], ss[:, :], 1.0 / HD, RMS_EPS, ALU.mult, ALU.add)\
                    .then_inc(sig[name + "_var"], 1)

            def key_square(t):
                dve.wait_ge(sig["k_squared"], t + 1)
                mean_square(k2s[:, :, :], k2_ss, k2_ve, "k", t + 1)

            def query_bias(t):
                for n in range(2):
                    dve.wait_ge(sig["q_projected"], 4 * t + 2 * n + 2)
                    nc.vector.tensor_tensor(q_work[:, n * 1024:(n + 1) * 1024], flat(banks[:, 2 * n:2 * n + 2, :]),
                                            bq_b[:, n * 1024:(n + 1) * 1024], ALU.add).then_inc(sig["q_biased"], 1)

            def query_norm(t):
                dve.wait_ge(sig["q_squared"], 2 * t + 2)
                mean_square(q2s[:, :, :], q2_ss, q2_ve, "q", t + 1)
                dve.wait_ge(sig["q_rstd"], t + 1)
                nc.vector.tensor_tensor(q2s[:, 0:half, :], q2[:, 0:half, :],
                                        q2_rs[:, 0:half].unsqueeze(2).to_broadcast([P, half, HD]), ALU.mult)\
                    .then_inc(sig["q_normed_a"], 1)

            def cross_softmax(t):
                rows = s2[:, :, :, :].rearrange("p a b c -> p (a b) c")
                for n in range(2):
                    dve.wait_ge(sig["scored"], 2 * t + n + 1)
                    nc.vector.tensor_tensor(s2[:, :, n, :], banks[:, n, :].rearrange("p (a e) -> p a e", e=S),
                                            mask_t[:, :].unsqueeze(1).to_broadcast([P, PAIRS, S]), ALU.add)\
                        .then_inc(sig["cross_masked"], 1)
                dve.wait_ge(sig["cross_masked"], 2 * t + 2)
                nc.vector.reduce_max(s2_max[:, :], rows, AX.X).then_inc(sig["cross_max"], 1)
                dve.wait_ge(sig["cross_max"], t + 1)
                nc.vector.tensor_tensor(rows, rows, s2_max[:, :].unsqueeze(2).to_broadcast([P, HEADS, S]),
                                        ALU.subtract).then_inc(sig["cross_shifted"], 1)
                dve.wait_ge(sig["cross_exp"], t + 1)
                nc.vector.tensor_reduce(s2_sum[:, :], rows, AX.X, ALU.add).then_inc(sig["cross_sum"], 1)
                dve.wait_ge(sig["cross_sum"], t + 1)
                nc.vector.reciprocal(s2_rec[:, :], s2_sum[:, :]).then_inc(sig["cross_recip"], 1)
                dve.wait_ge(sig["cross_recip"], t + 1)
                nc.vector.tensor_tensor(rows, rows, s2_rec[:, :].unsqueeze(2).to_broadcast([P, HEADS, S]),
                                        ALU.mult).then_inc(sig["cross_probs"], 1)

            def cross_out_low(t):
                for n in range(2):
                    low("ot_lo", o2t[LO][:, :, n * S:(n + 1) * S],
                        banks[:, 2 * n:2 * n + 2, :].rearrange("p a (h s) -> p (a h) s", s=S),
                        o2t[HI][:, :, n * S:(n + 1) * S], "ot_hi", 2 * t + n + 1)

            def x2_norm(t):
                dve.wait_ge(sig["cross_proj"], t + 1)
                dve.wait_ge(sig["x1_kept"], t + 1)
                nc.vector.tensor_tensor(h2[:, :], x1_keep[:, :], bank_c[:, 0:D], ALU.add).then_inc(sig["h2_done"], 1)
                dve.wait_ge(sig["h2_done"], t + 1)
                moments(h2, h2_stat, h2_mv, h2_ve, "h2", t + 1)
                normalise("x2_normed", x2, h2, h2_mv, h2_rs, "h2", t + 1)

            def route_choose(t):
                n1 = t + 1
                dve.wait_ge(sig["routed"], n1)
                nc.vector.tensor_copy(logits[:, :], bank_c[:, D:D + EXPERTS + 1]).then_inc(sig["logits_copied"], 1)
                wait_alone(dve, sig["logits_copied"], n1, sig["dve_held"])
                nc.vector.max(top[:, :], logits[:, 0:EXPERTS]).then_inc(sig["top8"], 1)
                dve.wait_ge(sig["top8"], n1)
                nc.vector.tensor_scalar_mul(top_neg[:, :], top[:, 0:1], -1.0).then_inc(sig["top_bias"], 1)
                nc.vector.match_replace(rest[:, :], top[:, :], logits[:, 0:EXPERTS], REMOVED)\
                    .then_inc(sig["top_removed"], 1)
                dve.wait_ge(sig["top_removed"], n1)
                nc.vector.tensor_tensor(chosen[:, :], rest[:, :], logits[:, 0:EXPERTS], ALU.not_equal)\
                    .then_inc(sig["top_mask"], 1)
                dve.wait_ge(sig["top_mask"], n1)
                dve.wait_ge(sig["route_exp"], n1)
                nc.vector.tensor_tensor(rkept[:, :], rexp[:, :], chosen[:, :], ALU.mult).then_inc(sig["route_kept"], 1)
                dve.wait_ge(sig["shared_exp"], n1)
                nc.vector.tensor_scalar_add(sh_p[:, :], sh_e[:, :], 1.0).then_inc(sig["shared_plus"], 1)
                dve.wait_ge(sig["route_kept"], n1)
                nc.vector.tensor_reduce(rsum[:, :], rkept[:, :], AX.X, ALU.add).then_inc(sig["route_sum"], 1)
                dve.wait_ge(sig["shared_plus"], n1)
                nc.vector.reciprocal(route[:, EXPERTS:EXPERTS + 1], sh_p[:, :]).then_inc(sig["shared_gate"], 1)
                dve.wait_ge(sig["route_sum"], n1)
                nc.vector.reciprocal(rrec[:, :], rsum[:, :]).then_inc(sig["route_recip"], 1)
                dve.wait_ge(sig["route_recip"], n1)
                nc.vector.tensor_scalar_mul(route[:, 0:EXPERTS], rkept[:, :], rrec[:, :]).then_inc(sig["route_w"], 1)
                dve.wait_ge(sig["split_hi"], n1)
                dve.wait_ge(sig["route_w"], n1)
                dve.wait_ge(sig["shared_gate"], n1)
                parts = split[:, :].bitcast(F32)
                nc.vector.tensor_tensor(split[:, EXPERTS:2 * EXPERTS], route[:, 0:EXPERTS], parts[:, 0:EXPERTS],
                                        ALU.subtract)
                nc.vector.tensor_tensor(split[:, 2 * EXPERTS + 1:2 * EXPERTS + 2], route[:, EXPERTS:EXPERTS + 1],
                                        parts[:, 2 * EXPERTS:2 * EXPERTS + 1], ALU.subtract)\
                    .then_inc(sig["split_lo"], 1)

            def step(t, u):
                if t is not None:
                    x_norm(t)
                    x_low(t)
                if u is not None:
                    ctx_low(u)
                    bias_keys(u)
                if t is not None:
                    copy_values(t)
                if u is not None:
                    key_square(u)
                    query_bias(u)
                    query_norm(u)
                if t is not None:
                    self_mask(t)
                    self_normalise(t)
                if u is not None:
                    cross_softmax(u)
                if t is not None:
                    x1_norm(t)
                if u is not None:
                    cross_out_low(u)
                if t is not None:
                    x1_low(t)
                if u is not None:
                    x2_norm(u)
                    route_choose(u)

            low("qkv_lo", flat(qkv_w[LO][:, :, :]), q_work[:, 0:C * 3 * D], flat(qkv_w[HI][:, :, :]), "qkv_hi", 1)
            low("wkv_lo", flat(wkv_w[LO][:, :, :]), stage_b[:, 0:C * 2 * KW], flat(wkv_w[HI][:, :, :]), "wkv_hi", 1)
            dve.wait_ge(sig["small_loaded"], 16 * 11)
            nc.vector.tensor_tensor(qn_c[:, :], qn_c[:, :], kn_c[:, :], ALU.mult).then_inc(sig["key_scale_a"], 1)
            dve.wait_ge(sig["key_scale_a"], 1)
            nc.vector.tensor_scalar_mul(key_scale[:, :], qn_c[:, :], float(HD) ** -0.5).then_inc(sig["key_scale"], 1)
            low("wq_lo", flat(wq_w[LO][:, :, :]), q_work[:, :], flat(wq_w[HI][:, :, :]), "wq_hi", 1)
            low("wo_lo", flat(wo_w[LO][:, :, :]), stage_b[:, :], flat(wo_w[HI][:, :, :]), "wo_hi", 1)
            dve.wait_ge(sig["causal_made"], 1)
            step(0, None)
            with dve.Fori(1, TILES) as t:
                step(t, t - 1)
            step(None, TILES - 1)


EXPERT_SIGNALS = """
dve_held2 pool_held2
weights_loaded weights_high weights_low selector_copied weights_free wt_loaded sh_loaded x_high x_low
selector_zeroed selector_half selector_made pair_ones identity_zeroed2 identity_made2 constants2
gated upped weight_spread silu_done gated_up weighted inter_hi inter_lo y_done y_added
y_final z_transposed z_copied z_stats z_moments z_var z_rstd z_normed out_stored
""".split()


def expert_phase(nc, sig, acc_loaded, gate_up, down, x2t_d, wt_d, sh_d, out):
    with ExitStack() as stack:
        def sb(name, shape, dt=F32):
            return stack.enter_context(nc.sbuf_tensor(name, shape, dt))

        acc = sb("acc", [P, BLOCKS, C, BLOCK])
        xt = [sb(f"xt{n}", [P, BLOCKS, C, BLOCK], F32R) for n in (HI, LO)]
        wt = sb("wt_all", [P, N], F32R)
        gu_raw = sb("gu_raw", [P, GROUP * 4 * P])
        dp_raw = sb("dp_raw", [P, GROUP * D])
        gu = [[sb(f"gu{u}{n}", [P, GROUP, 2, C, P], F32R) for n in (HI, LO)] for u in range(2)]
        dp = [[sb(f"dp{u}{n}", [P, GROUP, D], F32R) for n in (HI, LO)] for u in range(2)]
        selector = sb("selector", [P, EPAIRS, P], BF16)
        sel = [sb(f"sel{u}", [P, GROUP, P], F32R) for u in range(2)]
        ones2_f = sb("ones2_f", [2, P])
        ones2 = sb("ones2", [2, P], F32R)
        sh = sb("sh", [2, BLOCK], F32R)
        silu = sb("silu", [P, 2, BLOCK])
        gxu = sb("gxu", [P, 2, BLOCK])
        inter = sb("inter", [P, 2, BLOCK])
        int_p = [sb(f"int_p{n}", [P, 2, BLOCK], F32R) for n in (HI, LO)]
        y_sum = sb("y_sum", [P, C, BLOCK])
        identity = sb("identity2", [P, P])
        z = sb("z", [P, 4, D])
        z_stat = sb("z_stat", [P, 4, 6])
        z_mv = sb("z_mv", [P, 4, 2])
        z_ve = sb("z_ve", [P, 4])
        z_rs = sb("z_rs", [P, 4])
        minus_half = sb("minus_half2", [P, 4])

        def bank(name, n=1):
            return stack.enter_context(nc.psum_tensor(name, [P, n, 512], F32))

        bank_gate, bank_up = bank("bank_gate", 2), bank("bank_up", 2)
        bank_w, bank_y, bank_z = bank("bank_w"), bank("bank_y", 2), bank("bank_z")

        block = stack.enter_context(nc.Block())
        GU, DP = GROUP * 4 * P, GROUP * D
        STEP = ROUNDS * UNITS

        def groups(eng, run):
            with eng.Fori(0, (GROUPS - 1) // 2) as g2:
                for u in range(2):
                    run(2 * g2 + u, u, False)
            run(GROUPS - 1, 0, True)

        def rounds(eng, run):
            run(0)
            with eng.Fori(1, ROUNDS) as r:
                run(r)

        def columns(r, k):
            return bass.ds(r * (2 * BLOCK) + (k // GROUP) * BLOCK, BLOCK)

        @block.sync
        def _(sp):
            def load_weights(g):
                sp.wait_ge(sig["weights_low"], g)
                sp.dma_start(gu_raw[:, :], gate_up[g, :, :]).then_inc(sig["weights_loaded"], 16)
                sp.dma_start(dp_raw[:, :], down[g, :, :]).then_inc(sig["weights_loaded"], 16)

            load_weights(0)
            for b in range(BLOCKS):
                sp.dma_start(acc[:, b, :, :], x2t_d[:, :, b * BLOCK:(b + 1) * BLOCK]).then_inc(acc_loaded[b], 16)
            sp.dma_start(wt[:, :].bitcast(F32), wt_d).then_inc(sig["wt_loaded"], 16)
            with sp.Fori(1, GROUPS) as g:
                load_weights(g)

            def load_shared(b):
                sp.wait_ge(sig["y_added"], b + (GROUPS - 1) * BLOCKS)
                sp.dma_start(sh[:, :].bitcast(F32), sh_d[:, bass.ts(b, BLOCK)]).then_inc(sig["sh_loaded"], 16)

            def store(b):
                sp.wait_ge(sig["z_normed"], 4 * b + 4)
                sp.dma_start(out[bass.ts(b, BLOCK), :].rearrange("(j p) d -> p j d", p=P), z[:, :, :])\
                  .then_inc(sig["out_stored"], 16)

            load_shared(0)
            with sp.Fori(1, BLOCKS) as b:
                load_shared(b)
                store(b - 1)
            store(BLOCKS - 1)
            sp.wait_ge(sig["out_stored"], 16 * BLOCKS)

        @block.gpsimd
        def _(pool):
            nc.gpsimd.memset(minus_half[:, :], -0.5).then_inc(sig["constants2"], 1)
            nc.gpsimd.memset(ones2_f[:, :], 1.0).then_inc(sig["pair_ones"], 1)
            nc.gpsimd.memset(identity[:, :], 0.0).then_inc(sig["identity_zeroed2"], 1)
            nc.gpsimd.memset(selector[:, :, :], 0.0).then_inc(sig["selector_zeroed"], 1)
            pool.wait_ge(sig["identity_zeroed2"], 1)
            nc.gpsimd.affine_select(out=identity[:, :], in_=identity[:, :], compare_op=ALU.not_equal, fill=1.0,
                                    base=0, pattern=[[-1, P]], channel_multiplier=1).then_inc(sig["identity_made2"], 1)
            pool.wait_ge(sig["selector_zeroed"], 1)
            wide = selector[:, :, :].rearrange("k p (a i) -> k p a i", a=2)
            nc.gpsimd.affine_select(out=wide, in_=wide, compare_op=ALU.not_equal, fill=1.0, base=0,
                                    pattern=[[-2, EPAIRS], [-1, 2], [0, INNER]], channel_multiplier=1)\
                .then_inc(sig["selector_half"], 1)
            pool.wait_ge(sig["selector_half"], 1)
            nc.gpsimd.affine_select(out=wide, in_=wide, compare_op=ALU.not_equal, fill=1.0, base=-EXPERTS,
                                    pattern=[[-2, EPAIRS], [-1, 2], [0, INNER]], channel_multiplier=1)\
                .then_inc(sig["selector_made"], 1)
            pool.wait_ge(sig["selector_made"], 1)
            pool.wait_ge(sig["pair_ones"], 1)
            nc.gpsimd.tensor_copy(ones2[:, :], ones2_f[:, :])

            def split_weights(g, u, last):
                if not (isinstance(g, int) and g < 2):
                    pool.wait_ge(sig["weights_free"], g - 1)
                wait_alone(pool, sig["weights_loaded"], 32 * g + 32, sig["pool_held2"])
                flat = [w[:, :, :, :, :].rearrange("p a b c n -> p (a b c n)") for w in gu[u]]
                flat_d = [w[:, :, :].rearrange("p a n -> p (a n)") for w in dp[u]]
                nc.gpsimd.tensor_copy(flat[HI], gu_raw[:, :])
                nc.gpsimd.tensor_copy(flat_d[HI], dp_raw[:, :]).then_inc(sig["weights_high"], 1)
                nc.gpsimd.tensor_copy(sel[u][:, :, :], selector[:, bass.ds(g * GROUP, GROUP), :])\
                    .then_inc(sig["selector_copied"], 1)
                pool.wait_ge(sig["weights_high"], g + 1)
                nc.gpsimd.tensor_tensor(flat[LO], gu_raw[:, :], flat[HI].bitcast(F32), ALU.subtract)
                nc.gpsimd.tensor_tensor(flat_d[LO], dp_raw[:, :], flat_d[HI].bitcast(F32), ALU.subtract)\
                    .then_inc(sig["weights_low"], 1)

            split_weights(0, 0, False)
            split_weights(1, 1, False)
            with pool.Fori(1, (GROUPS - 1) // 2) as g2:
                for u in range(2):
                    split_weights(2 * g2 + u, u, False)
            split_weights(GROUPS - 1, 0, True)
            pool.wait_ge(sig["constants2"], 1)
            with pool.Fori(0, BLOCKS) as b:
                pool.wait_ge(sig["z_var"], b + 1)
                nc.gpsimd.tensor_tensor(z_rs[:, :], z_ve[:, :], minus_half[:, :], ALU.pow).then_inc(sig["z_rstd"], 1)

        @block.tensor
        def _(pe):
            def run_group(g, u, last):
                pe.wait_ge(sig["weights_low"], g + 1)
                pe.wait_ge(sig["selector_copied"], g + 1)

                def open_unit(r, k):
                    n = STEP * g + UNITS * r + k
                    p, par = k % GROUP, k % 2
                    cols = columns(r, k)
                    if first_group:
                        pe.wait_ge(sig["x_low"], 2 * r + k // GROUP + 1)
                    if not (isinstance(n, int) and n < 2):
                        pe.wait_ge(sig["gated_up"], n - 1)
                    for which, target, done in ((0, bank_gate, "gated"), (1, bank_up, "upped")):
                        for m, (a, b) in enumerate(PASSES):
                            for c in range(C):
                                mm = nc.tensor.matmul(target[:, par, :], gu[u][a][:, p, which, c, :], xt[b][:, 2 * r + k // GROUP, c, :],
                                                      start=(m == 0 and c == 0),
                                                      stop=(m == len(PASSES) - 1 and c == C - 1))
                        mm.then_inc(sig[done], 1)
                    if not (isinstance(n, int) and n < 1):
                        pe.wait_ge(sig["weighted"], n)
                    if last and p == GROUP - 1:
                        pe.wait_ge(sig["sh_loaded"], 32 * r + 16 * (k // GROUP) + 16)
                        mm = nc.tensor.matmul(bank_w[:, 0, :], ones2[:, :], sh[:, :], start=True, stop=True)
                    else:
                        mm = nc.tensor.matmul(bank_w[:, 0, :], sel[u][:, p, :], wt[:, cols], start=True, stop=True)
                    mm.then_inc(sig["weight_spread"], 1)

                def close_unit(r, k):
                    n = STEP * g + UNITS * r + k
                    p, par = k % GROUP, k % 2
                    done = BLOCKS * g + 2 * r + k // GROUP
                    pe.wait_ge(sig["inter_lo"], n + 1)
                    if p == 0:
                        pe.wait_ge(sig["y_added"], done)
                    for c in range(C):
                        for m, (a, b) in enumerate(PASSES):
                            mm = nc.tensor.matmul(bank_y[:, c, :], dp[u][a][:, p, c * P:(c + 1) * P],
                                                  int_p[b][:, par, :], start=(p == 0 and m == 0),
                                                  stop=(p == GROUP - 1 and m == len(PASSES) - 1))
                    if p == GROUP - 1:
                        mm.then_inc(sig["y_done"], 1)

                def transpose_out(r, k):
                    done = 2 * r + k // GROUP
                    pe.wait_ge(sig["y_added"], BLOCKS * g + done + 1)
                    for n in range(2):
                        pe.wait_ge(sig["z_copied"], 2 * done + n)
                        for j in range(2):
                            for c in range(C):
                                mm = nc.tensor.transpose(bank_z[:, 0, j * D + c * P:j * D + (c + 1) * P],
                                                         y_sum[:, c, (2 * n + j) * P:(2 * n + j + 1) * P],
                                                         identity[:, :])
                        mm.then_inc(sig["z_transposed"], 1)

                def run_round(r):
                    for k in range(UNITS):
                        open_unit(r, k)
                        if k:
                            close_unit(r, k - 1)
                        elif not isinstance(r, int):
                            close_unit(r - 1, UNITS - 1)
                        if last and k % GROUP == 1:
                            if k > GROUP:
                                transpose_out(r, 0)
                            elif not isinstance(r, int):
                                transpose_out(r - 1, GROUP)

                rounds(pe, run_round)
                close_unit(ROUNDS - 1, UNITS - 1)
                if last:
                    transpose_out(ROUNDS - 1, GROUP)

            pe.wait_ge(sig["identity_made2"], 1)
            pe.wait_ge(sig["wt_loaded"], 16)
            first_group = True

            def release(g, u, last):
                run_group(g, u, last)
                pe.drain().then_inc(sig["weights_free"], 1)

            release(0, 0, False)
            first_group = False
            release(1, 1, False)
            with pe.Fori(1, (GROUPS - 1) // 2) as g2:
                for u in range(2):
                    release(2 * g2 + u, u, False)
            release(GROUPS - 1, 0, True)

        @block.scalar
        def _(act):
            for b in range(BLOCKS):
                act.wait_ge(acc_loaded[b], 16)
                nc.scalar.activation(xt[HI][:, b, :, :], acc[:, b, :, :], ACT.Copy).then_inc(sig["x_high"], 1)

            def run_group(g, u, last):
                def run_round(r):
                    for k in range(UNITS):
                        n = STEP * g + UNITS * r + k
                        par = k % 2
                        act.wait_ge(sig["gated"], n + 1)
                        nc.scalar.activation(silu[:, par, :], bank_gate[:, par, :], ACT.Silu)\
                            .then_inc(sig["silu_done"], 1)
                        act.wait_ge(sig["weighted"], n + 1)
                        nc.scalar.activation(int_p[HI][:, par, :], inter[:, par, :], ACT.Copy)\
                            .then_inc(sig["inter_hi"], 1)
                        if last and k % GROUP == 1:
                            if k > GROUP:
                                copy_out(2 * r)
                            elif not isinstance(r, int):
                                copy_out(2 * r - 1)

                def copy_out(done):
                    for m in range(2):
                        act.wait_ge(sig["z_transposed"], 2 * done + m + 1)
                        act.wait_ge(sig["out_stored"], 16 * done)
                        nc.scalar.activation(z[:, 2 * m:2 * m + 2, :].rearrange("p a n -> p (a n)"), bank_z[:, 0, :],
                                             ACT.Copy).then_inc(sig["z_copied"], 1)

                rounds(act, run_round)
                if last:
                    copy_out(BLOCKS - 1)

            groups(act, run_group)

        @block.vector
        def _(dve):
            for b in range(BLOCKS):
                dve.wait_ge(sig["x_high"], b + 1)
                nc.vector.tensor_tensor(xt[LO][:, b, :, :], acc[:, b, :, :], xt[HI][:, b, :, :].bitcast(F32),
                                        ALU.subtract).then_inc(sig["x_low"], 1)

            def run_group(g, u, last):
                def work(r, k):
                    n = STEP * g + UNITS * r + k
                    par = k % 2
                    dve.wait_ge(sig["silu_done"], n + 1)
                    dve.wait_ge(sig["upped"], n + 1)
                    nc.vector.tensor_tensor(gxu[:, par, :], silu[:, par, :], bank_up[:, par, :], ALU.mult)\
                        .then_inc(sig["gated_up"], 1)
                    dve.wait_ge(sig["gated_up"], n + 1)
                    dve.wait_ge(sig["weight_spread"], n + 1)
                    nc.vector.tensor_tensor(inter[:, par, :], gxu[:, par, :], bank_w[:, 0, :], ALU.mult)\
                        .then_inc(sig["weighted"], 1)
                    dve.wait_ge(sig["inter_hi"], n + 1)
                    nc.vector.tensor_tensor(int_p[LO][:, par, :], inter[:, par, :], int_p[HI][:, par, :].bitcast(F32),
                                            ALU.subtract).then_inc(sig["inter_lo"], 1)

                def add(r, k):
                    done = BLOCKS * g + 2 * r + k // GROUP
                    dve.wait_ge(sig["y_done"], done + 1)
                    if last:
                        dve.wait_ge(sig["z_transposed"], 2 * (2 * r + k // GROUP))
                    total = acc[:, 2 * r + k // GROUP, :, :]
                    nc.vector.tensor_tensor(y_sum[:, :, :] if last else total, total, bank_y[:, :, :], ALU.add)\
                        .then_inc(sig["y_added"], 1)

                def finish(done):
                    dve.wait_ge(sig["z_copied"], 2 * done + 2)
                    for j in range(4):
                        st = nc.vector.bn_stats(z_stat[:, j, :], z[:, j, :])
                    st.then_inc(sig["z_stats"], 1)
                    wait_alone(dve, sig["z_stats"], done + 1, sig["dve_held2"])
                    for j in range(4):
                        st = nc.vector.bn_aggr(z_mv[:, j, :], z_stat[:, j, :])
                    st.then_inc(sig["z_moments"], 1)
                    dve.wait_ge(sig["z_moments"], done + 1)
                    nc.vector.tensor_scalar_add(z_ve[:, :], z_mv[:, :, 1], LN_EPS).then_inc(sig["z_var"], 1)
                    dve.wait_ge(sig["z_rstd"], done + 1)
                    for j in range(4):
                        nc.vector.tensor_scalar(z[:, j, :], z[:, j, :], z_mv[:, j, 0:1], z_rs[:, j:j + 1],
                                                ALU.subtract, ALU.mult).then_inc(sig["z_normed"], 1)

                def run_round(r):
                    for k in range(UNITS):
                        work(r, k)
                        if k % GROUP == 0:
                            if k:
                                add(r, k - 1)
                            elif not isinstance(r, int):
                                add(r - 1, UNITS - 1)
                        if last and k % GROUP == 2:
                            if k > GROUP:
                                finish(2 * r)
                            elif not isinstance(r, int):
                                finish(2 * r - 1)

                rounds(dve, run_round)
                add(ROUNDS - 1, UNITS - 1)
                if last:
                    finish(BLOCKS - 1)

            groups(dve, run_group)


def kernel(**inputs):
    import numpy as np
    import concourse.bacc as bacc
    from concourse.bass_utils import run_bass_kernel_spmd

    def of(name):
        return np.asarray(inputs[name])

    gu = np.zeros((2 * EPAIRS, 2, INNER, D), np.float32)
    gu[:EXPERTS] = of("L0_ffn_gu_w").reshape(EXPERTS, 2, INNER, D)
    gu[EXPERTS, 0] = of("L0_ffn_sh_gate_w")
    gu[EXPERTS, 1] = of("L0_ffn_sh_up_w")
    gu = gu.reshape(GROUPS, GROUP, 2, 2, INNER, C, P).transpose(0, 6, 1, 3, 5, 2, 4)
    dp = np.zeros((2 * EPAIRS, D, INNER), np.float32)
    dp[:EXPERTS] = of("L0_ffn_dp_w")
    dp[EXPERTS] = of("L0_ffn_sh_down_w")
    dp = dp.reshape(GROUPS, GROUP, 2, D, INNER).transpose(0, 2, 4, 1, 3)
    router = np.zeros((D, EXPERTS + 1), np.float32)
    router[:, :EXPERTS] = of("L0_ffn_gate_w").T
    router[:, EXPERTS] = of("L0_ffn_sh_gate1_w")[0]

    arrays = {
        "x": of("x").reshape(N, D), "ctx": of("ctx_2048").reshape(N, D), "mask": of("mask_1xSxS2_ff0").reshape(S, S),
        "qkv": of("L0_attn_qkv"), "o_proj": of("L0_attn_o_proj"), "gamma": of("L0_attn_gamma"),
        "beta": of("L0_attn_beta"), "wq": of("L0_xattn_Wq"), "bq": of("L0_xattn_bq"), "wk": of("L0_xattn_Wk"),
        "bk": of("L0_xattn_bk"), "wv": of("L0_xattn_Wv"), "bv": of("L0_xattn_bv"), "wo": of("L0_xattn_Wo"),
        "qn_w": of("L0_xattn_qn_w"), "kn_w": of("L0_xattn_kn_w"), "router": router,
        "gate_up": gu.reshape(GROUPS, P, GROUP * 4 * P), "down": dp.reshape(GROUPS, P, GROUP * D),
    }
    arrays = {f"in_{name}": np.ascontiguousarray(a) for name, a in arrays.items()}
    nc = bacc.Bacc("TRN2", target_bir_lowering=False, num_devices=1)
    args = [nc.dram_tensor(name, a.shape, mybir.dt.from_np(a.dtype), kind="ExternalInput").ap()
            for name, a in arrays.items()]
    out = nc.dram_tensor("out", [N, D], F32, kind="ExternalOutput").ap()
    decoder(nc, *args, out)
    result = run_bass_kernel_spmd(nc, [arrays], core_ids=[0])
    return result.results[0]["out"].reshape(B, S, D)
```

```python
from contextlib import ExitStack

import concourse.bass as bass
from concourse import mybir

F32 = mybir.dt.float32
F32R = mybir.dt.float32r
BF16 = mybir.dt.bfloat16
ALU = mybir.AluOpType
ACT = mybir.ActivationFunctionType
AX = mybir.AxisListType

P = 128
B, S, D = 64, 64, 256
C = D // P
N = B * S
TILES = N // P
HEADS, KV, HD = 16, 4, 128
PAIRS = HEADS // 2
QW, KW = HEADS * HD, KV * HD
EXPERTS, INNER, TOP_K = 64, 64, 8
EPAIRS = EXPERTS // 2 + 1
GROUP = 3
GROUPS = EPAIRS // GROUP
BLOCK = 512
BLOCKS = N // BLOCK
ROUNDS = BLOCKS // 2
UNITS = 2 * GROUP
LN_EPS, RMS_EPS = 1e-5, 1e-6
SELF_SCALE = float(D) ** -0.5
MASKED = -1e30
REMOVED = -3e38
HI, LO = 0, 1
PASSES = ((HI, HI), (LO, HI), (HI, LO))


def decoder(nc, x, ctx, mask, qkv, o_proj, gamma, beta, wq, bq, wk, bk, wv, bv, wo, qn_w, kn_w, router, gate_up,
            down, out):
    x1_d = nc.dram_tensor("x1_scratch", [N, D], F32).ap()
    x2t_d = nc.dram_tensor("x2t_scratch", [P, C, N], F32).ap()
    wt_d = nc.dram_tensor("route_weight_scratch", [P, N], F32).ap()
    sh_d = nc.dram_tensor("shared_gate_scratch", [2, N], F32).ap()
    attention = {name: nc.alloc_semaphore(name) for name in ATTENTION_SIGNALS}
    attention_phase(nc, attention, x, ctx, mask, qkv, o_proj, gamma, beta, wq, bq, wk, bk, wv, bv, wo, qn_w, kn_w,
                    router, x1_d, x2t_d, wt_d, sh_d)
    nc.clear_and_free_semaphores(list(attention.values()))
    nc.all_engine_barrier()
    expert = {name: nc.alloc_semaphore(name) for name in EXPERT_SIGNALS}
    acc_loaded = [nc.alloc_semaphore(f"acc_loaded{b}") for b in range(BLOCKS)]
    expert_phase(nc, expert, acc_loaded, gate_up, down, x2t_d, wt_d, sh_d, out)


def wait_alone(eng, signal, count, held):
    eng.wait_ge(signal, count)
    eng.sem_inc(held)


ATTENTION_SIGNALS = """
dve_held sp_held
qkv_loaded wkv_loaded wq_loaded wo_loaded small_loaded qkv_hi qkv_lo wkv_hi wkv_lo wq_hi wq_lo wo_hi wo_lo
key_scale_a key_scale constants identity_zeroed identity_made causal_zeroed causal_half causal_made
x_loaded x_res_loaded x1_res_loaded x1_stored x_stats x_moments x_var x_rstd x_hat x_scaled x_normed xn_transposed xn_hi xn_lo
qk_projected v_projected qk_copied v_copied qk_transposed qkt_copied self_scored self_masked self_max self_bias
self_exp self_recip self_probs self_pt self_pt_copied self_out self_ot self_proj h1_done h1_stats h1_moments h1_var
h1_rstd x1_normed x1_transposed x1_hi x1_lo
ctx_loaded ctx_transposed ctx_hi ctx_lo k_projected v2_projected k_biased v2_copied v2_biased k_squared k_sumsq k_var k_rstd
k_normed k_transposed kt_copied q_projected q_biased q_squared q_sumsq q_var q_rstd q_normed_a q_normed_b q_transposed
qt_copied scored cross_masked cross_max cross_shifted cross_exp cross_sum cross_recip cross_probs cross_pt
cross_pt_copied cross_out ot_hi ot_lo cross_proj h2_done h2_stats h2_moments h2_var h2_rstd x2_normed x2_transposed
x2t_copied x2_stored routed logits_copied top8 top_removed top_mask top_bias route_exp shared_exp route_kept route_sum
shared_plus route_recip shared_gate route_w split_hi split_lo w_transposed wt_copied wt_stored sh_stored
""".split()


def attention_phase(nc, sig, x, ctx, mask, qkv, o_proj, gamma, beta, wq, bq, wk, bk, wv, bv, wo, qn_w, kn_w, router,
                    x1_d, x2t_d, wt_d, sh_d):
    with ExitStack() as stack:
        def sb(name, shape, dt=F32):
            return stack.enter_context(nc.sbuf_tensor(name, shape, dt))

        qkv_w = [sb(f"qkv_w{n}", [P, C, 3 * D], F32R) for n in (HI, LO)]
        wq_w = [sb(f"wq_w{n}", [P, C, QW], F32R) for n in (HI, LO)]
        wkv_w = [sb(f"wkv_w{n}", [P, C, 2 * KW], F32R) for n in (HI, LO)]
        wo_w = [sb(f"wo_w{n}", [P, HEADS, D], F32R) for n in (HI, LO)]
        o_w = sb("o_w", [P, C, D])
        router_w = sb("router_w", [P, C, EXPERTS + 1])
        stage_b = sb("stage_b", [P, HEADS * D])
        bq_b = sb("bq_b", [P, QW])
        bkv_b = sb("bkv_b", [P, 2 * KW])
        gamma_b = sb("gamma_b", [P, D])
        beta_b = sb("beta_b", [P, D])
        mask_t = sb("mask_t", [P, S])
        causal = sb("causal", [P, P])
        identity = sb("identity", [P, P])
        minus_half = sb("minus_half", [P, HEADS])
        qn_c = sb("qn_c", [P, 1])
        kn_c = sb("kn_c", [P, 1])
        key_scale = sb("key_scale", [P, 1])

        x_in = sb("x_in", [P, D])
        x_res = sb("x_res", [P, D])
        x_stat = sb("x_stat", [P, 6])
        x_mv = sb("x_mv", [P, 2])
        x_ve = sb("x_ve", [P, 1])
        x_rs = sb("x_rs", [P, 1])
        x_hat = sb("x_hat", [P, D])
        x_g = sb("x_g", [P, D])
        x_n = sb("x_n", [P, D])
        xnt = [sb(f"xnt{n}", [P, C, P], F32R) for n in (HI, LO)]
        qk = sb("qk", [P, 2 * D])
        v = sb("v", [P, D])
        qkt = sb("qkt", [P, 2 * C, P])
        s1 = sb("s1", [P, P])
        s1_max = sb("s1_max", [P, 1])
        s1_bias = sb("s1_bias", [P, 1])
        p1 = sb("p1", [P, P])
        p1_sum = sb("p1_sum", [P, 1])
        p1_rec = sb("p1_rec", [P, 1])
        p1n = sb("p1n", [P, P])
        p1t = sb("p1t", [P, P])
        o1t = sb("o1t", [P, C, P])
        h1 = sb("h1", [P, D])
        h1_stat = sb("h1_stat", [P, 6])
        h1_mv = sb("h1_mv", [P, 2])
        h1_ve = sb("h1_ve", [P, 1])
        h1_rs = sb("h1_rs", [P, 1])
        x1 = sb("x1", [P, D])
        x1t = [sb(f"x1t{n}", [P, C, P], F32R) for n in (HI, LO)]

        ctx_in = sb("ctx_in", [P, D])
        x1_res = sb("x1_res", [P, D])
        ctxt = [sb(f"ctxt{n}", [P, C, P], F32R) for n in (HI, LO)]
        k2 = sb("k2", [P, KV, HD])
        v2_new = sb("v2_new", [P, KW])
        v2 = sb("v2", [P, KV, HD])
        k2s = sb("k2s", [P, KV, HD])
        k2_ss = sb("k2_ss", [P, KV])
        k2_ve = sb("k2_ve", [P, KV])
        k2_rs = sb("k2_rs", [P, KV])
        k2t = sb("k2t", [P, KV, P])
        q_work = sb("q_work", [P, 2 * QW])
        q2 = q_work[:, 0:QW].rearrange("p (h d) -> p h d", d=HD)
        q2s = q_work[:, QW:2 * QW].rearrange("p (h d) -> p h d", d=HD)
        q2_ss = sb("q2_ss", [P, HEADS])
        q2_ve = sb("q2_ve", [P, HEADS])
        q2_rs = sb("q2_rs", [P, HEADS])
        q2t = stage_b[:, 0:QW].rearrange("p (b h s) -> p b h s", b=2, s=S)
        s2 = stage_b[:, QW:QW + PAIRS * P].rearrange("p (a b e) -> p a b e", b=2, e=S)
        p2t = stage_b[:, QW + PAIRS * P:QW + 2 * PAIRS * P].rearrange("p (a n) -> p a n", n=P)
        s2_max = sb("s2_max", [P, HEADS])
        s2_sum = sb("s2_sum", [P, HEADS])
        s2_rec = sb("s2_rec", [P, HEADS])
        o2t = [sb(f"o2t{n}", [P, HEADS, P], F32R) for n in (HI, LO)]
        h2 = sb("h2", [P, D])
        h2_stat = sb("h2_stat", [P, 6])
        h2_mv = sb("h2_mv", [P, 2])
        h2_ve = sb("h2_ve", [P, 1])
        h2_rs = sb("h2_rs", [P, 1])
        x2 = sb("x2", [P, D])
        x2t = sb("x2t", [P, C, P])
        logits = sb("logits", [P, EXPERTS + 1])
        top = sb("top", [P, TOP_K])
        rest = sb("rest", [P, EXPERTS])
        chosen = sb("chosen", [P, EXPERTS])
        top_neg = sb("top_neg", [P, 1])
        rexp = sb("rexp", [P, EXPERTS])
        rkept = sb("rkept", [P, EXPERTS])
        rsum = sb("rsum", [P, 1])
        rrec = sb("rrec", [P, 1])
        route = sb("route", [P, EXPERTS + 1])
        sh_e = sb("sh_e", [P, 1])
        sh_p = sb("sh_p", [P, 1])
        split = sb("split", [P, 2 * EXPERTS + 2], F32R)
        wt = sb("wt", [P, P])
        sht = sb("sht", [2, P])

        def bank(name, n):
            return stack.enter_context(nc.psum_tensor(name, [P, n, 512], F32))

        bank_a, bank_b, bank_c, bank_d, bank_e = bank("bank_a", 2), bank("bank_b", 1), bank("bank_c", 2), \
            bank("bank_d", 2), bank("bank_e", 1)

        def split3(w):
            return w.rearrange("(c p) n -> p c n", p=P)

        def flat(a):
            return a.rearrange("p a b -> p (a b)")

        half = HEADS // 2
        LAG = 4

        def pipeline(eng, step, until=TILES):
            def peeled(i):
                step(*(i - k if 0 <= i - k < TILES else None for k in range(LAG + 1)))

            for i in range(LAG + 1):
                peeled(i)
            with eng.Fori(LAG + 1, until) as i:
                step(i, i - 1, i - 2, i - 3, i - 4)
            for i in range(until, TILES + LAG):
                peeled(i)

        block = stack.enter_context(nc.Block())

        @block.sync
        def _(sp):
            def load_x(t):
                sp.wait_ge(sig["x_hat"], t)
                sp.dma_start(x_in[:, :], x[bass.ts(t, P), :]).then_inc(sig["x_loaded"], 16)

            def load_ctx(t):
                sp.wait_ge(sig["ctx_transposed"], t)
                sp.dma_start(ctx_in[:, :], ctx[bass.ts(t, P), :]).then_inc(sig["ctx_loaded"], 16)

            def load_x_residual(t):
                sp.wait_ge(sig["h1_done"], t)
                sp.dma_start(x_res[:, :], x[bass.ts(t, P), :]).then_inc(sig["x_res_loaded"], 16)

            def load_x1_residual(t):
                wait_alone(sp, sig["x1_stored"], 16 * t + 16, sig["sp_held"])
                sp.wait_ge(sig["h2_done"], t)
                sp.dma_start(x1_res[:, :], x1_d[bass.ts(t, P), :]).then_inc(sig["x1_res_loaded"], 16)

            def store_x1(t):
                sp.wait_ge(sig["x1_normed"], t + 1)
                sp.dma_start(x1_d[bass.ts(t, P), :], x1[:, :]).then_inc(sig["x1_stored"], 16)

            def store_x2(t):
                wait_alone(sp, sig["x2t_copied"], t + 1, sig["sp_held"])
                sp.dma_start(x2t_d[:, :, bass.ts(t, P)], x2t[:, :, :]).then_inc(sig["x2_stored"], 16)

            def store_routes(t):
                sp.wait_ge(sig["wt_copied"], t + 1)
                sp.dma_start(wt_d[:, bass.ts(t, P)], wt[:, :]).then_inc(sig["wt_stored"], 16)
                sp.dma_start(sh_d[:, bass.ts(t, P)], sht[:, :]).then_inc(sig["sh_stored"], 16)

            def more(t):
                return t is not None and not (isinstance(t, int) and t + 1 >= TILES)

            def step(a, b, c, d, e):
                if e is not None:
                    load_x1_residual(e)
                if b is not None:
                    load_x_residual(b)
                if more(a):
                    load_x(a + 1)
                if more(c):
                    load_ctx(c + 1)
                if e is not None:
                    store_x2(e)
                if b is not None:
                    store_x1(b)
                if e is not None:
                    store_routes(e)

            sp.dma_start(q_work[:, 0:C * 3 * D].rearrange("p (c n) -> p c n", c=C), split3(qkv))\
              .then_inc(sig["qkv_loaded"], 16)
            sp.dma_start(x_in[:, :], x[0:P, :]).then_inc(sig["x_loaded"], 16)
            kv_stage = stage_b[:, 0:C * 2 * KW].rearrange("p (c n) -> p c n", c=C)
            sp.dma_start(kv_stage[:, :, 0:KW], split3(wk)).then_inc(sig["wkv_loaded"], 16)
            sp.dma_start(kv_stage[:, :, KW:2 * KW], split3(wv)).then_inc(sig["wkv_loaded"], 16)
            sp.dma_start(ctx_in[:, :], ctx[0:P, :]).then_inc(sig["ctx_loaded"], 16)
            sp.wait_ge(sig["qkv_lo"], 1)
            sp.dma_start(q_work[:, :].rearrange("p (c n) -> p c n", c=C), split3(wq)).then_inc(sig["wq_loaded"], 16)
            sp.wait_ge(sig["wkv_lo"], 1)
            sp.dma_start(stage_b[:, :].rearrange("p (h n) -> p h n", h=HEADS),
                         wo.rearrange("(h p) n -> p h n", p=P)).then_inc(sig["wo_loaded"], 16)
            pipeline(sp, step, TILES - 1)
            for name in ("x2_stored", "wt_stored", "sh_stored"):
                sp.wait_ge(sig[name], 16 * TILES)

        @block.gpsimd
        def _(pool):
            for part, source in ((gamma_b, gamma), (beta_b, beta), (bq_b, bq), (bkv_b[:, 0:KW], bk),
                                 (bkv_b[:, KW:2 * KW], bv)):
                pool.dma_start(part if isinstance(part, bass.AP) else part[:, :], source.partition_broadcast(P))\
                    .then_inc(sig["small_loaded"], 16)
            for n in range(2):
                pool.dma_start(mask_t[n * S:(n + 1) * S, :], mask).then_inc(sig["small_loaded"], 16)
            pool.dma_start(qn_c[:, :], qn_w.rearrange("(p a) -> p a", a=1)).then_inc(sig["small_loaded"], 16)
            pool.dma_start(kn_c[:, :], kn_w.rearrange("(p a) -> p a", a=1)).then_inc(sig["small_loaded"], 16)
            pool.dma_start(o_w[:, :, :], split3(o_proj)).then_inc(sig["small_loaded"], 16)
            pool.dma_start(router_w[:, :, :], split3(router)).then_inc(sig["small_loaded"], 16)
            nc.gpsimd.memset(minus_half[:, :], -0.5).then_inc(sig["constants"], 1)
            nc.gpsimd.memset(identity[:, :], 0.0).then_inc(sig["identity_zeroed"], 1)
            nc.gpsimd.memset(causal[:, :], 0.0).then_inc(sig["causal_zeroed"], 1)
            pool.wait_ge(sig["identity_zeroed"], 1)
            nc.gpsimd.affine_select(out=identity[:, :], in_=identity[:, :], compare_op=ALU.not_equal, fill=1.0,
                                    base=0, pattern=[[-1, P]], channel_multiplier=1).then_inc(sig["identity_made"], 1)
            pool.wait_ge(sig["causal_zeroed"], 1)
            nc.gpsimd.affine_select(out=causal[:, :], in_=causal[:, :], compare_op=ALU.is_ge, fill=MASKED,
                                    base=0, pattern=[[-1, P]], channel_multiplier=1).then_inc(sig["causal_half"], 1)
            pool.wait_ge(sig["causal_half"], 1)
            nc.gpsimd.affine_select(out=causal[:, 0:S], in_=causal[:, 0:S], compare_op=ALU.is_ge, fill=MASKED,
                                    base=S - 1, pattern=[[0, S]], channel_multiplier=-1)\
                .then_inc(sig["causal_made"], 1)
            pool.wait_ge(sig["constants"], 1)
            pool.wait_ge(sig["small_loaded"], 16 * 11)

            def power(done, out_, base, width, start, n1):
                pool.wait_ge(sig[start], n1)
                nc.gpsimd.tensor_tensor(out_, base, minus_half[:, 0:width], ALU.pow).then_inc(sig[done], 1)

            def norm_x(t):
                power("x_rstd", x_rs[:, :], x_ve[:, :], 1, "x_var", t + 1)
                pool.wait_ge(sig["x_hat"], t + 1)
                nc.gpsimd.tensor_tensor(x_g[:, :], x_hat[:, :], gamma_b[:, :], ALU.mult).then_inc(sig["x_scaled"], 1)
                pool.wait_ge(sig["x_scaled"], t + 1)
                nc.gpsimd.tensor_tensor(x_n[:, :], x_g[:, :], beta_b[:, :], ALU.add).then_inc(sig["x_normed"], 1)

            def norm_queries(t):
                power("q_rstd", q2_rs[:, :], q2_ve[:, :], HEADS, "q_var", t + 1)

            def square_keys(t):
                pool.wait_ge(sig["k_biased"], t + 1)
                nc.gpsimd.tensor_tensor(k2s[:, :, :], k2[:, :, :], k2[:, :, :], ALU.mult).then_inc(sig["k_squared"], 1)

            def scale_queries(t):
                pool.wait_ge(sig["q_rstd"], t + 1)
                nc.gpsimd.tensor_tensor(q2s[:, half:, :], q2[:, half:, :],
                                        q2_rs[:, half:].unsqueeze(2).to_broadcast([P, half, HD]),
                                        ALU.mult).then_inc(sig["q_normed_b"], 1)

            def norm_keys(t):
                power("k_rstd", k2_rs[:, :], k2_ve[:, :], KV, "k_var", t + 1)
                pool.wait_ge(sig["k_rstd"], t + 1)
                nc.gpsimd.tensor_tensor(k2s[:, :, :], k2[:, :, :], k2_rs[:, :].unsqueeze(2).to_broadcast([P, KV, HD]),
                                        ALU.mult).then_inc(sig["k_normed"], 1)

            def bias_values(t):
                pool.wait_ge(sig["v2_copied"], t + 1)
                pool.wait_ge(sig["cross_out"], 2 * t)
                nc.gpsimd.tensor_tensor(flat(v2[:, :, :]), v2_new[:, :], bkv_b[:, KW:2 * KW], ALU.add)\
                    .then_inc(sig["v2_biased"], 1)

            def step(a, b, c, d, e):
                if d is not None:
                    bias_values(d)
                if a is not None:
                    norm_x(a)
                if e is not None:
                    power("h2_rstd", h2_rs[:, :], h2_ve[:, :], 1, "h2_var", e + 1)
                if c is not None:
                    norm_queries(c)
                    square_keys(c)
                    scale_queries(c)
                    norm_keys(c)
                if b is not None:
                    power("h1_rstd", h1_rs[:, :], h1_ve[:, :], 1, "h1_var", b + 1)

            pipeline(pool, step)

        @block.tensor
        def _(pe):
            def transpose_in(target, source):
                for c in range(C):
                    last = nc.tensor.transpose(target[:, c * P:(c + 1) * P], source[:, c * P:(c + 1) * P],
                                               identity[:, :])
                return last

            def product(target, left, right):
                for n, (a, b) in enumerate(PASSES):
                    for c in range(C):
                        last = nc.tensor.matmul(target, left[a][:, c, :], right(b, c), start=(n == 0 and c == 0),
                                                stop=(n == len(PASSES) - 1 and c == C - 1))
                return last

            def x_transpose(t):
                pe.wait_ge(sig["x_normed"], t + 1)
                pe.wait_ge(sig["qkt_copied"], t)
                transpose_in(bank_a[:, 0, :], x_n).then_inc(sig["xn_transposed"], 1)

            def self_project(t):
                pe.wait_ge(sig["xn_lo"], t + 1)
                product(bank_a[:, 1, :], xnt, lambda b, c: qkv_w[b][:, c, 0:2 * D]).then_inc(sig["qk_projected"], 1)
                product(bank_a[:, 0, 0:D], xnt, lambda b, c: qkv_w[b][:, c, 2 * D:3 * D])\
                    .then_inc(sig["v_projected"], 1)

            def self_transpose(t):
                pe.wait_ge(sig["qk_copied"], t + 1)
                pe.wait_ge(sig["v_copied"], t + 1)
                for c in range(2 * C):
                    last = nc.tensor.transpose(bank_a[:, 0, c * P:(c + 1) * P], qk[:, c * P:(c + 1) * P],
                                               identity[:, :])
                last.then_inc(sig["qk_transposed"], 1)

            def self_score(t):
                pe.wait_ge(sig["qkt_copied"], t + 1)
                for c in range(C):
                    last = nc.tensor.matmul(bank_a[:, 1, 0:P], qkt[:, c, :], qkt[:, C + c, :], start=(c == 0),
                                            stop=(c == C - 1))
                last.then_inc(sig["self_scored"], 1)

            def self_probs_transpose(t):
                pe.wait_ge(sig["self_probs"], t + 1)
                pe.wait_ge(sig["x1_lo"], t)
                nc.tensor.transpose(bank_b[:, 0, 0:P], p1n[:, :], identity[:, :]).then_inc(sig["self_pt"], 1)

            def self_attend(t):
                pe.wait_ge(sig["self_pt_copied"], t + 1)
                for c in range(C):
                    last = nc.tensor.matmul(bank_b[:, 0, c * P:(c + 1) * P], v[:, c * P:(c + 1) * P], p1t[:, :],
                                            start=True, stop=True)
                last.then_inc(sig["self_out"], 1)

            def self_output(t):
                pe.wait_ge(sig["self_ot"], t + 1)
                for c in range(C):
                    last = nc.tensor.matmul(bank_b[:, 0, 0:D], o1t[:, c, :], o_w[:, c, :], start=(c == 0),
                                            stop=(c == C - 1))
                last.then_inc(sig["self_proj"], 1)

            def x1_transpose(t):
                pe.wait_ge(sig["x1_normed"], t + 1)
                transpose_in(bank_b[:, 0, :], x1).then_inc(sig["x1_transposed"], 1)

            def query_project(t):
                pe.wait_ge(sig["x1_lo"], t + 1)
                for g in range(KV):
                    if g < 2:
                        pe.wait_ge(sig["cross_masked"], 2 * t)
                    else:
                        pe.wait_ge(sig["q_biased"], 4 * t + g - 1)
                    product(bank_c[:, g % 2, :], x1t, lambda b, c: wq_w[b][:, c, g * 512:(g + 1) * 512])\
                        .then_inc(sig["q_projected"], 1)

            def ctx_transpose(t):
                pe.wait_ge(sig["ctx_loaded"], 16 * t + 16)
                pe.wait_ge(sig["self_masked"], self_masked_before(t))
                transpose_in(bank_a[:, 1, :], ctx_in).then_inc(sig["ctx_transposed"], 1)

            def self_masked_before(t):
                return min(t + 2, TILES) if isinstance(t, int) else t + 2

            def key_project(t):
                pe.wait_ge(sig["ctx_lo"], t + 1)
                pe.wait_ge(sig["q_biased"], 4 * t + 4)
                product(bank_c[:, 0, :], ctxt, lambda b, c: wkv_w[b][:, c, 0:KW]).then_inc(sig["k_projected"], 1)
                product(bank_c[:, 1, :], ctxt, lambda b, c: wkv_w[b][:, c, KW:2 * KW]).then_inc(sig["v2_projected"], 1)

            def query_transpose(t, n):
                pe.wait_ge(sig["q_normed_b" if n else "q_normed_a"], t + 1)
                if n:
                    pe.wait_ge(sig["qt_copied"], 2 * t + 1)
                else:
                    pe.wait_ge(sig["k_biased"], t + 1)
                    pe.wait_ge(sig["v2_copied"], t + 1)
                for h in range(half):
                    last = nc.tensor.transpose(bank_c[:, h // 4, (h % 4) * P:(h % 4 + 1) * P], q2s[:, n * half + h, :],
                                               identity[:, :])
                last.then_inc(sig["q_transposed"], 1)

            def key_transpose(t, e):
                pe.wait_ge(sig["k_normed"], t + 1)
                if e is not None:
                    pe.wait_ge(sig["logits_copied"], e + 1)
                for g in range(KV):
                    last = nc.tensor.transpose(bank_e[:, 0, g * P:(g + 1) * P], k2s[:, g, :], identity[:, :])
                last.then_inc(sig["k_transposed"], 1)

            def cross_score(t):
                pe.wait_ge(sig["kt_copied"], t + 1)
                pe.wait_ge(sig["qt_copied"], 2 * t + 2)
                for n in range(2):
                    for p in range(PAIRS):
                        last = nc.tensor.matmul(bank_c[:, n, p * S:(p + 1) * S],
                                                q2t[:, n, 2 * p:2 * p + 2, :].rearrange("p h s -> p (h s)"),
                                                k2t[:, p // 2, n * S:(n + 1) * S], start=True, stop=True)
                    last.then_inc(sig["scored"], 1)

            def cross_probs_transpose(t):
                pe.wait_ge(sig["cross_probs"], t + 1)
                pe.wait_ge(sig["h2_done"], t)
                for p in range(PAIRS):
                    last = nc.tensor.transpose(bank_d[:, p // 4, (p % 4) * P:(p % 4 + 1) * P],
                                               s2[:, p, :, :].rearrange("p a b -> p (a b)"), identity[:, :])
                last.then_inc(sig["cross_pt"], 1)

            def cross_attend(t, m):
                if m:
                    pe.wait_ge(sig["ot_lo"], 4 * t + 2)
                else:
                    pe.wait_ge(sig["cross_pt_copied"], t + 1)
                    pe.wait_ge(sig["v2_biased"], t + 1)
                for g in range(2 * m, 2 * m + 2):
                    for n in range(2):
                        last = nc.tensor.matmul(bank_d[:, n, (g % 2) * 256:(g % 2 + 1) * 256],
                                                v2[n * S:(n + 1) * S, g, :], p2t[n * S:(n + 1) * S, 2 * g:2 * g + 2, :],
                                                start=True, stop=True)
                last.then_inc(sig["cross_out"], 1)

            def cross_output(t):
                pe.wait_ge(sig["ot_lo"], 4 * t + 4)
                for n, (a, b) in enumerate(PASSES):
                    for h in range(HEADS):
                        last = nc.tensor.matmul(bank_d[:, 0, 0:D], o2t[a][:, h, :], wo_w[b][:, h, :],
                                                start=(n == 0 and h == 0),
                                                stop=(n == len(PASSES) - 1 and h == HEADS - 1))
                last.then_inc(sig["cross_proj"], 1)

            def x2_transpose(t):
                pe.wait_ge(sig["x2_normed"], t + 1)
                pe.wait_ge(sig["wt_copied"], t)
                transpose_in(bank_e[:, 0, :], x2).then_inc(sig["x2_transposed"], 1)

            def route_score(t):
                pe.wait_ge(sig["x2t_copied"], t + 1)
                for c in range(C):
                    last = nc.tensor.matmul(bank_e[:, 0, 0:EXPERTS + 1], x2t[:, c, :], router_w[:, c, :],
                                            start=(c == 0), stop=(c == C - 1))
                last.then_inc(sig["routed"], 1)

            def route_transpose(t, c):
                pe.wait_ge(sig["split_lo"], t + 1)
                if c is not None:
                    pe.wait_ge(sig["kt_copied"], c + 1)
                parts = split[:, :].bitcast(F32)
                nc.tensor.transpose(bank_e[:, 0, 0:P], parts[:, 0:P], identity[:, :])
                nc.tensor.transpose(bank_e[0:2, 0, P:2 * P], parts[:, P:P + 2], identity[:, :])\
                    .then_inc(sig["w_transposed"], 1)

            def step(a, b, c, d, e):
                if c is not None:
                    query_project(c)
                if a is not None:
                    x_transpose(a)
                if c is not None:
                    ctx_transpose(c)
                if b is not None:
                    self_probs_transpose(b)
                    self_attend(b)
                if c is not None:
                    key_project(c)
                if d is not None:
                    cross_probs_transpose(d)
                if e is not None:
                    x2_transpose(e)
                if a is not None:
                    self_project(a)
                if b is not None:
                    self_output(b)
                if d is not None:
                    cross_attend(d, 0)
                if e is not None:
                    route_score(e)
                if c is not None:
                    query_transpose(c, 0)
                if a is not None:
                    self_transpose(a)
                if d is not None:
                    cross_attend(d, 1)
                if c is not None:
                    key_transpose(c, e)
                    query_transpose(c, 1)
                if b is not None:
                    x1_transpose(b)
                if a is not None:
                    self_score(a)
                if c is not None:
                    cross_score(c)
                if e is not None:
                    route_transpose(e, c)
                if d is not None:
                    cross_output(d)

            pe.wait_ge(sig["identity_made"], 1)
            pe.wait_ge(sig["small_loaded"], 16 * 11)
            pe.wait_ge(sig["qkv_lo"], 1)
            for name in ("wkv_lo", "wq_lo", "wo_lo"):
                pe.wait_ge(sig[name], 1)
            pipeline(pe, step)

        @block.scalar
        def _(act):
            def copy(done, target, source, start, count):
                act.wait_ge(sig[start], count)
                nc.scalar.activation(target, source, ACT.Copy).then_inc(sig[done], 1)

            def self_exp(t):
                act.wait_ge(sig["self_bias"], t + 1)
                nc.scalar.activation(p1[:, :], s1[:, :], ACT.Exp, bias=s1_bias[:, :], scale=SELF_SCALE,
                                     accum_out=p1_sum[:, :]).then_inc(sig["self_exp"], 1)

            def square_queries(t, g):
                act.wait_ge(sig["q_biased"], 4 * t + g + 1)
                nc.scalar.activation(q2s[:, 4 * g:4 * g + 4, :], q2[:, 4 * g:4 * g + 4, :], ACT.Square)\
                    .then_inc(sig["q_squared"], 1)

            def copy_keys(t):
                act.wait_ge(sig["k_transposed"], t + 1)
                nc.scalar.activation(flat(k2t[:, :, :]), bank_e[:, 0, :], ACT.Copy, scale=key_scale[:, :])\
                    .then_inc(sig["kt_copied"], 1)

            def copy_queries(t, n):
                copy("qt_copied", q2t[:, :, n * half:(n + 1) * half, :].rearrange("p b h s -> p h b s"),
                     flat(bank_c[:, :, :]).rearrange("p (h b s) -> p h b s", b=2, s=S), "q_transposed", 2 * t + n + 1)

            def cross_exp(t):
                act.wait_ge(sig["cross_shifted"], t + 1)
                rows = s2[:, :, :, :].rearrange("p a b c -> p (a b c)")
                nc.scalar.activation(rows, rows, ACT.Exp).then_inc(sig["cross_exp"], 1)

            def cross_out_high(t, m):
                for n in range(2):
                    copy("ot_hi", o2t[HI][:, m * half:(m + 1) * half, n * S:(n + 1) * S],
                         bank_d[:, n, :].rearrange("p (h s) -> p h s", s=S), "cross_out", 2 * t + m + 1)

            def route_exp(t):
                act.wait_ge(sig["top_bias"], t + 1)
                nc.scalar.activation(rexp[:, :], logits[:, 0:EXPERTS], ACT.Exp, bias=top_neg[:, :])\
                    .then_inc(sig["route_exp"], 1)
                nc.scalar.activation(sh_e[:, :], logits[:, EXPERTS:EXPERTS + 1], ACT.Exp, scale=-1.0)\
                    .then_inc(sig["shared_exp"], 1)

            def route_split(t):
                act.wait_ge(sig["shared_gate"], t + 1)
                act.wait_ge(sig["route_w"], t + 1)
                nc.scalar.activation(split[:, 0:EXPERTS], route[:, 0:EXPERTS], ACT.Copy)
                nc.scalar.activation(split[:, 2 * EXPERTS:2 * EXPERTS + 1], route[:, EXPERTS:EXPERTS + 1], ACT.Copy)\
                    .then_inc(sig["split_hi"], 1)

            def route_store(t):
                act.wait_ge(sig["w_transposed"], t + 1)
                act.wait_ge(sig["wt_stored"], 16 * t)
                act.wait_ge(sig["sh_stored"], 16 * t)
                nc.scalar.activation(wt[:, :], bank_e[:, 0, 0:P], ACT.Copy)
                nc.scalar.activation(sht[:, :], bank_e[0:2, 0, P:2 * P], ACT.Copy).then_inc(sig["wt_copied"], 1)

            def step(a, b, c, d, e):
                if c is not None:
                    square_queries(c, 0)
                if d is not None:
                    cross_exp(d)
                if c is not None:
                    for g in range(1, KV):
                        square_queries(c, g)
                if a is not None:
                    copy("xn_hi", flat(xnt[HI][:, :, :]), bank_a[:, 0, 0:D], "xn_transposed", a + 1)
                if c is not None:
                    copy("ctx_hi", flat(ctxt[HI][:, :, :]), bank_a[:, 1, 0:D], "ctx_transposed", c + 1)
                if b is not None:
                    copy("self_pt_copied", p1t[:, :], bank_b[:, 0, 0:P], "self_pt", b + 1)
                    copy("self_ot", flat(o1t[:, :, :]), bank_b[:, 0, 0:D], "self_out", b + 1)
                if c is not None:
                    act.wait_ge(sig["v2_biased"], c)
                    copy("v2_copied", v2_new[:, :], bank_c[:, 1, :], "v2_projected", c + 1)
                if d is not None:
                    copy("cross_pt_copied", flat(p2t[:, :, :]), flat(bank_d[:, :, :]), "cross_pt", d + 1)
                if e is not None:
                    act.wait_ge(sig["x2_stored"], 16 * e)
                    copy("x2t_copied", flat(x2t[:, :, :]), bank_e[:, 0, 0:D], "x2_transposed", e + 1)
                if a is not None:
                    copy("qk_copied", qk[:, :], bank_a[:, 1, :], "qk_projected", a + 1)
                    copy("v_copied", v[:, :], bank_a[:, 0, 0:D], "v_projected", a + 1)
                if d is not None:
                    cross_out_high(d, 0)
                if c is not None:
                    copy_queries(c, 0)
                if a is not None:
                    copy("qkt_copied", flat(qkt[:, :, :]), bank_a[:, 0, :], "qk_transposed", a + 1)
                if e is not None:
                    route_exp(e)
                if d is not None:
                    cross_out_high(d, 1)
                if c is not None:
                    copy_keys(c)
                    copy_queries(c, 1)
                if b is not None:
                    copy("x1_hi", flat(x1t[HI][:, :, :]), bank_b[:, 0, 0:D], "x1_transposed", b + 1)
                if a is not None:
                    self_exp(a)
                if e is not None:
                    route_split(e)
                    route_store(e)

            copy("qkv_hi", flat(qkv_w[HI][:, :, :]), q_work[:, 0:C * 3 * D], "qkv_loaded", 16)
            copy("wkv_hi", flat(wkv_w[HI][:, :, :]), stage_b[:, 0:C * 2 * KW], "wkv_loaded", 32)
            act.wait_ge(sig["small_loaded"], 16 * 11)
            copy("wq_hi", flat(wq_w[HI][:, :, :]), q_work[:, :], "wq_loaded", 16)
            copy("wo_hi", flat(wo_w[HI][:, :, :]), stage_b[:, :], "wo_loaded", 16)
            act.wait_ge(sig["key_scale"], 1)
            pipeline(act, step)

        @block.vector
        def _(dve):
            def low(done, target, source, high, ready, count):
                dve.wait_ge(sig[ready], count)
                nc.vector.tensor_tensor(target, source, high.bitcast(F32), ALU.subtract).then_inc(sig[done], 1)

            def moments(source, stat, mv, ve, name, n1):
                nc.vector.bn_stats(stat[:, :], source[:, :]).then_inc(sig[name + "_stats"], 1)
                wait_alone(dve, sig[name + "_stats"], n1, sig["dve_held"])
                nc.vector.bn_aggr(mv[:, :], stat[:, :]).then_inc(sig[name + "_moments"], 1)
                dve.wait_ge(sig[name + "_moments"], n1)
                nc.vector.tensor_scalar_add(ve[:, :], mv[:, 1:2], LN_EPS).then_inc(sig[name + "_var"], 1)

            def normalise(done, target, source, mv, rs, name, n1):
                dve.wait_ge(sig[name + "_rstd"], n1)
                nc.vector.tensor_scalar(target[:, :], source[:, :], mv[:, 0:1], rs[:, :], ALU.subtract, ALU.mult)\
                    .then_inc(sig[done], 1)

            def x_moments(t):
                dve.wait_ge(sig["x_loaded"], 16 * t + 16)
                moments(x_in, x_stat, x_mv, x_ve, "x", t + 1)

            def x_norm(t):
                normalise("x_hat", x_hat, x_in, x_mv, x_rs, "x", t + 1)

            def x_low(t):
                low("xn_lo", flat(xnt[LO][:, :, :]), bank_a[:, 0, 0:D], flat(xnt[HI][:, :, :]), "xn_hi", t + 1)

            def self_mask(t):
                dve.wait_ge(sig["self_scored"], t + 1)
                nc.vector.tensor_tensor(s1[:, :], bank_a[:, 1, 0:P], causal[:, :], ALU.add)\
                    .then_inc(sig["self_masked"], 1)
                dve.wait_ge(sig["self_masked"], t + 1)
                nc.vector.reduce_max(s1_max[:, :], s1[:, :], AX.X).then_inc(sig["self_max"], 1)
                dve.wait_ge(sig["self_max"], t + 1)
                nc.vector.tensor_scalar_mul(s1_bias[:, :], s1_max[:, :], -SELF_SCALE).then_inc(sig["self_bias"], 1)

            def self_normalise(t):
                dve.wait_ge(sig["self_exp"], t + 1)
                nc.vector.reciprocal(p1_rec[:, :], p1_sum[:, :]).then_inc(sig["self_recip"], 1)
                dve.wait_ge(sig["self_recip"], t + 1)
                nc.vector.tensor_scalar_mul(p1n[:, :], p1[:, :], p1_rec[:, :]).then_inc(sig["self_probs"], 1)

            def x1_norm(t):
                dve.wait_ge(sig["self_proj"], t + 1)
                dve.wait_ge(sig["x_res_loaded"], 16 * t + 16)
                nc.vector.scalar_tensor_tensor(h1[:, :], x_res[:, :], 2.0, bank_b[:, 0, 0:D], ALU.mult, ALU.add)\
                    .then_inc(sig["h1_done"], 1)
                dve.wait_ge(sig["h1_done"], t + 1)
                moments(h1, h1_stat, h1_mv, h1_ve, "h1", t + 1)
                dve.wait_ge(sig["x1_stored"], 16 * t)
                normalise("x1_normed", x1, h1, h1_mv, h1_rs, "h1", t + 1)

            def x1_low(t):
                low("x1_lo", flat(x1t[LO][:, :, :]), bank_b[:, 0, 0:D], flat(x1t[HI][:, :, :]), "x1_hi", t + 1)

            def ctx_low(t):
                low("ctx_lo", flat(ctxt[LO][:, :, :]), bank_a[:, 1, 0:D], flat(ctxt[HI][:, :, :]), "ctx_hi", t + 1)

            def bias_keys(t):
                dve.wait_ge(sig["k_projected"], t + 1)
                nc.vector.tensor_tensor(flat(k2[:, :, :]), bank_c[:, 0, :], bkv_b[:, 0:KW], ALU.add)\
                    .then_inc(sig["k_biased"], 1)

            def mean_square(squares, ss, ve, name, n1):
                nc.vector.tensor_reduce(ss[:, :], squares, AX.X, ALU.add).then_inc(sig[name + "_sumsq"], 1)
                dve.wait_ge(sig[name + "_sumsq"], n1)
                nc.vector.tensor_scalar(ve[:, :], ss[:, :], 1.0 / HD, RMS_EPS, ALU.mult, ALU.add)\
                    .then_inc(sig[name + "_var"], 1)

            def key_square(t):
                dve.wait_ge(sig["k_squared"], t + 1)
                mean_square(k2s[:, :, :], k2_ss, k2_ve, "k", t + 1)

            def query_bias(t, g):
                dve.wait_ge(sig["q_projected"], 4 * t + g + 1)
                nc.vector.tensor_tensor(q_work[:, g * 512:(g + 1) * 512], bank_c[:, g % 2, :],
                                        bq_b[:, g * 512:(g + 1) * 512], ALU.add).then_inc(sig["q_biased"], 1)

            def query_square(t):
                dve.wait_ge(sig["q_squared"], 4 * t + 4)
                mean_square(q2s[:, :, :], q2_ss, q2_ve, "q", t + 1)

            def query_norm(t):
                dve.wait_ge(sig["q_rstd"], t + 1)
                nc.vector.tensor_tensor(q2s[:, 0:half, :], q2[:, 0:half, :],
                                        q2_rs[:, 0:half].unsqueeze(2).to_broadcast([P, half, HD]), ALU.mult)\
                    .then_inc(sig["q_normed_a"], 1)

            def cross_mask(t):
                for n in range(2):
                    dve.wait_ge(sig["scored"], 2 * t + n + 1)
                    nc.vector.tensor_tensor(s2[:, :, n, :], bank_c[:, n, :].rearrange("p (a e) -> p a e", e=S),
                                            mask_t[:, :].unsqueeze(1).to_broadcast([P, PAIRS, S]), ALU.add)\
                        .then_inc(sig["cross_masked"], 1)

            rows = s2[:, :, :, :].rearrange("p a b c -> p (a b) c")

            def cross_max(t):
                dve.wait_ge(sig["cross_masked"], 2 * t + 2)
                nc.vector.reduce_max(s2_max[:, :], rows, AX.X).then_inc(sig["cross_max"], 1)

            def cross_shift(t):
                dve.wait_ge(sig["cross_max"], t + 1)
                nc.vector.tensor_tensor(rows, rows, s2_max[:, :].unsqueeze(2).to_broadcast([P, HEADS, S]),
                                        ALU.subtract).then_inc(sig["cross_shifted"], 1)

            def cross_sum(t):
                dve.wait_ge(sig["cross_exp"], t + 1)
                nc.vector.tensor_reduce(s2_sum[:, :], rows, AX.X, ALU.add).then_inc(sig["cross_sum"], 1)
                dve.wait_ge(sig["cross_sum"], t + 1)
                nc.vector.reciprocal(s2_rec[:, :], s2_sum[:, :]).then_inc(sig["cross_recip"], 1)

            def cross_normalise(t):
                dve.wait_ge(sig["cross_recip"], t + 1)
                nc.vector.tensor_tensor(rows, rows, s2_rec[:, :].unsqueeze(2).to_broadcast([P, HEADS, S]),
                                        ALU.mult).then_inc(sig["cross_probs"], 1)

            def cross_out_low(t, m):
                for n in range(2):
                    low("ot_lo", o2t[LO][:, m * half:(m + 1) * half, n * S:(n + 1) * S],
                        bank_d[:, n, :].rearrange("p (h s) -> p h s", s=S),
                        o2t[HI][:, m * half:(m + 1) * half, n * S:(n + 1) * S], "ot_hi", 4 * t + 2 * m + n + 1)

            def x2_norm(t):
                dve.wait_ge(sig["cross_proj"], t + 1)
                dve.wait_ge(sig["x1_res_loaded"], 16 * t + 16)
                nc.vector.tensor_tensor(h2[:, :], x1_res[:, :], bank_d[:, 0, 0:D], ALU.add).then_inc(sig["h2_done"], 1)
                dve.wait_ge(sig["h2_done"], t + 1)
                moments(h2, h2_stat, h2_mv, h2_ve, "h2", t + 1)
                normalise("x2_normed", x2, h2, h2_mv, h2_rs, "h2", t + 1)

            def route_choose(t):
                n1 = t + 1
                dve.wait_ge(sig["routed"], n1)
                nc.vector.tensor_copy(logits[:, :], bank_e[:, 0, 0:EXPERTS + 1]).then_inc(sig["logits_copied"], 1)
                wait_alone(dve, sig["logits_copied"], n1, sig["dve_held"])
                nc.vector.max(top[:, :], logits[:, 0:EXPERTS]).then_inc(sig["top8"], 1)
                dve.wait_ge(sig["top8"], n1)
                nc.vector.tensor_scalar_mul(top_neg[:, :], top[:, 0:1], -1.0).then_inc(sig["top_bias"], 1)
                nc.vector.match_replace(rest[:, :], top[:, :], logits[:, 0:EXPERTS], REMOVED)\
                    .then_inc(sig["top_removed"], 1)
                dve.wait_ge(sig["top_removed"], n1)
                nc.vector.tensor_tensor(chosen[:, :], rest[:, :], logits[:, 0:EXPERTS], ALU.not_equal)\
                    .then_inc(sig["top_mask"], 1)

            def route_weigh(t):
                n1 = t + 1
                dve.wait_ge(sig["top_mask"], n1)
                dve.wait_ge(sig["route_exp"], n1)
                nc.vector.tensor_tensor(rkept[:, :], rexp[:, :], chosen[:, :], ALU.mult).then_inc(sig["route_kept"], 1)
                dve.wait_ge(sig["shared_exp"], n1)
                nc.vector.tensor_scalar_add(sh_p[:, :], sh_e[:, :], 1.0).then_inc(sig["shared_plus"], 1)
                dve.wait_ge(sig["route_kept"], n1)
                nc.vector.tensor_reduce(rsum[:, :], rkept[:, :], AX.X, ALU.add).then_inc(sig["route_sum"], 1)
                dve.wait_ge(sig["shared_plus"], n1)
                nc.vector.reciprocal(route[:, EXPERTS:EXPERTS + 1], sh_p[:, :]).then_inc(sig["shared_gate"], 1)
                dve.wait_ge(sig["route_sum"], n1)
                nc.vector.reciprocal(rrec[:, :], rsum[:, :]).then_inc(sig["route_recip"], 1)
                dve.wait_ge(sig["route_recip"], n1)
                nc.vector.tensor_scalar_mul(route[:, 0:EXPERTS], rkept[:, :], rrec[:, :]).then_inc(sig["route_w"], 1)

            def route_low(t):
                n1 = t + 1
                dve.wait_ge(sig["split_hi"], n1)
                dve.wait_ge(sig["route_w"], n1)
                dve.wait_ge(sig["shared_gate"], n1)
                parts = split[:, :].bitcast(F32)
                nc.vector.tensor_tensor(split[:, EXPERTS:2 * EXPERTS], route[:, 0:EXPERTS], parts[:, 0:EXPERTS],
                                        ALU.subtract)
                nc.vector.tensor_tensor(split[:, 2 * EXPERTS + 1:2 * EXPERTS + 2], route[:, EXPERTS:EXPERTS + 1],
                                        parts[:, 2 * EXPERTS:2 * EXPERTS + 1], ALU.subtract)\
                    .then_inc(sig["split_lo"], 1)

            def step(a, b, c, d, e):
                if a is not None:
                    x_moments(a)
                if d is not None:
                    cross_max(d)
                if a is not None:
                    x_norm(a)
                if c is not None:
                    query_bias(c, 0)
                if d is not None:
                    cross_shift(d)
                if c is not None:
                    query_bias(c, 1)
                    query_bias(c, 2)
                if d is not None:
                    cross_sum(d)
                if c is not None:
                    query_bias(c, 3)
                if d is not None:
                    cross_normalise(d)
                if a is not None:
                    x_low(a)
                if c is not None:
                    ctx_low(c)
                if e is not None:
                    x2_norm(e)
                if c is not None:
                    query_square(c)
                    bias_keys(c)
                    query_norm(c)
                    key_square(c)
                if b is not None:
                    x1_norm(b)
                if d is not None:
                    cross_out_low(d, 0)
                if e is not None:
                    route_choose(e)
                if d is not None:
                    cross_out_low(d, 1)
                if b is not None:
                    x1_low(b)
                if e is not None:
                    route_weigh(e)
                if a is not None:
                    self_mask(a)
                    self_normalise(a)
                if c is not None:
                    cross_mask(c)
                if e is not None:
                    route_low(e)

            low("qkv_lo", flat(qkv_w[LO][:, :, :]), q_work[:, 0:C * 3 * D], flat(qkv_w[HI][:, :, :]), "qkv_hi", 1)
            low("wkv_lo", flat(wkv_w[LO][:, :, :]), stage_b[:, 0:C * 2 * KW], flat(wkv_w[HI][:, :, :]), "wkv_hi", 1)
            dve.wait_ge(sig["small_loaded"], 16 * 11)
            nc.vector.tensor_tensor(qn_c[:, :], qn_c[:, :], kn_c[:, :], ALU.mult).then_inc(sig["key_scale_a"], 1)
            dve.wait_ge(sig["key_scale_a"], 1)
            nc.vector.tensor_scalar_mul(key_scale[:, :], qn_c[:, :], float(HD) ** -0.5).then_inc(sig["key_scale"], 1)
            low("wq_lo", flat(wq_w[LO][:, :, :]), q_work[:, :], flat(wq_w[HI][:, :, :]), "wq_hi", 1)
            low("wo_lo", flat(wo_w[LO][:, :, :]), stage_b[:, :], flat(wo_w[HI][:, :, :]), "wo_hi", 1)
            dve.wait_ge(sig["causal_made"], 1)
            pipeline(dve, step)


EXPERT_SIGNALS = """
dve_held2 pool_held2
weights_loaded weights_high weights_low selector_copied weights_free wt_loaded sh_loaded x_high x_low
selector_zeroed selector_half selector_made pair_ones identity_zeroed2 identity_made2 constants2
gated upped weight_spread silu_done gated_up weighted inter_hi inter_lo y_done y_added
y_final z_transposed z_copied z_stats z_moments z_var z_rstd z_normed out_stored
""".split()


def expert_phase(nc, sig, acc_loaded, gate_up, down, x2t_d, wt_d, sh_d, out):
    with ExitStack() as stack:
        def sb(name, shape, dt=F32):
            return stack.enter_context(nc.sbuf_tensor(name, shape, dt))

        acc = sb("acc", [P, BLOCKS, C, BLOCK])
        xt = [sb(f"xt{n}", [P, BLOCKS, C, BLOCK], F32R) for n in (HI, LO)]
        wt = sb("wt_all", [P, N], F32R)
        gu_raw = sb("gu_raw", [P, GROUP * 4 * P])
        dp_raw = sb("dp_raw", [P, GROUP * D])
        gu = [[sb(f"gu{u}{n}", [P, GROUP, 2, C, P], F32R) for n in (HI, LO)] for u in range(2)]
        dp = [[sb(f"dp{u}{n}", [P, GROUP, D], F32R) for n in (HI, LO)] for u in range(2)]
        selector = sb("selector", [P, EPAIRS, P], BF16)
        sel = [sb(f"sel{u}", [P, GROUP, P], F32R) for u in range(2)]
        ones2_f = sb("ones2_f", [2, P])
        ones2 = sb("ones2", [2, P], F32R)
        sh = sb("sh", [2, BLOCK], F32R)
        silu = sb("silu", [P, 2, BLOCK])
        gxu = sb("gxu", [P, 2, BLOCK])
        inter = sb("inter", [P, 2, BLOCK])
        int_p = [sb(f"int_p{n}", [P, 2, BLOCK], F32R) for n in (HI, LO)]
        y_sum = sb("y_sum", [P, C, BLOCK])
        identity = sb("identity2", [P, P])
        z = sb("z", [P, 4, D])
        z_stat = sb("z_stat", [P, 4, 6])
        z_mv = sb("z_mv", [P, 4, 2])
        z_ve = sb("z_ve", [P, 4])
        z_rs = sb("z_rs", [P, 4])
        minus_half = sb("minus_half2", [P, 4])

        def bank(name, n=1):
            return stack.enter_context(nc.psum_tensor(name, [P, n, 512], F32))

        bank_gate, bank_up = bank("bank_gate", 2), bank("bank_up", 2)
        bank_w, bank_y, bank_z = bank("bank_w"), bank("bank_y", 2), bank("bank_z")

        block = stack.enter_context(nc.Block())
        GU, DP = GROUP * 4 * P, GROUP * D
        STEP = ROUNDS * UNITS

        def groups(eng, run):
            with eng.Fori(0, (GROUPS - 1) // 2) as g2:
                for u in range(2):
                    run(2 * g2 + u, u, False)
            run(GROUPS - 1, 0, True)

        def rounds(eng, run):
            run(0)
            with eng.Fori(1, ROUNDS) as r:
                run(r)

        def columns(r, k):
            return bass.ds(r * (2 * BLOCK) + (k // GROUP) * BLOCK, BLOCK)

        @block.sync
        def _(sp):
            def load_weights(g):
                sp.wait_ge(sig["weights_low"], g)
                sp.dma_start(gu_raw[:, :], gate_up[g, :, :]).then_inc(sig["weights_loaded"], 16)
                sp.dma_start(dp_raw[:, :], down[g, :, :]).then_inc(sig["weights_loaded"], 16)

            load_weights(0)
            for b in range(BLOCKS):
                sp.dma_start(acc[:, b, :, :], x2t_d[:, :, b * BLOCK:(b + 1) * BLOCK]).then_inc(acc_loaded[b], 16)
            sp.dma_start(wt[:, :].bitcast(F32), wt_d).then_inc(sig["wt_loaded"], 16)
            with sp.Fori(1, GROUPS) as g:
                load_weights(g)

            def load_shared(b):
                sp.wait_ge(sig["y_added"], b + (GROUPS - 1) * BLOCKS)
                sp.dma_start(sh[:, :].bitcast(F32), sh_d[:, bass.ts(b, BLOCK)]).then_inc(sig["sh_loaded"], 16)

            def store(b):
                sp.wait_ge(sig["z_normed"], 4 * b + 4)
                sp.dma_start(out[bass.ts(b, BLOCK), :].rearrange("(j p) d -> p j d", p=P), z[:, :, :])\
                  .then_inc(sig["out_stored"], 16)

            load_shared(0)
            with sp.Fori(1, BLOCKS) as b:
                load_shared(b)
                store(b - 1)
            store(BLOCKS - 1)
            sp.wait_ge(sig["out_stored"], 16 * BLOCKS)

        @block.gpsimd
        def _(pool):
            nc.gpsimd.memset(minus_half[:, :], -0.5).then_inc(sig["constants2"], 1)
            nc.gpsimd.memset(ones2_f[:, :], 1.0).then_inc(sig["pair_ones"], 1)
            nc.gpsimd.memset(identity[:, :], 0.0).then_inc(sig["identity_zeroed2"], 1)
            nc.gpsimd.memset(selector[:, :, :], 0.0).then_inc(sig["selector_zeroed"], 1)
            pool.wait_ge(sig["identity_zeroed2"], 1)
            nc.gpsimd.affine_select(out=identity[:, :], in_=identity[:, :], compare_op=ALU.not_equal, fill=1.0,
                                    base=0, pattern=[[-1, P]], channel_multiplier=1).then_inc(sig["identity_made2"], 1)
            pool.wait_ge(sig["selector_zeroed"], 1)
            wide = selector[:, :, :].rearrange("k p (a i) -> k p a i", a=2)
            nc.gpsimd.affine_select(out=wide, in_=wide, compare_op=ALU.not_equal, fill=1.0, base=0,
                                    pattern=[[-2, EPAIRS], [-1, 2], [0, INNER]], channel_multiplier=1)\
                .then_inc(sig["selector_half"], 1)
            pool.wait_ge(sig["selector_half"], 1)
            nc.gpsimd.affine_select(out=wide, in_=wide, compare_op=ALU.not_equal, fill=1.0, base=-EXPERTS,
                                    pattern=[[-2, EPAIRS], [-1, 2], [0, INNER]], channel_multiplier=1)\
                .then_inc(sig["selector_made"], 1)
            pool.wait_ge(sig["selector_made"], 1)
            pool.wait_ge(sig["pair_ones"], 1)
            nc.gpsimd.tensor_copy(ones2[:, :], ones2_f[:, :])

            def split_weights(g, u, last):
                if not (isinstance(g, int) and g < 2):
                    pool.wait_ge(sig["weights_free"], g - 1)
                wait_alone(pool, sig["weights_loaded"], 32 * g + 32, sig["pool_held2"])
                flat = [w[:, :, :, :, :].rearrange("p a b c n -> p (a b c n)") for w in gu[u]]
                flat_d = [w[:, :, :].rearrange("p a n -> p (a n)") for w in dp[u]]
                nc.gpsimd.tensor_copy(flat[HI], gu_raw[:, :])
                nc.gpsimd.tensor_copy(flat_d[HI], dp_raw[:, :]).then_inc(sig["weights_high"], 1)
                nc.gpsimd.tensor_copy(sel[u][:, :, :], selector[:, bass.ds(g * GROUP, GROUP), :])\
                    .then_inc(sig["selector_copied"], 1)
                pool.wait_ge(sig["weights_high"], g + 1)
                nc.gpsimd.tensor_tensor(flat[LO], gu_raw[:, :], flat[HI].bitcast(F32), ALU.subtract)
                nc.gpsimd.tensor_tensor(flat_d[LO], dp_raw[:, :], flat_d[HI].bitcast(F32), ALU.subtract)\
                    .then_inc(sig["weights_low"], 1)

            split_weights(0, 0, False)
            split_weights(1, 1, False)
            with pool.Fori(1, (GROUPS - 1) // 2) as g2:
                for u in range(2):
                    split_weights(2 * g2 + u, u, False)
            split_weights(GROUPS - 1, 0, True)
            pool.wait_ge(sig["constants2"], 1)
            with pool.Fori(0, BLOCKS) as b:
                pool.wait_ge(sig["z_var"], b + 1)
                nc.gpsimd.tensor_tensor(z_rs[:, :], z_ve[:, :], minus_half[:, :], ALU.pow).then_inc(sig["z_rstd"], 1)

        @block.tensor
        def _(pe):
            def run_group(g, u, last):
                pe.wait_ge(sig["weights_low"], g + 1)
                pe.wait_ge(sig["selector_copied"], g + 1)

                def open_unit(r, k):
                    n = STEP * g + UNITS * r + k
                    p, par = k % GROUP, k % 2
                    cols = columns(r, k)
                    if first_group:
                        pe.wait_ge(sig["x_low"], 2 * r + k // GROUP + 1)
                    if not (isinstance(n, int) and n < 2):
                        pe.wait_ge(sig["gated_up"], n - 1)
                    for which, target, done in ((0, bank_gate, "gated"), (1, bank_up, "upped")):
                        for m, (a, b) in enumerate(PASSES):
                            for c in range(C):
                                mm = nc.tensor.matmul(target[:, par, :], gu[u][a][:, p, which, c, :], xt[b][:, 2 * r + k // GROUP, c, :],
                                                      start=(m == 0 and c == 0),
                                                      stop=(m == len(PASSES) - 1 and c == C - 1))
                        mm.then_inc(sig[done], 1)
                    if not (isinstance(n, int) and n < 1):
                        pe.wait_ge(sig["weighted"], n)
                    if last and p == GROUP - 1:
                        pe.wait_ge(sig["sh_loaded"], 32 * r + 16 * (k // GROUP) + 16)
                        mm = nc.tensor.matmul(bank_w[:, 0, :], ones2[:, :], sh[:, :], start=True, stop=True)
                    else:
                        mm = nc.tensor.matmul(bank_w[:, 0, :], sel[u][:, p, :], wt[:, cols], start=True, stop=True)
                    mm.then_inc(sig["weight_spread"], 1)

                def close_unit(r, k):
                    n = STEP * g + UNITS * r + k
                    p, par = k % GROUP, k % 2
                    done = BLOCKS * g + 2 * r + k // GROUP
                    pe.wait_ge(sig["inter_lo"], n + 1)
                    if p == 0:
                        pe.wait_ge(sig["y_added"], done)
                    for c in range(C):
                        for m, (a, b) in enumerate(PASSES):
                            mm = nc.tensor.matmul(bank_y[:, c, :], dp[u][a][:, p, c * P:(c + 1) * P],
                                                  int_p[b][:, par, :], start=(p == 0 and m == 0),
                                                  stop=(p == GROUP - 1 and m == len(PASSES) - 1))
                    if p == GROUP - 1:
                        mm.then_inc(sig["y_done"], 1)

                def transpose_out(r, k):
                    done = 2 * r + k // GROUP
                    pe.wait_ge(sig["y_added"], BLOCKS * g + done + 1)
                    for n in range(2):
                        pe.wait_ge(sig["z_copied"], 2 * done + n)
                        for j in range(2):
                            for c in range(C):
                                mm = nc.tensor.transpose(bank_z[:, 0, j * D + c * P:j * D + (c + 1) * P],
                                                         y_sum[:, c, (2 * n + j) * P:(2 * n + j + 1) * P],
                                                         identity[:, :])
                        mm.then_inc(sig["z_transposed"], 1)

                def run_round(r):
                    for k in range(UNITS):
                        open_unit(r, k)
                        if k:
                            close_unit(r, k - 1)
                        elif not isinstance(r, int):
                            close_unit(r - 1, UNITS - 1)
                        if last and k % GROUP == 1:
                            if k > GROUP:
                                transpose_out(r, 0)
                            elif not isinstance(r, int):
                                transpose_out(r - 1, GROUP)

                rounds(pe, run_round)
                close_unit(ROUNDS - 1, UNITS - 1)
                if last:
                    transpose_out(ROUNDS - 1, GROUP)

            pe.wait_ge(sig["identity_made2"], 1)
            pe.wait_ge(sig["wt_loaded"], 16)
            first_group = True

            def release(g, u, last):
                run_group(g, u, last)
                pe.drain().then_inc(sig["weights_free"], 1)

            release(0, 0, False)
            first_group = False
            release(1, 1, False)
            with pe.Fori(1, (GROUPS - 1) // 2) as g2:
                for u in range(2):
                    release(2 * g2 + u, u, False)
            release(GROUPS - 1, 0, True)

        @block.scalar
        def _(act):
            for b in range(BLOCKS):
                act.wait_ge(acc_loaded[b], 16)
                nc.scalar.activation(xt[HI][:, b, :, :], acc[:, b, :, :], ACT.Copy).then_inc(sig["x_high"], 1)

            def run_group(g, u, last):
                def run_round(r):
                    for k in range(UNITS):
                        n = STEP * g + UNITS * r + k
                        par = k % 2
                        act.wait_ge(sig["gated"], n + 1)
                        nc.scalar.activation(silu[:, par, :], bank_gate[:, par, :], ACT.Silu)\
                            .then_inc(sig["silu_done"], 1)
                        act.wait_ge(sig["weighted"], n + 1)
                        nc.scalar.activation(int_p[HI][:, par, :], inter[:, par, :], ACT.Copy)\
                            .then_inc(sig["inter_hi"], 1)
                        if last and k % GROUP == 1:
                            if k > GROUP:
                                copy_out(2 * r)
                            elif not isinstance(r, int):
                                copy_out(2 * r - 1)

                def copy_out(done):
                    for m in range(2):
                        act.wait_ge(sig["z_transposed"], 2 * done + m + 1)
                        act.wait_ge(sig["out_stored"], 16 * done)
                        nc.scalar.activation(z[:, 2 * m:2 * m + 2, :].rearrange("p a n -> p (a n)"), bank_z[:, 0, :],
                                             ACT.Copy).then_inc(sig["z_copied"], 1)

                rounds(act, run_round)
                if last:
                    copy_out(BLOCKS - 1)

            groups(act, run_group)

        @block.vector
        def _(dve):
            for b in range(BLOCKS):
                dve.wait_ge(sig["x_high"], b + 1)
                nc.vector.tensor_tensor(xt[LO][:, b, :, :], acc[:, b, :, :], xt[HI][:, b, :, :].bitcast(F32),
                                        ALU.subtract).then_inc(sig["x_low"], 1)

            def run_group(g, u, last):
                def work(r, k):
                    n = STEP * g + UNITS * r + k
                    par = k % 2
                    dve.wait_ge(sig["silu_done"], n + 1)
                    dve.wait_ge(sig["upped"], n + 1)
                    nc.vector.tensor_tensor(gxu[:, par, :], silu[:, par, :], bank_up[:, par, :], ALU.mult)\
                        .then_inc(sig["gated_up"], 1)
                    dve.wait_ge(sig["gated_up"], n + 1)
                    dve.wait_ge(sig["weight_spread"], n + 1)
                    nc.vector.tensor_tensor(inter[:, par, :], gxu[:, par, :], bank_w[:, 0, :], ALU.mult)\
                        .then_inc(sig["weighted"], 1)
                    dve.wait_ge(sig["inter_hi"], n + 1)
                    nc.vector.tensor_tensor(int_p[LO][:, par, :], inter[:, par, :], int_p[HI][:, par, :].bitcast(F32),
                                            ALU.subtract).then_inc(sig["inter_lo"], 1)

                def add(r, k):
                    done = BLOCKS * g + 2 * r + k // GROUP
                    dve.wait_ge(sig["y_done"], done + 1)
                    if last:
                        dve.wait_ge(sig["z_transposed"], 2 * (2 * r + k // GROUP))
                    total = acc[:, 2 * r + k // GROUP, :, :]
                    nc.vector.tensor_tensor(y_sum[:, :, :] if last else total, total, bank_y[:, :, :], ALU.add)\
                        .then_inc(sig["y_added"], 1)

                def finish(done):
                    dve.wait_ge(sig["z_copied"], 2 * done + 2)
                    for j in range(4):
                        st = nc.vector.bn_stats(z_stat[:, j, :], z[:, j, :])
                    st.then_inc(sig["z_stats"], 1)
                    wait_alone(dve, sig["z_stats"], done + 1, sig["dve_held2"])
                    for j in range(4):
                        st = nc.vector.bn_aggr(z_mv[:, j, :], z_stat[:, j, :])
                    st.then_inc(sig["z_moments"], 1)
                    dve.wait_ge(sig["z_moments"], done + 1)
                    nc.vector.tensor_scalar_add(z_ve[:, :], z_mv[:, :, 1], LN_EPS).then_inc(sig["z_var"], 1)
                    dve.wait_ge(sig["z_rstd"], done + 1)
                    for j in range(4):
                        nc.vector.tensor_scalar(z[:, j, :], z[:, j, :], z_mv[:, j, 0:1], z_rs[:, j:j + 1],
                                                ALU.subtract, ALU.mult).then_inc(sig["z_normed"], 1)

                def run_round(r):
                    for k in range(UNITS):
                        work(r, k)
                        if k % GROUP == 0:
                            if k:
                                add(r, k - 1)
                            elif not isinstance(r, int):
                                add(r - 1, UNITS - 1)
                        if last and k % GROUP == 2:
                            if k > GROUP:
                                finish(2 * r)
                            elif not isinstance(r, int):
                                finish(2 * r - 1)

                rounds(dve, run_round)
                add(ROUNDS - 1, UNITS - 1)
                if last:
                    finish(BLOCKS - 1)

            groups(dve, run_group)


def kernel(**inputs):
    import numpy as np
    import concourse.bacc as bacc
    from concourse.bass_utils import run_bass_kernel_spmd

    def of(name):
        return np.asarray(inputs[name])

    gu = np.zeros((2 * EPAIRS, 2, INNER, D), np.float32)
    gu[:EXPERTS] = of("L0_ffn_gu_w").reshape(EXPERTS, 2, INNER, D)
    gu[EXPERTS, 0] = of("L0_ffn_sh_gate_w")
    gu[EXPERTS, 1] = of("L0_ffn_sh_up_w")
    gu = gu.reshape(GROUPS, GROUP, 2, 2, INNER, C, P).transpose(0, 6, 1, 3, 5, 2, 4)
    dp = np.zeros((2 * EPAIRS, D, INNER), np.float32)
    dp[:EXPERTS] = of("L0_ffn_dp_w")
    dp[EXPERTS] = of("L0_ffn_sh_down_w")
    dp = dp.reshape(GROUPS, GROUP, 2, D, INNER).transpose(0, 2, 4, 1, 3)
    router = np.zeros((D, EXPERTS + 1), np.float32)
    router[:, :EXPERTS] = of("L0_ffn_gate_w").T
    router[:, EXPERTS] = of("L0_ffn_sh_gate1_w")[0]

    arrays = {
        "x": of("x").reshape(N, D), "ctx": of("ctx_2048").reshape(N, D), "mask": of("mask_1xSxS2_ff0").reshape(S, S),
        "qkv": of("L0_attn_qkv"), "o_proj": of("L0_attn_o_proj"), "gamma": of("L0_attn_gamma"),
        "beta": of("L0_attn_beta"), "wq": of("L0_xattn_Wq"), "bq": of("L0_xattn_bq"), "wk": of("L0_xattn_Wk"),
        "bk": of("L0_xattn_bk"), "wv": of("L0_xattn_Wv"), "bv": of("L0_xattn_bv"), "wo": of("L0_xattn_Wo"),
        "qn_w": of("L0_xattn_qn_w"), "kn_w": of("L0_xattn_kn_w"), "router": router,
        "gate_up": gu.reshape(GROUPS, P, GROUP * 4 * P), "down": dp.reshape(GROUPS, P, GROUP * D),
    }
    arrays = {f"in_{name}": np.ascontiguousarray(a) for name, a in arrays.items()}
    nc = bacc.Bacc("TRN2", target_bir_lowering=False, num_devices=1)
    args = [nc.dram_tensor(name, a.shape, mybir.dt.from_np(a.dtype), kind="ExternalInput").ap()
            for name, a in arrays.items()]
    out = nc.dram_tensor("out", [N, D], F32, kind="ExternalOutput").ap()
    decoder(nc, *args, out)
    result = run_bass_kernel_spmd(nc, [arrays], core_ids=[0])
    return result.results[0]["out"].reshape(B, S, D)
```

```python
from contextlib import ExitStack

import concourse.bass as bass
from concourse import mybir

F32 = mybir.dt.float32
F32R = mybir.dt.float32r
BF16 = mybir.dt.bfloat16
ALU = mybir.AluOpType
ACT = mybir.ActivationFunctionType
AX = mybir.AxisListType

P = 128
B, S, D = 64, 64, 256
C = D // P
N = B * S
TILES = N // P
HEADS, KV, HD = 16, 4, 128
PAIRS = HEADS // 2
QW, KW = HEADS * HD, KV * HD
EXPERTS, INNER, TOP_K = 64, 64, 8
EPAIRS = EXPERTS // 2 + 1
GROUP = 3
GROUPS = EPAIRS // GROUP
BLOCK = 512
BLOCKS = N // BLOCK
ROUNDS = BLOCKS // 2
UNITS = 2 * GROUP
LN_EPS, RMS_EPS = 1e-5, 1e-6
SELF_SCALE = float(D) ** -0.5
MASKED = -1e30
REMOVED = -3e38
HI, LO = 0, 1
PASSES = ((HI, HI), (LO, HI), (HI, LO))


def decoder(nc, x, ctx, mask, qkv, o_proj, gamma, beta, wq, bq, wk, bk, wv, bv, wo, qn_w, kn_w, router, gate_up,
            down, out):
    x1_d = nc.dram_tensor("x1_scratch", [N, D], F32).ap()
    x2t_d = nc.dram_tensor("x2t_scratch", [P, C, N], F32).ap()
    wt_d = nc.dram_tensor("route_weight_scratch", [2 * EPAIRS, N], F32).ap()
    raw = ExitStack()
    gu_raw = raw.enter_context(nc.sbuf_tensor("gu_raw", [P, GROUP * 4 * P], F32))
    dp_raw = raw.enter_context(nc.sbuf_tensor("dp_raw", [P, GROUP * D], F32))
    attention = {name: nc.alloc_semaphore(name) for name in ATTENTION_SIGNALS}
    attention_phase(nc, attention, x, ctx, mask, qkv, o_proj, gamma, beta, wq, bq, wk, bk, wv, bv, wo, qn_w, kn_w,
                    router, x1_d, x2t_d, wt_d, gate_up, down, gu_raw, dp_raw)
    nc.clear_and_free_semaphores(list(attention.values()))
    nc.all_engine_barrier()
    expert = {name: nc.alloc_semaphore(name) for name in EXPERT_SIGNALS}
    acc_loaded = [nc.alloc_semaphore(f"acc_loaded{b}") for b in range(BLOCKS)]
    expert_phase(nc, expert, acc_loaded, gate_up, down, gu_raw, dp_raw, x2t_d, wt_d, out)
    raw.close()


def wait_alone(eng, signal, count, held):
    eng.wait_ge(signal, count)
    eng.sem_inc(held)


ATTENTION_SIGNALS = """
dve_held sp_held
norm_loaded qkv_loaded wkv_loaded wq_loaded wo_loaded small_loaded first_experts_loaded
qkv_hi qkv_lo wkv_hi wkv_lo wq_hi wq_lo wo_hi wo_lo
key_scale_a key_scale constants identity_zeroed identity_made causal_zeroed causal_half causal_made
x_loaded x_res_loaded x1_res_loaded x1_stored x_stats x_moments x_var x_rstd x_hat x_scaled x_normed xn_transposed
xn_hi xn_lo qk_projected v_projected qk_copied v_copied qk_transposed qkt_copied self_scored self_masked self_max
self_bias self_exp self_recip self_probs self_pt self_pt_copied self_out self_ot self_proj h1_done h1_stats h1_moments h1_var
h1_rstd x1_normed x1_transposed x1_hi x1_lo
ctx_loaded ctx_hi ctx_lo k_projected v2_projected k_biased v2_copied v2_biased k_squared k_sumsq k_var k_rstd
k_normed k_transposed kt_copied q_projected q_biased q_squared q_sumsq q_var q_rstd q_normed_a q_normed_b q_transposed
qt_copied scored cross_masked cross_max cross_shifted cross_exp cross_sum cross_recip cross_probs cross_pt
cross_pt_copied cross_out ot_hi ot_lo cross_proj h2_done h2_stats h2_moments h2_var h2_rstd x2_normed x2_transposed
x2t_copied x2_stored routed logits_copied top8 top_removed top_mask top_bias route_exp shared_exp route_kept route_sum
shared_plus route_recip shared_gate route_w w_transposed wt_copied wt_stored
""".split()


def attention_phase(nc, sig, x, ctx, mask, qkv, o_proj, gamma, beta, wq, bq, wk, bk, wv, bv, wo, qn_w, kn_w, router,
                    x1_d, x2t_d, wt_d, gate_up, down, gu_raw, dp_raw):
    with ExitStack() as stack:
        def sb(name, shape, dt=F32):
            return stack.enter_context(nc.sbuf_tensor(name, shape, dt))

        qkv_w = [sb(f"qkv_w{n}", [P, C, 3 * D], F32R) for n in (HI, LO)]
        wq_w = [sb(f"wq_w{n}", [P, C, QW], F32R) for n in (HI, LO)]
        wkv_w = [sb(f"wkv_w{n}", [P, C, 2 * KW], F32R) for n in (HI, LO)]
        wo_w = [sb(f"wo_w{n}", [P, HEADS, D], F32R) for n in (HI, LO)]
        o_w = sb("o_w", [P, C, D])
        router_w = sb("router_w", [P, C, EXPERTS + 1])
        stage_b = sb("stage_b", [P, HEADS * D])
        bq_b = sb("bq_b", [P, QW])
        bkv_b = sb("bkv_b", [P, 2 * KW])
        gamma_b = sb("gamma_b", [P, D])
        beta_b = sb("beta_b", [P, D])
        mask_t = sb("mask_t", [P, S])
        causal = sb("causal", [P, P])
        identity = sb("identity", [P, P])
        minus_half = sb("minus_half", [P, HEADS])
        qn_c = sb("qn_c", [P, 1])
        kn_c = sb("kn_c", [P, 1])
        key_scale = sb("key_scale", [P, 1])

        x_in = sb("x_in", [P, D])
        x_res = sb("x_res", [P, D])
        x_stat = sb("x_stat", [P, 6])
        x_mv = sb("x_mv", [P, 2])
        x_ve = sb("x_ve", [P, 1])
        x_rs = sb("x_rs", [P, 1])
        x_hat = sb("x_hat", [P, D])
        x_g = sb("x_g", [P, D])
        x_n = sb("x_n", [P, D])
        xnt = [sb(f"xnt{n}", [P, C, P], F32R) for n in (HI, LO)]
        qk = sb("qk", [P, 2 * D])
        v = sb("v", [P, D])
        qkt = sb("qkt", [P, 2 * C, P])
        s1 = sb("s1", [P, P])
        s1_max = sb("s1_max", [P, 1])
        s1_bias = sb("s1_bias", [P, 1])
        p1 = sb("p1", [P, P])
        p1_sum = sb("p1_sum", [P, 1])
        p1_rec = sb("p1_rec", [P, 1])
        p1n = sb("p1n", [P, P])
        p1t = sb("p1t", [P, P])
        o1t = sb("o1t", [P, C, P])
        h1 = sb("h1", [P, D])
        h1_stat = sb("h1_stat", [P, 6])
        h1_mv = sb("h1_mv", [P, 2])
        h1_ve = sb("h1_ve", [P, 1])
        h1_rs = sb("h1_rs", [P, 1])
        x1 = sb("x1", [P, D])
        x1t = [sb(f"x1t{n}", [P, C, P], F32R) for n in (HI, LO)]

        ctx_in = sb("ctx_in", [P, C, P])
        x1_res = sb("x1_res", [P, D])
        ctxt = [sb(f"ctxt{n}", [P, C, P], F32R) for n in (HI, LO)]
        k2 = sb("k2", [P, KV, HD])
        v2_new = sb("v2_new", [P, KW])
        v2 = sb("v2", [P, KV, HD])
        k2s = sb("k2s", [P, KV, HD])
        k2_ss = sb("k2_ss", [P, KV])
        k2_ve = sb("k2_ve", [P, KV])
        k2_rs = sb("k2_rs", [P, KV])
        k2t = sb("k2t", [P, KV, P])
        q_work = sb("q_work", [P, 2 * QW])
        q2 = q_work[:, 0:QW].rearrange("p (h d) -> p h d", d=HD)
        q2s = q_work[:, QW:2 * QW].rearrange("p (h d) -> p h d", d=HD)
        q2_ss = sb("q2_ss", [P, HEADS])
        q2_ve = sb("q2_ve", [P, HEADS])
        q2_rs = sb("q2_rs", [P, HEADS])
        q2t = stage_b[:, 0:QW].rearrange("p (b h s) -> p b h s", b=2, s=S)
        s2 = stage_b[:, QW:QW + PAIRS * P].rearrange("p (a b e) -> p a b e", b=2, e=S)
        p2t = stage_b[:, QW + PAIRS * P:QW + 2 * PAIRS * P].rearrange("p (a n) -> p a n", n=P)
        s2_max = sb("s2_max", [P, HEADS])
        s2_sum = sb("s2_sum", [P, HEADS])
        s2_rec = sb("s2_rec", [P, HEADS])
        o2t = [sb(f"o2t{n}", [P, HEADS, P], F32R) for n in (HI, LO)]
        h2 = sb("h2", [P, D])
        h2_stat = sb("h2_stat", [P, 6])
        h2_mv = sb("h2_mv", [P, 2])
        h2_ve = sb("h2_ve", [P, 1])
        h2_rs = sb("h2_rs", [P, 1])
        x2 = sb("x2", [P, D])
        x2t = sb("x2t", [P, C, P])
        logits = sb("logits", [P, EXPERTS + 1])
        top = sb("top", [P, TOP_K])
        rest = sb("rest", [P, EXPERTS])
        chosen = sb("chosen", [P, EXPERTS])
        top_neg = sb("top_neg", [P, 1])
        rexp = sb("rexp", [P, EXPERTS])
        rkept = sb("rkept", [P, EXPERTS])
        rsum = sb("rsum", [P, 1])
        rrec = sb("rrec", [P, 1])
        route = sb("route", [P, 2 * EPAIRS])
        sh_e = sb("sh_e", [P, 1])
        sh_p = sb("sh_p", [P, 1])
        wt = sb("wt", [2 * EPAIRS, P])

        def bank(name, n):
            return stack.enter_context(nc.psum_tensor(name, [P, n, 512], F32))

        bank_a, bank_b, bank_c, bank_d, bank_e = bank("bank_a", 2), bank("bank_b", 1), bank("bank_c", 2), \
            bank("bank_d", 2), bank("bank_e", 1)

        def split3(w):
            return w.rearrange("(c p) n -> p c n", p=P)

        def at(tile, stage, *which):
            if tile is not None:
                stage(tile, *which)

        def flat(a):
            return a.rearrange("p a b -> p (a b)")

        half = HEADS // 2
        SMALL = 9
        LAG = 5

        def pipeline(eng, step, until=TILES, ahead=None):
            def peeled(i):
                step(*(i - k if 0 <= i - k < TILES else None for k in range(LAG + 1)))

            for i in range(LAG + 1):
                if ahead:
                    ahead(i)
                peeled(i)
            with eng.Fori(LAG + 1, until) as i:
                step(*(i - k if k else i for k in range(LAG + 1)))
            for i in range(until, TILES + LAG):
                peeled(i)

        block = stack.enter_context(nc.Block())

        @block.sync
        def _(sp):
            def load_x(t):
                sp.wait_ge(sig["x_hat"], t)
                sp.dma_start(x_in[:, :], x[bass.ts(t, P), :]).then_inc(sig["x_loaded"], 16)

            def load_ctx(t):
                wait_alone(sp, sig["ctx_lo"], t, sig["sp_held"])
                sp.dma_start(ctx_in[:, :, :], ctx[:, :, bass.ts(t, P)]).then_inc(sig["ctx_loaded"], 16)

            def load_x_residual(t):
                sp.wait_ge(sig["h1_done"], t)
                sp.dma_start(x_res[:, :], x[bass.ts(t, P), :]).then_inc(sig["x_res_loaded"], 16)

            def load_x1_residual(t):
                wait_alone(sp, sig["x1_stored"], 16 * t + 16, sig["sp_held"])
                sp.wait_ge(sig["h2_done"], t)
                sp.dma_start(x1_res[:, :], x1_d[bass.ts(t, P), :]).then_inc(sig["x1_res_loaded"], 16)

            def store_x1(t):
                sp.wait_ge(sig["x1_normed"], t + 1)
                sp.dma_start(x1_d[bass.ts(t, P), :], x1[:, :]).then_inc(sig["x1_stored"], 16)

            def store_x2(t):
                wait_alone(sp, sig["x2t_copied"], t + 1, sig["sp_held"])
                sp.dma_start(x2t_d[:, :, bass.ts(t, P)], x2t[:, :, :]).then_inc(sig["x2_stored"], 16)

            def store_routes(t):
                sp.wait_ge(sig["wt_copied"], t + 1)
                sp.dma_start(wt_d[:, bass.ts(t, P)], wt[:, :]).then_inc(sig["wt_stored"], 16)

            def more(t):
                return t is not None and not (isinstance(t, int) and t + 1 >= TILES)

            def step(a, b, c, d, e, f):
                at(e, load_x1_residual)
                at(b, load_x_residual)
                if more(a):
                    load_x(a + 1)
                if more(c):
                    load_ctx(c + 1)
                at(e, store_x2)
                at(b, store_x1)
                at(e, store_routes)

            sp.dma_start(x_in[:, :], x[0:P, :]).then_inc(sig["x_loaded"], 16)
            for part, source in ((gamma_b, gamma), (beta_b, beta)):
                sp.dma_start(part[:, :], source.partition_broadcast(P)).then_inc(sig["norm_loaded"], 16)
            sp.dma_start(q_work[:, 0:C * 3 * D].rearrange("p (c n) -> p c n", c=C), split3(qkv))\
              .then_inc(sig["qkv_loaded"], 16)
            kv_stage = stage_b[:, 0:C * 2 * KW].rearrange("p (c n) -> p c n", c=C)
            sp.dma_start(kv_stage[:, :, 0:KW], split3(wk)).then_inc(sig["wkv_loaded"], 16)
            sp.dma_start(kv_stage[:, :, KW:2 * KW], split3(wv)).then_inc(sig["wkv_loaded"], 16)
            sp.dma_start(ctx_in[:, :, :], ctx[:, :, 0:P]).then_inc(sig["ctx_loaded"], 16)
            sp.wait_ge(sig["qkv_lo"], 1)
            sp.dma_start(q_work[:, :].rearrange("p (c n) -> p c n", c=C), split3(wq)).then_inc(sig["wq_loaded"], 16)

            def ahead(i):
                if i == 1:
                    sp.wait_ge(sig["wkv_lo"], 1)
                    sp.dma_start(stage_b[:, :].rearrange("p (h n) -> p h n", h=HEADS),
                                 wo.rearrange("(h p) n -> p h n", p=P)).then_inc(sig["wo_loaded"], 16)
                elif i == LAG:
                    sp.dma_start(gu_raw[:, :], gate_up[0, :, :]).then_inc(sig["first_experts_loaded"], 16)
                    sp.dma_start(dp_raw[:, :], down[0, :, :]).then_inc(sig["first_experts_loaded"], 16)

            pipeline(sp, step, TILES - 1, ahead)
            sp.wait_ge(sig["first_experts_loaded"], 32)
            for name in ("x2_stored", "wt_stored"):
                sp.wait_ge(sig[name], 16 * TILES)

        @block.gpsimd
        def _(pool):
            nc.gpsimd.memset(minus_half[:, :], -0.5).then_inc(sig["constants"], 1)
            nc.gpsimd.memset(route[:, EXPERTS + 1:], 0.0).then_inc(sig["constants"], 1)
            nc.gpsimd.memset(identity[:, :], 0.0).then_inc(sig["identity_zeroed"], 1)
            nc.gpsimd.memset(causal[:, :], 0.0).then_inc(sig["causal_zeroed"], 1)
            pool.wait_ge(sig["identity_zeroed"], 1)
            nc.gpsimd.affine_select(out=identity[:, :], in_=identity[:, :], compare_op=ALU.not_equal, fill=1.0,
                                    base=0, pattern=[[-1, P]], channel_multiplier=1).then_inc(sig["identity_made"], 1)
            pool.wait_ge(sig["causal_zeroed"], 1)
            nc.gpsimd.affine_select(out=causal[:, :], in_=causal[:, :], compare_op=ALU.is_ge, fill=MASKED,
                                    base=0, pattern=[[-1, P]], channel_multiplier=1).then_inc(sig["causal_half"], 1)
            pool.wait_ge(sig["causal_half"], 1)
            nc.gpsimd.affine_select(out=causal[:, 0:S], in_=causal[:, 0:S], compare_op=ALU.is_ge, fill=MASKED,
                                    base=S - 1, pattern=[[0, S]], channel_multiplier=-1)\
                .then_inc(sig["causal_made"], 1)
            pool.wait_ge(sig["constants"], 2)
            pool.wait_ge(sig["norm_loaded"], 32)

            def ahead(i):
                if i == 1:
                    pool.wait_ge(sig["wkv_hi"], 1)
                    nc.gpsimd.tensor_tensor(flat(wkv_w[LO][:, :, :]), stage_b[:, 0:C * 2 * KW],
                                            flat(wkv_w[HI][:, :, :]).bitcast(F32), ALU.subtract)\
                        .then_inc(sig["wkv_lo"], 1)

            def power(done, out_, base, width, start, n1):
                pool.wait_ge(sig[start], n1)
                nc.gpsimd.tensor_tensor(out_, base, minus_half[:, 0:width], ALU.pow).then_inc(sig[done], 1)

            def power_x(t):
                power("x_rstd", x_rs[:, :], x_ve[:, :], 1, "x_var", t + 1)

            def power_h1(t):
                power("h1_rstd", h1_rs[:, :], h1_ve[:, :], 1, "h1_var", t + 1)

            def power_h2(t):
                power("h2_rstd", h2_rs[:, :], h2_ve[:, :], 1, "h2_var", t + 1)

            def scale_x(t):
                pool.wait_ge(sig["x_hat"], t + 1)
                nc.gpsimd.tensor_tensor(x_g[:, :], x_hat[:, :], gamma_b[:, :], ALU.mult).then_inc(sig["x_scaled"], 1)
                pool.wait_ge(sig["x_scaled"], t + 1)
                nc.gpsimd.tensor_tensor(x_n[:, :], x_g[:, :], beta_b[:, :], ALU.add).then_inc(sig["x_normed"], 1)

            def power_queries(t, n):
                heads = slice(n * half, (n + 1) * half)
                power("q_rstd", q2_rs[:, heads], q2_ve[:, heads], half, "q_var", 2 * t + n + 1)

            def power_keys(t):
                power("k_rstd", k2_rs[:, :], k2_ve[:, :], KV, "k_var", t + 1)

            def square_keys(t):
                pool.wait_ge(sig["k_biased"], t + 1)
                nc.gpsimd.tensor_tensor(k2s[:, :, :], k2[:, :, :], k2[:, :, :], ALU.mult).then_inc(sig["k_squared"], 1)

            def scale_queries(t):
                pool.wait_ge(sig["q_rstd"], 2 * t + 2)
                nc.gpsimd.tensor_tensor(q2s[:, half:, :], q2[:, half:, :],
                                        q2_rs[:, half:].unsqueeze(2).to_broadcast([P, half, HD]),
                                        ALU.mult).then_inc(sig["q_normed_b"], 1)

            def scale_keys(t):
                pool.wait_ge(sig["k_rstd"], t + 1)
                nc.gpsimd.tensor_tensor(k2s[:, :, :], k2[:, :, :], k2_rs[:, :].unsqueeze(2).to_broadcast([P, KV, HD]),
                                        ALU.mult).then_inc(sig["k_normed"], 1)

            def bias_values(t):
                if isinstance(t, int) and t == 0:
                    pool.wait_ge(sig["small_loaded"], 16 * SMALL)
                pool.wait_ge(sig["v2_copied"], t + 1)
                pool.wait_ge(sig["cross_out"], 2 * t)
                nc.gpsimd.tensor_tensor(flat(v2[:, :, :]), v2_new[:, :], bkv_b[:, KW:2 * KW], ALU.add)\
                    .then_inc(sig["v2_biased"], 1)

            def step(a, b, c, d, e, f):
                at(d, power_keys)
                at(d, scale_keys)
                at(d, scale_queries)
                at(a, power_x)
                at(c, power_h1)
                at(a, scale_x)
                at(d, bias_values)
                at(e, power_h2)
                at(c, power_queries, 0)
                at(c, square_keys)
                at(c, power_queries, 1)

            pipeline(pool, step, ahead=ahead)

        @block.tensor
        def _(pe):
            def transpose_in(target, source):
                for c in range(C):
                    last = nc.tensor.transpose(target[:, c * P:(c + 1) * P], source[:, c * P:(c + 1) * P],
                                               identity[:, :])
                return last

            def product(target, left, right):
                for n, (a, b) in enumerate(PASSES):
                    for c in range(C):
                        last = nc.tensor.matmul(target, left[a][:, c, :], right(b, c), start=(n == 0 and c == 0),
                                                stop=(n == len(PASSES) - 1 and c == C - 1))
                return last

            def x_transpose(t):
                pe.wait_ge(sig["x_normed"], t + 1)
                pe.wait_ge(sig["qkt_copied"], t)
                transpose_in(bank_a[:, 0, :], x_n).then_inc(sig["xn_transposed"], 1)

            def self_project(t):
                if isinstance(t, int) and t == 0:
                    pe.wait_ge(sig["qkv_lo"], 1)
                pe.wait_ge(sig["xn_lo"], t + 1)
                product(bank_a[:, 1, :], xnt, lambda b, c: qkv_w[b][:, c, 0:2 * D]).then_inc(sig["qk_projected"], 1)
                product(bank_a[:, 0, 0:D], xnt, lambda b, c: qkv_w[b][:, c, 2 * D:3 * D])\
                    .then_inc(sig["v_projected"], 1)

            def self_transpose(t):
                pe.wait_ge(sig["qk_copied"], t + 1)
                pe.wait_ge(sig["v_copied"], t + 1)
                for c in range(2 * C):
                    last = nc.tensor.transpose(bank_a[:, 0, c * P:(c + 1) * P], qk[:, c * P:(c + 1) * P],
                                               identity[:, :])
                last.then_inc(sig["qk_transposed"], 1)

            def self_score(t):
                pe.wait_ge(sig["qkt_copied"], t + 1)
                for c in range(C):
                    last = nc.tensor.matmul(bank_a[:, 1, 0:P], qkt[:, c, :], qkt[:, C + c, :], start=(c == 0),
                                            stop=(c == C - 1))
                last.then_inc(sig["self_scored"], 1)

            def self_probs_transpose(t):
                pe.wait_ge(sig["self_probs"], t + 1)
                pe.wait_ge(sig["x1_lo"], t)
                nc.tensor.transpose(bank_b[:, 0, 0:P], p1n[:, :], identity[:, :]).then_inc(sig["self_pt"], 1)

            def self_attend(t):
                pe.wait_ge(sig["self_pt_copied"], t + 1)
                for c in range(C):
                    last = nc.tensor.matmul(bank_b[:, 0, c * P:(c + 1) * P], v[:, c * P:(c + 1) * P], p1t[:, :],
                                            start=True, stop=True)
                last.then_inc(sig["self_out"], 1)

            def self_output(t):
                if isinstance(t, int) and t == 0:
                    pe.wait_ge(sig["small_loaded"], 16 * SMALL)
                pe.wait_ge(sig["self_ot"], t + 1)
                for c in range(C):
                    last = nc.tensor.matmul(bank_b[:, 0, 0:D], o1t[:, c, :], o_w[:, c, :], start=(c == 0),
                                            stop=(c == C - 1))
                last.then_inc(sig["self_proj"], 1)

            def x1_transpose(t):
                pe.wait_ge(sig["x1_normed"], t + 1)
                transpose_in(bank_b[:, 0, :], x1).then_inc(sig["x1_transposed"], 1)

            def query_project(t, g):
                if isinstance(t, int) and t == 0 and g == 0:
                    pe.wait_ge(sig["wq_lo"], 1)
                if g == 0:
                    pe.wait_ge(sig["x1_lo"], t + 1)
                if g < 2:
                    pe.wait_ge(sig["cross_masked"], 2 * t)
                else:
                    pe.wait_ge(sig["q_biased"], 4 * t + g - 1)
                product(bank_c[:, g % 2, :], x1t, lambda b, c: wq_w[b][:, c, g * 512:(g + 1) * 512])\
                    .then_inc(sig["q_projected"], 1)

            def key_project(t):
                if isinstance(t, int) and t == 0:
                    pe.wait_ge(sig["wkv_lo"], 1)
                pe.wait_ge(sig["ctx_lo"], t + 1)
                pe.wait_ge(sig["q_biased"], 4 * t + 3)
                product(bank_c[:, 0, :], ctxt, lambda b, c: wkv_w[b][:, c, 0:KW]).then_inc(sig["k_projected"], 1)

            def value_project(t):
                pe.wait_ge(sig["q_biased"], 4 * t + 4)
                product(bank_c[:, 1, :], ctxt, lambda b, c: wkv_w[b][:, c, KW:2 * KW]).then_inc(sig["v2_projected"], 1)

            def query_transpose(t, n):
                pe.wait_ge(sig["q_normed_b" if n else "q_normed_a"], t + 1)
                if n:
                    pe.wait_ge(sig["qt_copied"], 2 * t + 1)
                else:
                    pe.wait_ge(sig["k_biased"], t + 1)
                    pe.wait_ge(sig["v2_copied"], t + 1)
                for h in range(half):
                    last = nc.tensor.transpose(bank_c[:, h // 4, (h % 4) * P:(h % 4 + 1) * P], q2s[:, n * half + h, :],
                                               identity[:, :])
                last.then_inc(sig["q_transposed"], 1)

            def key_transpose(t):
                pe.wait_ge(sig["k_normed"], t + 1)
                if not (isinstance(t, int) and t < 2):
                    pe.wait_ge(sig["logits_copied"], t - 1)
                for g in range(KV):
                    last = nc.tensor.transpose(bank_e[:, 0, g * P:(g + 1) * P], k2s[:, g, :], identity[:, :])
                last.then_inc(sig["k_transposed"], 1)

            def cross_score(t):
                pe.wait_ge(sig["kt_copied"], t + 1)
                pe.wait_ge(sig["qt_copied"], 2 * t + 2)
                for n in range(2):
                    for p in range(PAIRS):
                        last = nc.tensor.matmul(bank_c[:, n, p * S:(p + 1) * S],
                                                q2t[:, n, 2 * p:2 * p + 2, :].rearrange("p h s -> p (h s)"),
                                                k2t[:, p // 2, n * S:(n + 1) * S], start=True, stop=True)
                    last.then_inc(sig["scored"], 1)

            def cross_probs_transpose(t):
                pe.wait_ge(sig["cross_probs"], t + 1)
                pe.wait_ge(sig["h2_done"], t)
                for p in range(PAIRS):
                    last = nc.tensor.transpose(bank_d[:, p // 4, (p % 4) * P:(p % 4 + 1) * P],
                                               s2[:, p, :, :].rearrange("p a b -> p (a b)"), identity[:, :])
                last.then_inc(sig["cross_pt"], 1)

            def cross_attend(t, m):
                if m:
                    pe.wait_ge(sig["ot_lo"], 4 * t + 2)
                else:
                    pe.wait_ge(sig["cross_pt_copied"], t + 1)
                    pe.wait_ge(sig["v2_biased"], t + 1)
                for g in range(2 * m, 2 * m + 2):
                    for n in range(2):
                        last = nc.tensor.matmul(bank_d[:, n, (g % 2) * 256:(g % 2 + 1) * 256],
                                                v2[n * S:(n + 1) * S, g, :], p2t[n * S:(n + 1) * S, 2 * g:2 * g + 2, :],
                                                start=True, stop=True)
                last.then_inc(sig["cross_out"], 1)

            def cross_output(t):
                if isinstance(t, int) and t == 0:
                    pe.wait_ge(sig["wo_lo"], 1)
                pe.wait_ge(sig["ot_lo"], 4 * t + 4)
                for n, (a, b) in enumerate(PASSES):
                    for h in range(HEADS):
                        last = nc.tensor.matmul(bank_d[:, 0, 0:D], o2t[a][:, h, :], wo_w[b][:, h, :],
                                                start=(n == 0 and h == 0),
                                                stop=(n == len(PASSES) - 1 and h == HEADS - 1))
                last.then_inc(sig["cross_proj"], 1)

            def x2_transpose(t):
                pe.wait_ge(sig["x2_normed"], t + 1)
                pe.wait_ge(sig["wt_copied"], t)
                transpose_in(bank_e[:, 0, :], x2).then_inc(sig["x2_transposed"], 1)

            def route_score(t):
                pe.wait_ge(sig["x2t_copied"], t + 1)
                for c in range(C):
                    last = nc.tensor.matmul(bank_e[:, 0, 0:EXPERTS + 1], x2t[:, c, :], router_w[:, c, :],
                                            start=(c == 0), stop=(c == C - 1))
                last.then_inc(sig["routed"], 1)

            def route_transpose(t):
                pe.wait_ge(sig["route_w"], t + 1)
                pe.wait_ge(sig["shared_gate"], t + 1)
                pe.wait_ge(sig["kt_copied"], min(t + 3, TILES) if isinstance(t, int) else t + 3)
                nc.tensor.transpose(bank_e[0:2 * EPAIRS, 0, 0:P], route[:, :], identity[:, :])\
                    .then_inc(sig["w_transposed"], 1)

            def step(a, b, c, d, e, f):
                at(c, self_attend)
                at(d, query_transpose, 0)
                at(f, x2_transpose)
                at(b, self_project)
                at(f, route_score)
                at(c, self_output)
                at(b, self_transpose)
                at(d, key_transpose)
                at(d, query_transpose, 1)
                at(b, self_score)
                at(e, cross_attend, 1)
                at(d, cross_score)
                at(f, route_transpose)
                at(c, x1_transpose)
                at(a, x_transpose)
                at(e, cross_output)
                at(c, query_project, 0)
                at(c, query_project, 1)
                at(c, query_project, 2)
                at(c, query_project, 3)
                at(b, self_probs_transpose)
                at(d, cross_probs_transpose)
                at(c, key_project)
                at(c, value_project)
                at(d, cross_attend, 0)

            pe.wait_ge(sig["identity_made"], 1)
            pe.wait_ge(sig["constants"], 2)
            pipeline(pe, step)

        @block.scalar
        def _(act):
            def copy(done, target, source, start, count):
                act.wait_ge(sig[start], count)
                nc.scalar.activation(target, source, ACT.Copy).then_inc(sig[done], 1)

            def self_exp(t):
                act.wait_ge(sig["self_bias"], t + 1)
                nc.scalar.activation(p1[:, :], s1[:, :], ACT.Exp, bias=s1_bias[:, :], scale=SELF_SCALE,
                                     accum_out=p1_sum[:, :]).then_inc(sig["self_exp"], 1)
                if isinstance(t, int) and t == 0:
                    copy("wq_hi", flat(wq_w[HI][:, :, :]), q_work[:, :], "wq_loaded", 16)

            def square_queries(t, g):
                act.wait_ge(sig["q_biased"], 4 * t + g + 1)
                nc.scalar.activation(q2s[:, 4 * g:4 * g + 4, :], q2[:, 4 * g:4 * g + 4, :], ACT.Square)\
                    .then_inc(sig["q_squared"], 1)

            def x_high(t):
                copy("xn_hi", flat(xnt[HI][:, :, :]), bank_a[:, 0, 0:D], "xn_transposed", t + 1)
                if isinstance(t, int) and t == 1:
                    copy("wo_hi", flat(wo_w[HI][:, :, :]), stage_b[:, :], "wo_loaded", 16)

            def copy_qk(t):
                copy("qk_copied", qk[:, :], bank_a[:, 1, :], "qk_projected", t + 1)

            def copy_v(t):
                copy("v_copied", v[:, :], bank_a[:, 0, 0:D], "v_projected", t + 1)

            def copy_qkt(t):
                copy("qkt_copied", flat(qkt[:, :, :]), bank_a[:, 0, :], "qk_transposed", t + 1)

            def copy_self_probs(t):
                copy("self_pt_copied", p1t[:, :], bank_b[:, 0, 0:P], "self_pt", t + 1)

            def copy_self_out(t):
                copy("self_ot", flat(o1t[:, :, :]), bank_b[:, 0, 0:D], "self_out", t + 1)

            def x1_high(t):
                copy("x1_hi", flat(x1t[HI][:, :, :]), bank_b[:, 0, 0:D], "x1_transposed", t + 1)

            def ctx_high(t):
                act.wait_ge(sig["v2_projected"], t)
                copy("ctx_hi", flat(ctxt[HI][:, :, :]), flat(ctx_in[:, :, :]), "ctx_loaded", 16 * t + 16)

            def copy_values(t):
                act.wait_ge(sig["v2_biased"], t)
                copy("v2_copied", v2_new[:, :], bank_c[:, 1, :], "v2_projected", t + 1)

            def copy_cross_probs(t):
                copy("cross_pt_copied", flat(p2t[:, :, :]), flat(bank_d[:, :, :]), "cross_pt", t + 1)

            def copy_x2(t):
                act.wait_ge(sig["x2_stored"], 16 * t)
                copy("x2t_copied", flat(x2t[:, :, :]), bank_e[:, 0, 0:D], "x2_transposed", t + 1)

            def copy_keys(t):
                if isinstance(t, int) and t == 0:
                    act.wait_ge(sig["key_scale"], 1)
                act.wait_ge(sig["k_transposed"], t + 1)
                nc.scalar.activation(flat(k2t[:, :, :]), bank_e[:, 0, :], ACT.Copy, scale=key_scale[:, :])\
                    .then_inc(sig["kt_copied"], 1)

            def copy_queries(t, n):
                copy("qt_copied", q2t[:, :, n * half:(n + 1) * half, :].rearrange("p b h s -> p h b s"),
                     flat(bank_c[:, :, :]).rearrange("p (h b s) -> p h b s", b=2, s=S), "q_transposed", 2 * t + n + 1)

            def cross_exp(t):
                act.wait_ge(sig["cross_shifted"], t + 1)
                rows = s2[:, :, :, :].rearrange("p a b c -> p (a b c)")
                nc.scalar.activation(rows, rows, ACT.Exp).then_inc(sig["cross_exp"], 1)

            def cross_out_high(t, m):
                for n in range(2):
                    copy("ot_hi", o2t[HI][:, m * half:(m + 1) * half, n * S:(n + 1) * S],
                         bank_d[:, n, :].rearrange("p (h s) -> p h s", s=S), "cross_out", 2 * t + m + 1)

            def route_exp(t):
                act.wait_ge(sig["top_bias"], t + 1)
                nc.scalar.activation(rexp[:, :], logits[:, 0:EXPERTS], ACT.Exp, bias=top_neg[:, :])\
                    .then_inc(sig["route_exp"], 1)
                nc.scalar.activation(sh_e[:, :], logits[:, EXPERTS:EXPERTS + 1], ACT.Exp, scale=-1.0)\
                    .then_inc(sig["shared_exp"], 1)

            def route_store(t):
                act.wait_ge(sig["w_transposed"], t + 1)
                act.wait_ge(sig["wt_stored"], 16 * t)
                nc.scalar.activation(wt[:, :], bank_e[0:2 * EPAIRS, 0, 0:P], ACT.Copy).then_inc(sig["wt_copied"], 1)

            def step(a, b, c, d, e, f):
                at(b, copy_qk)
                at(b, copy_v)
                at(f, route_exp)
                at(b, copy_qkt)
                at(d, copy_keys)
                at(d, copy_queries, 1)
                at(e, cross_out_high, 1)
                at(c, x1_high)
                at(b, self_exp)
                at(a, x_high)
                at(f, route_store)
                at(d, cross_exp)
                at(c, square_queries, 0)
                at(c, ctx_high)
                at(c, square_queries, 1)
                at(c, square_queries, 2)
                at(c, square_queries, 3)
                at(b, copy_self_probs)
                at(d, copy_cross_probs)
                at(c, copy_values)
                at(d, cross_out_high, 0)
                at(e, copy_x2)
                at(c, copy_queries, 0)
                at(b, copy_self_out)

            copy("qkv_hi", flat(qkv_w[HI][:, :, :]), q_work[:, 0:C * 3 * D], "qkv_loaded", 16)
            for part, source in ((bq_b[:, :], bq), (bkv_b[:, 0:KW], bk), (bkv_b[:, KW:2 * KW], bv)):
                act.dma_start(part, source.partition_broadcast(P)).then_inc(sig["small_loaded"], 16)
            for n in range(2):
                act.dma_start(mask_t[n * S:(n + 1) * S, :], mask).then_inc(sig["small_loaded"], 16)
            act.dma_start(qn_c[:, :], qn_w.rearrange("(p a) -> p a", a=1)).then_inc(sig["small_loaded"], 16)
            act.dma_start(kn_c[:, :], kn_w.rearrange("(p a) -> p a", a=1)).then_inc(sig["small_loaded"], 16)
            act.dma_start(o_w[:, :, :], split3(o_proj)).then_inc(sig["small_loaded"], 16)
            act.dma_start(router_w[:, :, :], split3(router)).then_inc(sig["small_loaded"], 16)

            def ahead(i):
                if i == 0:
                    copy("wkv_hi", flat(wkv_w[HI][:, :, :]), stage_b[:, 0:C * 2 * KW], "wkv_loaded", 32)

            pipeline(act, step, ahead=ahead)

        @block.vector
        def _(dve):
            def low(done, target, source, high, ready, count):
                dve.wait_ge(sig[ready], count)
                nc.vector.tensor_tensor(target, source, high.bitcast(F32), ALU.subtract).then_inc(sig[done], 1)

            def moments(source, stat, mv, ve, name, n1):
                nc.vector.bn_stats(stat[:, :], source[:, :]).then_inc(sig[name + "_stats"], 1)
                wait_alone(dve, sig[name + "_stats"], n1, sig["dve_held"])
                nc.vector.bn_aggr(mv[:, :], stat[:, :]).then_inc(sig[name + "_moments"], 1)
                dve.wait_ge(sig[name + "_moments"], n1)
                nc.vector.tensor_scalar_add(ve[:, :], mv[:, 1:2], LN_EPS).then_inc(sig[name + "_var"], 1)

            def normalise(done, target, source, mv, rs, name, n1):
                dve.wait_ge(sig[name + "_rstd"], n1)
                nc.vector.tensor_scalar(target[:, :], source[:, :], mv[:, 0:1], rs[:, :], ALU.subtract, ALU.mult)\
                    .then_inc(sig[done], 1)

            def x_moments(t):
                dve.wait_ge(sig["x_loaded"], 16 * t + 16)
                moments(x_in, x_stat, x_mv, x_ve, "x", t + 1)

            def x_norm(t):
                normalise("x_hat", x_hat, x_in, x_mv, x_rs, "x", t + 1)
                if isinstance(t, int) and t == 0:
                    low("qkv_lo", flat(qkv_w[LO][:, :, :]), q_work[:, 0:C * 3 * D], flat(qkv_w[HI][:, :, :]),
                        "qkv_hi", 1)

            def x_low(t):
                low("xn_lo", flat(xnt[LO][:, :, :]), bank_a[:, 0, 0:D], flat(xnt[HI][:, :, :]), "xn_hi", t + 1)
                if isinstance(t, int) and t == 1:
                    low("wo_lo", flat(wo_w[LO][:, :, :]), stage_b[:, :], flat(wo_w[HI][:, :, :]), "wo_hi", 1)

            def self_mask(t):
                dve.wait_ge(sig["self_scored"], t + 1)
                nc.vector.tensor_tensor(s1[:, :], bank_a[:, 1, 0:P], causal[:, :], ALU.add)\
                    .then_inc(sig["self_masked"], 1)
                dve.wait_ge(sig["self_masked"], t + 1)
                nc.vector.reduce_max(s1_max[:, :], s1[:, :], AX.X).then_inc(sig["self_max"], 1)
                dve.wait_ge(sig["self_max"], t + 1)
                nc.vector.tensor_scalar_mul(s1_bias[:, :], s1_max[:, :], -SELF_SCALE).then_inc(sig["self_bias"], 1)

            def self_normalise(t):
                dve.wait_ge(sig["self_exp"], t + 1)
                nc.vector.reciprocal(p1_rec[:, :], p1_sum[:, :]).then_inc(sig["self_recip"], 1)
                dve.wait_ge(sig["self_recip"], t + 1)
                nc.vector.tensor_scalar_mul(p1n[:, :], p1[:, :], p1_rec[:, :]).then_inc(sig["self_probs"], 1)
                if isinstance(t, int) and t == 0:
                    low("wq_lo", flat(wq_w[LO][:, :, :]), q_work[:, :], flat(wq_w[HI][:, :, :]), "wq_hi", 1)

            def x1_add(t):
                dve.wait_ge(sig["self_proj"], t + 1)
                dve.wait_ge(sig["x_res_loaded"], 16 * t + 16)
                nc.vector.scalar_tensor_tensor(h1[:, :], x_res[:, :], 2.0, bank_b[:, 0, 0:D], ALU.mult, ALU.add)\
                    .then_inc(sig["h1_done"], 1)
                dve.wait_ge(sig["h1_done"], t + 1)
                moments(h1, h1_stat, h1_mv, h1_ve, "h1", t + 1)

            def x1_norm(t):
                dve.wait_ge(sig["x1_stored"], 16 * t)
                normalise("x1_normed", x1, h1, h1_mv, h1_rs, "h1", t + 1)

            def x1_low(t):
                low("x1_lo", flat(x1t[LO][:, :, :]), bank_b[:, 0, 0:D], flat(x1t[HI][:, :, :]), "x1_hi", t + 1)

            def ctx_low(t):
                low("ctx_lo", flat(ctxt[LO][:, :, :]), flat(ctx_in[:, :, :]), flat(ctxt[HI][:, :, :]), "ctx_hi", t + 1)

            def bias_keys(t):
                dve.wait_ge(sig["k_projected"], t + 1)
                nc.vector.tensor_tensor(flat(k2[:, :, :]), bank_c[:, 0, :], bkv_b[:, 0:KW], ALU.add)\
                    .then_inc(sig["k_biased"], 1)

            def mean_square(squares, ss, ve, name, n1):
                nc.vector.tensor_reduce(ss, squares, AX.X, ALU.add).then_inc(sig[name + "_sumsq"], 1)
                dve.wait_ge(sig[name + "_sumsq"], n1)
                nc.vector.tensor_scalar(ve, ss, 1.0 / HD, RMS_EPS, ALU.mult, ALU.add)\
                    .then_inc(sig[name + "_var"], 1)

            def key_square(t):
                dve.wait_ge(sig["k_squared"], t + 1)
                mean_square(k2s[:, :, :], k2_ss[:, :], k2_ve[:, :], "k", t + 1)

            def query_bias(t, g):
                dve.wait_ge(sig["q_projected"], 4 * t + g + 1)
                nc.vector.tensor_tensor(q_work[:, g * 512:(g + 1) * 512], bank_c[:, g % 2, :],
                                        bq_b[:, g * 512:(g + 1) * 512], ALU.add).then_inc(sig["q_biased"], 1)

            def query_square(t, n):
                heads = slice(n * half, (n + 1) * half)
                dve.wait_ge(sig["q_squared"], 4 * t + 2 * n + 2)
                mean_square(q2s[:, heads, :], q2_ss[:, heads], q2_ve[:, heads], "q", 2 * t + n + 1)

            def query_norm(t):
                dve.wait_ge(sig["q_rstd"], 2 * t + 1)
                nc.vector.tensor_tensor(q2s[:, 0:half, :], q2[:, 0:half, :],
                                        q2_rs[:, 0:half].unsqueeze(2).to_broadcast([P, half, HD]), ALU.mult)\
                    .then_inc(sig["q_normed_a"], 1)

            def cross_mask(t, n):
                dve.wait_ge(sig["scored"], 2 * t + n + 1)
                nc.vector.tensor_tensor(s2[:, :, n, :], bank_c[:, n, :].rearrange("p (a e) -> p a e", e=S),
                                        mask_t[:, :].unsqueeze(1).to_broadcast([P, PAIRS, S]), ALU.add)\
                    .then_inc(sig["cross_masked"], 1)

            rows = s2[:, :, :, :].rearrange("p a b c -> p (a b) c")

            def cross_max(t):
                dve.wait_ge(sig["cross_masked"], 2 * t + 2)
                nc.vector.reduce_max(s2_max[:, :], rows, AX.X).then_inc(sig["cross_max"], 1)

            def cross_shift(t):
                dve.wait_ge(sig["cross_max"], t + 1)
                nc.vector.tensor_tensor(rows, rows, s2_max[:, :].unsqueeze(2).to_broadcast([P, HEADS, S]),
                                        ALU.subtract).then_inc(sig["cross_shifted"], 1)

            def cross_sum(t):
                dve.wait_ge(sig["cross_exp"], t + 1)
                nc.vector.tensor_reduce(s2_sum[:, :], rows, AX.X, ALU.add).then_inc(sig["cross_sum"], 1)
                dve.wait_ge(sig["cross_sum"], t + 1)
                nc.vector.reciprocal(s2_rec[:, :], s2_sum[:, :]).then_inc(sig["cross_recip"], 1)

            def cross_normalise(t):
                dve.wait_ge(sig["cross_recip"], t + 1)
                nc.vector.tensor_tensor(rows, rows, s2_rec[:, :].unsqueeze(2).to_broadcast([P, HEADS, S]),
                                        ALU.mult).then_inc(sig["cross_probs"], 1)

            def cross_out_low(t, m):
                for n in range(2):
                    low("ot_lo", o2t[LO][:, m * half:(m + 1) * half, n * S:(n + 1) * S],
                        bank_d[:, n, :].rearrange("p (h s) -> p h s", s=S),
                        o2t[HI][:, m * half:(m + 1) * half, n * S:(n + 1) * S], "ot_hi", 4 * t + 2 * m + n + 1)

            def x2_add(t):
                dve.wait_ge(sig["cross_proj"], t + 1)
                dve.wait_ge(sig["x1_res_loaded"], 16 * t + 16)
                nc.vector.tensor_tensor(h2[:, :], x1_res[:, :], bank_d[:, 0, 0:D], ALU.add).then_inc(sig["h2_done"], 1)
                dve.wait_ge(sig["h2_done"], t + 1)
                moments(h2, h2_stat, h2_mv, h2_ve, "h2", t + 1)

            def x2_norm(t):
                normalise("x2_normed", x2, h2, h2_mv, h2_rs, "h2", t + 1)

            def route_choose(t):
                n1 = t + 1
                dve.wait_ge(sig["routed"], n1)
                nc.vector.tensor_copy(logits[:, :], bank_e[:, 0, 0:EXPERTS + 1]).then_inc(sig["logits_copied"], 1)
                wait_alone(dve, sig["logits_copied"], n1, sig["dve_held"])
                nc.vector.max(top[:, :], logits[:, 0:EXPERTS]).then_inc(sig["top8"], 1)
                dve.wait_ge(sig["top8"], n1)
                nc.vector.tensor_scalar_mul(top_neg[:, :], top[:, 0:1], -1.0).then_inc(sig["top_bias"], 1)
                nc.vector.match_replace(rest[:, :], top[:, :], logits[:, 0:EXPERTS], REMOVED)\
                    .then_inc(sig["top_removed"], 1)
                dve.wait_ge(sig["top_removed"], n1)
                nc.vector.tensor_tensor(chosen[:, :], rest[:, :], logits[:, 0:EXPERTS], ALU.not_equal)\
                    .then_inc(sig["top_mask"], 1)

            def route_weigh(t):
                n1 = t + 1
                dve.wait_ge(sig["top_mask"], n1)
                dve.wait_ge(sig["route_exp"], n1)
                nc.vector.tensor_tensor(rkept[:, :], rexp[:, :], chosen[:, :], ALU.mult).then_inc(sig["route_kept"], 1)
                dve.wait_ge(sig["shared_exp"], n1)
                nc.vector.tensor_scalar_add(sh_p[:, :], sh_e[:, :], 1.0).then_inc(sig["shared_plus"], 1)
                dve.wait_ge(sig["route_kept"], n1)
                nc.vector.tensor_reduce(rsum[:, :], rkept[:, :], AX.X, ALU.add).then_inc(sig["route_sum"], 1)
                dve.wait_ge(sig["shared_plus"], n1)
                nc.vector.reciprocal(route[:, EXPERTS:EXPERTS + 1], sh_p[:, :]).then_inc(sig["shared_gate"], 1)
                dve.wait_ge(sig["route_sum"], n1)
                nc.vector.reciprocal(rrec[:, :], rsum[:, :]).then_inc(sig["route_recip"], 1)
                dve.wait_ge(sig["route_recip"], n1)
                nc.vector.tensor_scalar_mul(route[:, 0:EXPERTS], rkept[:, :], rrec[:, :]).then_inc(sig["route_w"], 1)

            def step(a, b, c, d, e, f):
                at(a, x_moments)
                at(f, route_choose)
                at(c, x1_add)
                at(a, x_norm)
                at(c, x1_norm)
                at(f, route_weigh)
                at(e, cross_out_low, 1)
                at(b, self_mask)
                at(d, cross_mask, 0)
                at(d, cross_mask, 1)
                at(d, cross_max)
                at(d, cross_shift)
                at(c, x1_low)
                at(b, self_normalise)
                at(a, x_low)
                at(d, cross_sum)
                at(e, x2_add)
                at(c, query_bias, 0)
                at(c, query_bias, 1)
                at(d, cross_normalise)
                at(c, ctx_low)
                at(c, query_bias, 2)
                at(c, query_bias, 3)
                at(c, query_square, 0)
                at(e, x2_norm)
                at(c, bias_keys)
                at(c, query_square, 1)
                at(c, query_norm)
                at(c, key_square)
                at(d, cross_out_low, 0)

            def ahead(i):
                if i == 0:
                    dve.wait_ge(sig["causal_made"], 1)
                elif i == 2:
                    dve.wait_ge(sig["small_loaded"], 16 * SMALL)
                    nc.vector.tensor_tensor(qn_c[:, :], qn_c[:, :], kn_c[:, :], ALU.mult)\
                        .then_inc(sig["key_scale_a"], 1)
                    dve.wait_ge(sig["key_scale_a"], 1)
                    nc.vector.tensor_scalar_mul(key_scale[:, :], qn_c[:, :], float(HD) ** -0.5)\
                        .then_inc(sig["key_scale"], 1)

            pipeline(dve, step, ahead=ahead)


EXPERT_SIGNALS = """
sp_held2 dve_held2 pool_held2
weights_loaded down_loaded weights_high weights_low spread0 spread1 spread2 x_high x_low
identity_zeroed2 identity_made2 constants2
gated upped silu_done gated_up weighted inter_hi inter_lo y_done y_added
z_transposed z_copied z_stats z_moments z_var z_rstd z_normed out_stored0 out_stored1
""".split()


def expert_phase(nc, sig, acc_loaded, gate_up, down, gu_raw, dp_raw, x2t_d, wt_d, out):
    with ExitStack() as stack:
        def sb(name, shape, dt=F32):
            return stack.enter_context(nc.sbuf_tensor(name, shape, dt))

        acc = sb("acc", [P, BLOCKS, C, BLOCK])
        xt = [sb(f"xt{n}", [P, BLOCKS, C, BLOCK], F32R) for n in (HI, LO)]
        gu = [[sb(f"gu{u}{n}", [P, GROUP, 2, C, P], F32R) for n in (HI, LO)] for u in range(2)]
        dp = [[sb(f"dp{u}{n}", [P, GROUP, D], F32R) for n in (HI, LO)] for u in range(2)]
        spread = sb("spread", [P, GROUP, BLOCK])
        silu = sb("silu", [P, 2, BLOCK])
        gxu = sb("gxu", [P, 2, BLOCK])
        inter = sb("inter", [P, 2, BLOCK])
        int_p = [sb(f"int_p{n}", [P, 2, BLOCK], F32R) for n in (HI, LO)]
        y_sum = sb("y_sum", [P, C, BLOCK])
        identity = sb("identity2", [P, P])
        z = sb("z", [P, 2, 4, D])
        z_stat = sb("z_stat", [P, 4, 6])
        z_mv = sb("z_mv", [P, 4, 2])
        z_ve = sb("z_ve", [P, 4])
        z_rs = sb("z_rs", [P, 4])
        minus_half = sb("minus_half2", [P, 4])

        def bank(name, n=1):
            return stack.enter_context(nc.psum_tensor(name, [P, n, 512], F32))

        bank_gate, bank_up = bank("bank_gate", 2), bank("bank_up", 2)
        bank_y, bank_z = bank("bank_y", 2), bank("bank_z")

        block = stack.enter_context(nc.Block())
        STEP = ROUNDS * UNITS

        def groups(eng, run):
            run(0, 0, True, False)
            run(1, 1, False, False)
            with eng.Fori(1, (GROUPS - 1) // 2) as g2:
                for u in range(2):
                    run(2 * g2 + u, u, False, False)
            run(GROUPS - 1, 0, False, True)

        def rounds(eng, run):
            run(0)
            with eng.Fori(1, ROUNDS) as r:
                run(r)

        @block.sync
        def _(sp):
            def load_weights(g):
                sp.wait_ge(sig["weights_low"], g)
                sp.dma_start(gu_raw[:, :], gate_up[g, :, :]).then_inc(sig["weights_loaded"], 16)
                sp.dma_start(dp_raw[:, :], down[g, :, :]).then_inc(sig["down_loaded"], 16)

            def load_tokens(b):
                sp.dma_start(acc[:, b, :, :], x2t_d[:, :, b * BLOCK:(b + 1) * BLOCK]).then_inc(acc_loaded[b], 16)

            def load_spread(g, r, k, first):
                p = k % GROUP
                if not (first and k < GROUP and isinstance(r, int)):
                    wait_alone(sp, sig["weighted"], STEP * g + UNITS * r + k - GROUP + 1, sig["sp_held2"])
                for half in range(2):
                    row = wt_d[bass.ds(2 * (GROUP * g + p) + half, 1), bass.ds((2 * r + k // GROUP) * BLOCK, BLOCK)]
                    sp.dma_start(spread[half * INNER:(half + 1) * INNER, p, :], row.to_broadcast([INNER, BLOCK]))\
                      .then_inc(sig[f"spread{p}"], 16)

            def store(b, parity):
                sp.wait_ge(sig["z_normed"], 4 * b + 4)
                sp.dma_start(out[bass.ts(b, BLOCK), :].rearrange("(j p) d -> p j d", p=P), z[:, parity, :, :])\
                  .then_inc(sig[f"out_stored{parity}"], 16)

            def run_group(g, u, first, last):
                def run_round(r):
                    for k in range(UNITS):
                        load_spread(g, r, k, first)

                if first:
                    for b in range(BLOCKS):
                        load_tokens(b)
                        if b == 0:
                            for k in range(GROUP):
                                load_spread(0, 0, k, True)
                    load_weights(1)
                    for k in range(GROUP, UNITS):
                        load_spread(0, 0, k, True)
                    with sp.Fori(1, ROUNDS) as r:
                        run_round(r)
                elif not last:
                    load_weights(g + 1)
                    rounds(sp, run_round)
                else:
                    for r in range(ROUNDS):
                        for k in range(UNITS):
                            load_spread(g, r, k, False)
                            done = 2 * r + k // GROUP - 3
                            if k % GROUP == 2 and done >= 0:
                                store(done, done % 2)
                    for b in range(BLOCKS - 3, BLOCKS):
                        store(b, b % 2)

            groups(sp, run_group)
            for parity in range(2):
                sp.wait_ge(sig[f"out_stored{parity}"], 16 * ROUNDS)

        @block.gpsimd
        def _(pool):
            nc.gpsimd.memset(minus_half[:, :], -0.5).then_inc(sig["constants2"], 1)
            nc.gpsimd.memset(identity[:, :], 0.0).then_inc(sig["identity_zeroed2"], 1)
            pool.wait_ge(sig["identity_zeroed2"], 1)
            nc.gpsimd.affine_select(out=identity[:, :], in_=identity[:, :], compare_op=ALU.not_equal, fill=1.0,
                                    base=0, pattern=[[-1, P]], channel_multiplier=1).then_inc(sig["identity_made2"], 1)

            def split_weights(g, u):
                if not (isinstance(g, int) and g < 2):
                    pool.wait_ge(sig["y_done"], BLOCKS * (g - 1))
                wait_alone(pool, sig["weights_loaded"], 16 * g, sig["pool_held2"])
                wait_alone(pool, sig["down_loaded"], 16 * g, sig["pool_held2"])
                flat = [w[:, :, :, :, :].rearrange("p a b c n -> p (a b c n)") for w in gu[u]]
                flat_d = [w[:, :, :].rearrange("p a n -> p (a n)") for w in dp[u]]
                nc.gpsimd.tensor_copy(flat[HI], gu_raw[:, :])
                nc.gpsimd.tensor_copy(flat_d[HI], dp_raw[:, :]).then_inc(sig["weights_high"], 1)
                pool.wait_ge(sig["weights_high"], g + 1)
                nc.gpsimd.tensor_tensor(flat[LO], gu_raw[:, :], flat[HI].bitcast(F32), ALU.subtract)
                nc.gpsimd.tensor_tensor(flat_d[LO], dp_raw[:, :], flat_d[HI].bitcast(F32), ALU.subtract)\
                    .then_inc(sig["weights_low"], 1)

            split_weights(1, 1)
            with pool.Fori(1, (GROUPS - 1) // 2) as g2:
                for u in range(2):
                    split_weights(2 * g2 + u, u)
            split_weights(GROUPS - 1, 0)
            pool.wait_ge(sig["constants2"], 1)
            with pool.Fori(0, BLOCKS) as b:
                pool.wait_ge(sig["z_var"], b + 1)
                nc.gpsimd.tensor_tensor(z_rs[:, :], z_ve[:, :], minus_half[:, :], ALU.pow).then_inc(sig["z_rstd"], 1)

        @block.tensor
        def _(pe):
            def run_group(g, u, first, last):
                if last:
                    pe.wait_ge(sig["identity_made2"], 1)
                pe.wait_ge(sig["weights_low"], g + 1)

                def open_unit(r, k):
                    n = STEP * g + UNITS * r + k
                    p, par = k % GROUP, k % 2
                    if first:
                        pe.wait_ge(sig["x_low"], 2 * r + k // GROUP + 1)
                    if not (isinstance(n, int) and n < 2):
                        pe.wait_ge(sig["gated_up"], n - 1)
                    for which, target, done in ((0, bank_gate, "gated"), (1, bank_up, "upped")):
                        for m, (a, b) in enumerate(PASSES):
                            for c in range(C):
                                mm = nc.tensor.matmul(target[:, par, :], gu[u][a][:, p, which, c, :],
                                                      xt[b][:, 2 * r + k // GROUP, c, :],
                                                      start=(m == 0 and c == 0),
                                                      stop=(m == len(PASSES) - 1 and c == C - 1))
                        mm.then_inc(sig[done], 1)

                def close_unit(r, k, g=g, u=u):
                    n = STEP * g + UNITS * r + k
                    p, par = k % GROUP, k % 2
                    done = BLOCKS * g + 2 * r + k // GROUP
                    pe.wait_ge(sig["inter_lo"], n + 1)
                    if p == 0:
                        pe.wait_ge(sig["y_added"], done)
                    for c in range(C):
                        for m, (a, b) in enumerate(PASSES):
                            mm = nc.tensor.matmul(bank_y[:, c, :], dp[u][a][:, p, c * P:(c + 1) * P],
                                                  int_p[b][:, par, :], start=(p == 0 and m == 0),
                                                  stop=(p == GROUP - 1 and m == len(PASSES) - 1))
                    if p == GROUP - 1:
                        mm.then_inc(sig["y_done"], 1)

                def transpose_out(done, n):
                    pe.wait_ge(sig["y_added"], BLOCKS * g + done + 1)
                    pe.wait_ge(sig["z_copied"], 2 * done + n)
                    for j in range(2):
                        for c in range(C):
                            mm = nc.tensor.transpose(bank_z[:, 0, j * D + c * P:j * D + (c + 1) * P],
                                                     y_sum[:, c, (2 * n + j) * P:(2 * n + j + 1) * P],
                                                     identity[:, :])
                    mm.then_inc(sig["z_transposed"], 1)

                def transpose_before(r, k, n):
                    if k > GROUP:
                        transpose_out(2 * r, n)
                    elif not isinstance(r, int):
                        transpose_out(2 * r - 1, n)

                def run_round(r):
                    for k in range(UNITS):
                        open_unit(r, k)
                        if last and k % GROUP == 2:
                            transpose_before(r, k, 1)
                        if k:
                            close_unit(r, k - 1)
                        elif not isinstance(r, int):
                            close_unit(r - 1, UNITS - 1)
                        elif not first:
                            close_unit(ROUNDS - 1, UNITS - 1, g - 1, 1 - u)
                        if last and k % GROUP == 1:
                            transpose_before(r, k, 0)

                rounds(pe, run_round)
                if last:
                    close_unit(ROUNDS - 1, UNITS - 1)
                    for n in range(2):
                        transpose_out(BLOCKS - 1, n)

            groups(pe, run_group)

        @block.scalar
        def _(act):
            nc.scalar.activation(gu[0][HI][:, :, :, :, :].rearrange("p a b c n -> p (a b c n)"), gu_raw[:, :], ACT.Copy)
            nc.scalar.activation(dp[0][HI][:, :, :].rearrange("p a n -> p (a n)"), dp_raw[:, :], ACT.Copy)\
                .then_inc(sig["weights_high"], 1)

            def x_high(b):
                act.wait_ge(acc_loaded[b], 16)
                nc.scalar.activation(xt[HI][:, b, :, :], acc[:, b, :, :], ACT.Copy).then_inc(sig["x_high"], 1)

            def run_group(g, u, first, last):
                def run_round(r):
                    for k in range(UNITS):
                        n = STEP * g + UNITS * r + k
                        par = k % 2
                        act.wait_ge(sig["gated"], n + 1)
                        nc.scalar.activation(silu[:, par, :], bank_gate[:, par, :], ACT.Silu)\
                            .then_inc(sig["silu_done"], 1)
                        act.wait_ge(sig["weighted"], n + 1)
                        nc.scalar.activation(int_p[HI][:, par, :], inter[:, par, :], ACT.Copy)\
                            .then_inc(sig["inter_hi"], 1)
                        if first and isinstance(r, int):
                            x_high(k + 2)
                        if last and k % GROUP:
                            if k > GROUP:
                                copy_out(r, 0, k % GROUP - 1)
                            elif not isinstance(r, int):
                                copy_out(r - 1, 1, k % GROUP - 1)

                def copy_out(r, parity, n):
                    act.wait_ge(sig["z_transposed"], 2 * (2 * r + parity) + n + 1)
                    act.wait_ge(sig[f"out_stored{parity}"], 16 * r)
                    nc.scalar.activation(z[:, parity, 2 * n:2 * n + 2, :].rearrange("p a n -> p (a n)"),
                                         bank_z[:, 0, :], ACT.Copy).then_inc(sig["z_copied"], 1)

                rounds(act, run_round)
                if last:
                    for n in range(2):
                        copy_out(ROUNDS - 1, 1, n)

            for b in range(2):
                x_high(b)
            groups(act, run_group)

        @block.vector
        def _(dve):
            dve.wait_ge(sig["weights_high"], 1)
            for low, raw, high in ((gu[0][LO][:, :, :, :, :].rearrange("p a b c n -> p (a b c n)"), gu_raw,
                                    gu[0][HI][:, :, :, :, :].rearrange("p a b c n -> p (a b c n)")),
                                   (dp[0][LO][:, :, :].rearrange("p a n -> p (a n)"), dp_raw,
                                    dp[0][HI][:, :, :].rearrange("p a n -> p (a n)"))):
                lows = nc.vector.tensor_tensor(low, raw[:, :], high.bitcast(F32), ALU.subtract)
            lows.then_inc(sig["weights_low"], 1)

            def x_low(b):
                dve.wait_ge(sig["x_high"], b + 1)
                nc.vector.tensor_tensor(xt[LO][:, b, :, :], acc[:, b, :, :], xt[HI][:, b, :, :].bitcast(F32),
                                        ALU.subtract).then_inc(sig["x_low"], 1)

            for b in range(2):
                x_low(b)

            def run_group(g, u, first, last):
                def weigh(r, k):
                    n = STEP * g + UNITS * r + k
                    par = k % 2
                    dve.wait_ge(sig["silu_done"], n + 1)
                    dve.wait_ge(sig["upped"], n + 1)
                    nc.vector.tensor_tensor(gxu[:, par, :], silu[:, par, :], bank_up[:, par, :], ALU.mult)\
                        .then_inc(sig["gated_up"], 1)
                    dve.wait_ge(sig["gated_up"], n + 1)
                    dve.wait_ge(sig[f"spread{k % GROUP}"], 32 * (BLOCKS * g + 2 * r + k // GROUP + 1))
                    nc.vector.tensor_tensor(inter[:, par, :], gxu[:, par, :], spread[:, k % GROUP, :], ALU.mult)\
                        .then_inc(sig["weighted"], 1)

                def inter_low(r, k):
                    n = STEP * g + UNITS * r + k
                    par = k % 2
                    dve.wait_ge(sig["inter_hi"], n + 1)
                    nc.vector.tensor_tensor(int_p[LO][:, par, :], inter[:, par, :], int_p[HI][:, par, :].bitcast(F32),
                                            ALU.subtract).then_inc(sig["inter_lo"], 1)

                def add(r, k, g=g, last=last):
                    done = BLOCKS * g + 2 * r + k // GROUP
                    dve.wait_ge(sig["y_done"], done + 1)
                    if last:
                        dve.wait_ge(sig["z_transposed"], 2 * (2 * r + k // GROUP))
                    total = acc[:, 2 * r + k // GROUP, :, :]
                    nc.vector.tensor_tensor(y_sum[:, :, :] if last else total, total, bank_y[:, :, :], ALU.add)\
                        .then_inc(sig["y_added"], 1)

                def finish_moments(done, parity):
                    dve.wait_ge(sig["z_copied"], 2 * done + 2)
                    for j in range(4):
                        st = nc.vector.bn_stats(z_stat[:, j, :], z[:, parity, j, :])
                    st.then_inc(sig["z_stats"], 1)
                    wait_alone(dve, sig["z_stats"], done + 1, sig["dve_held2"])
                    for j in range(4):
                        st = nc.vector.bn_aggr(z_mv[:, j, :], z_stat[:, j, :])
                    st.then_inc(sig["z_moments"], 1)
                    dve.wait_ge(sig["z_moments"], done + 1)
                    nc.vector.tensor_scalar_add(z_ve[:, :], z_mv[:, :, 1], LN_EPS).then_inc(sig["z_var"], 1)

                def finish_norm(done, parity):
                    dve.wait_ge(sig["z_rstd"], done + 1)
                    for j in range(4):
                        nc.vector.tensor_scalar(z[:, parity, j, :], z[:, parity, j, :], z_mv[:, j, 0:1],
                                                z_rs[:, j:j + 1], ALU.subtract, ALU.mult).then_inc(sig["z_normed"], 1)

                def run_round(r):
                    fixed = isinstance(r, int)
                    for k in range(UNITS):
                        parity = k // GROUP
                        weigh(r, k)
                        if first and fixed:
                            x_low(k + 2)
                        if k % GROUP == 0:
                            if k:
                                add(r, k - 1)
                            elif not fixed:
                                add(r - 1, UNITS - 1)
                            elif not first:
                                add(ROUNDS - 1, UNITS - 1, g - 1, False)
                        if last and k % GROUP == 1 and not fixed:
                            finish_norm(2 * r + parity - 2, parity)
                        inter_low(r, k)
                        if last and k % GROUP == 2 and (parity or not fixed):
                            finish_moments(2 * r + parity - 1, 1 - parity)

                rounds(dve, run_round)
                if last:
                    add(ROUNDS - 1, UNITS - 1)
                    finish_norm(BLOCKS - 2, 0)
                    finish_moments(BLOCKS - 1, 1)
                    finish_norm(BLOCKS - 1, 1)

            groups(dve, run_group)


def kernel(**inputs):
    import numpy as np
    import concourse.bacc as bacc
    from concourse.bass_utils import run_bass_kernel_spmd

    def of(name):
        return np.asarray(inputs[name])

    gu = np.zeros((2 * EPAIRS, 2, INNER, D), np.float32)
    gu[:EXPERTS] = of("L0_ffn_gu_w").reshape(EXPERTS, 2, INNER, D)
    gu[EXPERTS, 0] = of("L0_ffn_sh_gate_w")
    gu[EXPERTS, 1] = of("L0_ffn_sh_up_w")
    gu = gu.reshape(GROUPS, GROUP, 2, 2, INNER, C, P).transpose(0, 6, 1, 3, 5, 2, 4)
    dp = np.zeros((2 * EPAIRS, D, INNER), np.float32)
    dp[:EXPERTS] = of("L0_ffn_dp_w")
    dp[EXPERTS] = of("L0_ffn_sh_down_w")
    dp = dp.reshape(GROUPS, GROUP, 2, D, INNER).transpose(0, 2, 4, 1, 3)
    router = np.zeros((D, EXPERTS + 1), np.float32)
    router[:, :EXPERTS] = of("L0_ffn_gate_w").T
    router[:, EXPERTS] = of("L0_ffn_sh_gate1_w")[0]

    arrays = {
        "x": of("x").reshape(N, D), "ctx": of("ctx_2048").reshape(N, C, P).transpose(2, 1, 0),
        "mask": of("mask_1xSxS2_ff0").reshape(S, S),
        "qkv": of("L0_attn_qkv"), "o_proj": of("L0_attn_o_proj"), "gamma": of("L0_attn_gamma"),
        "beta": of("L0_attn_beta"), "wq": of("L0_xattn_Wq"), "bq": of("L0_xattn_bq"), "wk": of("L0_xattn_Wk"),
        "bk": of("L0_xattn_bk"), "wv": of("L0_xattn_Wv"), "bv": of("L0_xattn_bv"), "wo": of("L0_xattn_Wo"),
        "qn_w": of("L0_xattn_qn_w"), "kn_w": of("L0_xattn_kn_w"), "router": router,
        "gate_up": gu.reshape(GROUPS, P, GROUP * 4 * P), "down": dp.reshape(GROUPS, P, GROUP * D),
    }
    arrays = {f"in_{name}": np.ascontiguousarray(a) for name, a in arrays.items()}
    nc = bacc.Bacc("TRN2", target_bir_lowering=False, num_devices=1)
    args = [nc.dram_tensor(name, a.shape, mybir.dt.from_np(a.dtype), kind="ExternalInput").ap()
            for name, a in arrays.items()]
    out = nc.dram_tensor("out", [N, D], F32, kind="ExternalOutput").ap()
    decoder(nc, *args, out)
    result = run_bass_kernel_spmd(nc, [arrays], core_ids=[0])
    return result.results[0]["out"].reshape(B, S, D)
```
